# Optimizing a Trainium2 kernel written in Bass

```python
import numpy as np
import jax
import jax.numpy as jnp

def _softmax(x, axis=-1):
    return jax.nn.softmax(x, axis=axis)

def _gelu(x):
    return jax.nn.gelu(x, approximate=True)

def _silu(x):
    return jax.nn.silu(x)

def _sigmoid(x):
    return jax.nn.sigmoid(x)

def _layernorm(x, axis=-1, eps=1e-05):
    m = jnp.mean(x, axis=axis, keepdims=True)
    v = jnp.var(x, axis=axis, keepdims=True)
    return (x - m) / jnp.sqrt(v + eps)

def _scatter_add(tgt, idx, src, axis=0):
    return tgt.at[idx].add(src)

def _segment_sum(src, seg, n):
    return jax.ops.segment_sum(src, seg, n)
kernel_name = 'mk_xattn_seq_d4_seqx_r4_d24949'

def setup_inputs(seed: int=0):
    np.random.seed(seed)
    _w = jnp.asarray

    def _rec_inputs():
        import jax
        import jax.numpy as jnp
        _rk = jax.random.key(seed)
        x = -0.000125 + 0.9999 * jax.random.normal(jax.random.fold_in(_rk, 1), (8, 256, 512), jnp.float32)
        _lenS = 256 - jax.random.randint(jax.random.fold_in(_rk, 7), (8,), 0, max(1, 256 // 4) + 1, jnp.int32)
        _lenS2 = 256 - jax.random.randint(jax.random.fold_in(_rk, 8), (8,), 0, max(1, 256 // 4) + 1, jnp.int32)
        _ctx_2048P = jax.random.normal(jax.random.fold_in(_rk, 11), (8, 16, 512), jnp.float32)
        _ctx_2048c = jax.random.dirichlet(jax.random.fold_in(_rk, 511), 0.3 * jnp.ones((16,), jnp.float32), (8, 256))
        _ctx_2048t = jnp.einsum('bsk,bkd->bsd', _ctx_2048c, _ctx_2048P)
        _ctx_2048t = _ctx_2048t * jax.lax.rsqrt(jnp.mean(jnp.square(_ctx_2048t)) + 1e-12) * 0.953939
        ctx_2048 = -0.00401388 + 1.00018 * (_ctx_2048t + 0.3 * jax.random.normal(jax.random.fold_in(_rk, 611), (8, 256, 512), jnp.float32))
        _validS = jnp.arange(256)[None, :] < _lenS[:, None]
        _validS2 = jnp.arange(256)[None, :] < _lenS2[:, None]
        _causal = jnp.tril(jnp.ones((256, 256), dtype=bool))
        mask_1x1xSxS2_fc1 = jnp.where(jnp.broadcast_to(_validS2[0:1, None, None, :], (1, 1, 256, 256)), 1.0, 0.0).astype(jnp.float32)
        mask_Bx1xSxS2_ff1 = jnp.where(jnp.ones((8, 1, 256, 256), dtype=bool), 1.0, 0.0).astype(jnp.float32)
        return (x, ctx_2048, mask_1x1xSxS2_fc1, mask_Bx1xSxS2_ff1)
    x, ctx_2048, mask_1x1xSxS2_fc1, mask_Bx1xSxS2_ff1 = _rec_inputs()

    def _L0_xattn_setup():
        import jax, jax.numpy as jnp
        import numpy as np
        H = 512
        B, L, S = (4, 1024, 10)
        key = jax.random.key(seed)
        k1, k2, k3, k4, k5, k6 = jax.random.split(key, 6)
        scale = 1.0 / np.sqrt(H)
        return {'h_english': jax.random.normal(k1, (B, L, H), dtype=jnp.float32), 'h_lojban': jax.random.normal(k2, (B, S, H), dtype=jnp.float32), 'w_q': jax.random.normal(k3, (H, H), dtype=jnp.float32) * scale, 'w_k': jax.random.normal(k4, (H, H), dtype=jnp.float32) * scale, 'w_v': jax.random.normal(k5, (H, H), dtype=jnp.float32) * scale, 'w_o': jax.random.normal(k6, (H, H), dtype=jnp.float32) * scale, 'alpha': jnp.float32(0.1)}
    _L0_xattn_all = _L0_xattn_setup()
    _L0_xattn_in = {k: v for k, v in _L0_xattn_all.items() if k in ('w_q', 'w_k', 'w_v', 'w_o', 'alpha')}
    del _L0_xattn_all

    def _L1_xattn_setup():
        import jax, jax.numpy as jnp
        import numpy as np
        D_MODEL = 256
        N_HEAD = 16
        D_HEAD = 64
        IDX_LIST = [256, 512]
        SCALE = 1.0 / D_HEAD ** 0.5
        LN_EPS = 1e-05
        key = jax.random.key(seed)
        ks = jax.random.split(key, 9)
        s = 0.02
        B, L = (2, 512)
        return {'z1ss': jax.random.normal(ks[0], (B, D_MODEL, L), dtype=jnp.float32), 'u1ss': jax.random.normal(ks[1], (B, D_MODEL, L), dtype=jnp.float32), 'Wqkv0': jax.random.normal(ks[2], (3 * N_HEAD * D_HEAD, D_MODEL), dtype=jnp.float32) * s, 'Wqkv1': jax.random.normal(ks[3], (3 * N_HEAD * D_HEAD, D_MODEL), dtype=jnp.float32) * s, 'Winj0': jax.random.normal(ks[4], (3 * N_HEAD * D_HEAD, D_MODEL), dtype=jnp.float32) * s, 'Winj1': jax.random.normal(ks[5], (3 * N_HEAD * D_HEAD, D_MODEL), dtype=jnp.float32) * s, 'Wo': jax.random.normal(ks[6], (D_MODEL, N_HEAD * D_HEAD), dtype=jnp.float32) * s, 'bo': jax.random.normal(ks[7], (D_MODEL,), dtype=jnp.float32) * s, 'r_w_bias': jax.random.uniform(ks[8], (N_HEAD, D_HEAD), minval=-0.05, maxval=0.05, dtype=jnp.float32)}
    _L1_xattn_all = _L1_xattn_setup()
    _L1_xattn_in = {k: v for k, v in _L1_xattn_all.items() if k in ('Wqkv0', 'Wqkv1', 'Winj0', 'Winj1', 'Wo', 'bo', 'r_w_bias')}
    del _L1_xattn_all

    def _L2_xattn_setup():
        import jax, jax.numpy as jnp
        import numpy as np
        H = 512
        NH = 16
        HD = H // NH
        EPS = 1e-05

        def gelu(x):
            return 0.5 * x * (1.0 + jnp.tanh(0.7978845608028654 * x * (1.0 + 0.044715 * x * x)))

        def layernorm(x, scale, bias):
            m = jnp.mean(x, axis=-1, keepdims=True)
            v = jnp.mean(jnp.square(x - m), axis=-1, keepdims=True)
            return (x - m) * jax.lax.rsqrt(v + EPS) * scale + bias

        def split_heads(x):
            b, s, _ = x.shape
            return x.reshape(b, s, NH, HD).transpose(0, 2, 1, 3)

        def merge_heads(x):
            b, nh, s, hd = x.shape
            return x.transpose(0, 2, 1, 3).reshape(b, s, nh * hd)

        def attention(q, k, v, mask):
            scores = jnp.einsum('bhqd,bhkd->bhqk', q, k) / jnp.sqrt(jnp.float32(HD))
            scores = scores * mask - 10000.0 * (1.0 - mask)
            probs = jax.nn.softmax(scores, axis=-1)
            return jnp.einsum('bhqk,bhkd->bhqd', probs, v)
        key = jax.random.key(seed)
        ks = jax.random.split(key, 16)
        b, s, t = (2, 256, 256)
        w = lambda k, i, o: jax.random.normal(k, (i, o), jnp.float32) * 0.02
        inp = {'hidden_states': jax.random.normal(ks[0], (b, s, H), jnp.float32), 'encoder_states': jax.random.normal(ks[1], (b, t, H), jnp.float32), 'ltor_mask': jnp.tril(jnp.ones((1, 1, s, s), jnp.float32)), 'cross_mask': jnp.ones((b, 1, s, t), jnp.float32), 'ln1_s': jnp.ones((H,), jnp.float32), 'ln1_b': jnp.zeros((H,), jnp.float32), 'w_qkv': w(ks[2], H, 3 * H), 'b_qkv': jnp.zeros((3 * H,), jnp.float32), 'w_ao': w(ks[3], H, H), 'b_ao': jnp.zeros((H,), jnp.float32), 'ln2_s': jnp.ones((H,), jnp.float32), 'ln2_b': jnp.zeros((H,), jnp.float32), 'w_q': w(ks[4], H, H), 'b_q': jnp.zeros((H,), jnp.float32), 'w_kv': w(ks[5], H, 2 * H), 'b_kv': jnp.zeros((2 * H,), jnp.float32), 'w_co': w(ks[6], H, H), 'b_co': jnp.zeros((H,), jnp.float32), 'ln3_s': jnp.ones((H,), jnp.float32), 'ln3_b': jnp.zeros((H,), jnp.float32), 'w1': w(ks[7], H, 4 * H), 'b1': jnp.zeros((4 * H,), jnp.float32), 'w2': w(ks[8], 4 * H, H), 'b2': jnp.zeros((H,), jnp.float32)}
        return inp
    _L2_xattn_all = _L2_xattn_setup()
    _L2_xattn_in = {k: v for k, v in _L2_xattn_all.items() if k in ('ln1_s', 'ln1_b', 'w_qkv', 'b_qkv', 'w_ao', 'b_ao', 'ln2_s', 'ln2_b', 'w_q', 'b_q', 'w_kv', 'b_kv', 'w_co', 'b_co', 'ln3_s', 'ln3_b', 'w1', 'b1', 'w2', 'b2')}
    del _L2_xattn_all

    def _L3_xattn_setup():
        import jax, jax.numpy as jnp
        import numpy as np
        E, H, L, B = (512, 32, 256, 4)
        S = E // H
        DM, DD = (32, 64)

        def _ln(x, w, b, eps=1e-05):
            m = x.mean(-1, keepdims=True)
            v = ((x - m) ** 2).mean(-1, keepdims=True)
            return (x - m) / jnp.sqrt(v + eps) * w + b

        def _block(x, state, ln1_w, ln1_b, ln2_w, ln2_b, maa_x, maa_w1, maa_w2, maa_stack, time_decay, td_w1, td_w2, u, Wr, Wk, Wv, Wg, Wo, gn_w, gn_b, ffn_maa_k, ffn_maa_r, Wfk, Wfr, Wfv):
            b, l, e = x.shape
            h = u.shape[0]
            s_ = e // h
            xa = _ln(x, ln1_w, ln1_b)
            sx = jnp.concatenate([state[:, 1:2] - xa[:, :1], xa[:, :-1] - xa[:, 1:]], axis=1)
            xxx = jnp.tanh((xa + sx * maa_x) @ maa_w1).reshape(b, l, 5, DM)
            xxx = jnp.einsum('blfd,fde->blfe', xxx, maa_w2)
            xm = xa[:, :, None] + sx[:, :, None] * (maa_stack + xxx)
            xk, xw, xv, xr, xg = (xm[:, :, j] for j in range(5))
            w = jnp.exp(-jnp.exp(time_decay + jnp.tanh(xw @ td_w1) @ td_w2)).reshape(b, l, h, s_)
            r = (xr @ Wr.T).reshape(b, l, h, s_)
            k = (xk @ Wk.T).reshape(b, l, h, s_)
            v = (xv @ Wv.T).reshape(b, l, h, s_)
            g = jax.nn.silu(xg @ Wg.T)
            s0 = state[:, 2:2 + s_].reshape(b, h, s_, s_)

            def step(s, rkvw):
                r_t, k_t, v_t, w_t = rkvw
                a = k_t[..., :, None] * v_t[..., None, :]
                out = jnp.einsum('bhi,bhij->bhj', r_t, u * a + s)
                s = a + w_t[..., :, None] * s
                return (s, out)
            rkvw = tuple((jnp.moveaxis(t, 1, 0) for t in (r, k, v, w)))
            _, out = jax.lax.scan(step, s0, rkvw)
            out = jnp.moveaxis(out, 0, 1).reshape(b, l, e)
            og = out.reshape(b, l, h, s_)
            m = og.mean(-1, keepdims=True)
            va = ((og - m) ** 2).mean(-1, keepdims=True)
            og = ((og - m) / jnp.sqrt(va + 1e-05)).reshape(b, l, e) * gn_w + gn_b
            x1 = x + og * g @ Wo.T
            xc = _ln(x1, ln2_w, ln2_b)
            sx2 = jnp.concatenate([state[:, 0:1] - xc[:, :1], xc[:, :-1] - xc[:, 1:]], axis=1)
            xk2 = xc + sx2 * ffn_maa_k
            xr2 = xc + sx2 * ffn_maa_r
            rr = jax.nn.sigmoid(xr2 @ Wfr.T)
            kk = jnp.square(jax.nn.relu(xk2 @ Wfk.T))
            return x1 + rr * (kk @ Wfv.T)
        key = jax.random.key(seed)
        ks = jax.random.split(key, 24)
        sc = 0.02
        d = {'x': jax.random.normal(ks[0], (B, L, E), jnp.float32), 'state': jax.random.normal(ks[1], (B, 2 + S, E), jnp.float32) * 0.1, 'ln1_w': jnp.ones((E,), jnp.float32), 'ln1_b': jnp.zeros((E,), jnp.float32), 'ln2_w': jnp.ones((E,), jnp.float32), 'ln2_b': jnp.zeros((E,), jnp.float32), 'maa_x': jax.random.normal(ks[2], (E,), jnp.float32) * 0.1, 'maa_w1': jax.random.normal(ks[3], (E, 5 * DM), jnp.float32) * sc, 'maa_w2': jax.random.normal(ks[4], (5, DM, E), jnp.float32) * sc, 'maa_stack': jax.random.normal(ks[5], (1, 5, E), jnp.float32) * 0.1, 'time_decay': jax.random.normal(ks[6], (E,), jnp.float32) * 0.5, 'td_w1': jax.random.normal(ks[7], (E, DD), jnp.float32) * sc, 'td_w2': jax.random.normal(ks[8], (DD, E), jnp.float32) * sc, 'u': jax.random.normal(ks[9], (H, S, 1), jnp.float32) * 0.1, 'Wr': jax.random.normal(ks[10], (E, E), jnp.float32) * sc, 'Wk': jax.random.normal(ks[11], (E, E), jnp.float32) * sc, 'Wv': jax.random.normal(ks[12], (E, E), jnp.float32) * sc, 'Wg': jax.random.normal(ks[13], (E, E), jnp.float32) * sc, 'Wo': jax.random.normal(ks[14], (E, E), jnp.float32) * sc, 'gn_w': jnp.ones((E,), jnp.float32), 'gn_b': jnp.zeros((E,), jnp.float32), 'ffn_maa_k': jax.random.normal(ks[15], (E,), jnp.float32) * 0.1, 'ffn_maa_r': jax.random.normal(ks[16], (E,), jnp.float32) * 0.1, 'Wfk': jax.random.normal(ks[17], (E, E), jnp.float32) * sc, 'Wfr': jax.random.normal(ks[18], (E, E), jnp.float32) * sc, 'Wfv': jax.random.normal(ks[19], (E, E), jnp.float32) * sc}
        return d
    _L3_xattn_all = _L3_xattn_setup()
    _L3_xattn_in = {k: v for k, v in _L3_xattn_all.items() if k in ('ln1_w', 'ln1_b', 'ln2_w', 'ln2_b', 'maa_x', 'maa_w1', 'maa_w2', 'maa_stack', 'time_decay', 'td_w1', 'td_w2', 'u', 'Wr', 'Wk', 'Wv', 'Wg', 'Wo', 'gn_w', 'gn_b', 'ffn_maa_k', 'ffn_maa_r', 'Wfk', 'Wfr', 'Wfv')}
    del _L3_xattn_all
    return {'x': x, 'ctx_2048': ctx_2048, 'mask_1x1xSxS2_fc1': mask_1x1xSxS2_fc1, 'mask_Bx1xSxS2_ff1': mask_Bx1xSxS2_ff1, 'L0_xattn_w_q': _L0_xattn_in['w_q'], 'L0_xattn_w_k': _L0_xattn_in['w_k'], 'L0_xattn_w_v': _L0_xattn_in['w_v'], 'L0_xattn_w_o': _L0_xattn_in['w_o'], 'L0_xattn_alpha': _L0_xattn_in['alpha'], 'L1_xattn_Wqkv0': _L1_xattn_in['Wqkv0'], 'L1_xattn_Wqkv1': _L1_xattn_in['Wqkv1'], 'L1_xattn_Winj0': _L1_xattn_in['Winj0'], 'L1_xattn_Winj1': _L1_xattn_in['Winj1'], 'L1_xattn_Wo': _L1_xattn_in['Wo'], 'L1_xattn_bo': _L1_xattn_in['bo'], 'L1_xattn_r_w_bias': _L1_xattn_in['r_w_bias'], 'L2_xattn_ln1_s': _L2_xattn_in['ln1_s'], 'L2_xattn_ln1_b': _L2_xattn_in['ln1_b'], 'L2_xattn_w_qkv': _L2_xattn_in['w_qkv'], 'L2_xattn_b_qkv': _L2_xattn_in['b_qkv'], 'L2_xattn_w_ao': _L2_xattn_in['w_ao'], 'L2_xattn_b_ao': _L2_xattn_in['b_ao'], 'L2_xattn_ln2_s': _L2_xattn_in['ln2_s'], 'L2_xattn_ln2_b': _L2_xattn_in['ln2_b'], 'L2_xattn_w_q': _L2_xattn_in['w_q'], 'L2_xattn_b_q': _L2_xattn_in['b_q'], 'L2_xattn_w_kv': _L2_xattn_in['w_kv'], 'L2_xattn_b_kv': _L2_xattn_in['b_kv'], 'L2_xattn_w_co': _L2_xattn_in['w_co'], 'L2_xattn_b_co': _L2_xattn_in['b_co'], 'L2_xattn_ln3_s': _L2_xattn_in['ln3_s'], 'L2_xattn_ln3_b': _L2_xattn_in['ln3_b'], 'L2_xattn_w1': _L2_xattn_in['w1'], 'L2_xattn_b1': _L2_xattn_in['b1'], 'L2_xattn_w2': _L2_xattn_in['w2'], 'L2_xattn_b2': _L2_xattn_in['b2'], 'L3_xattn_ln1_w': _L3_xattn_in['ln1_w'], 'L3_xattn_ln1_b': _L3_xattn_in['ln1_b'], 'L3_xattn_ln2_w': _L3_xattn_in['ln2_w'], 'L3_xattn_ln2_b': _L3_xattn_in['ln2_b'], 'L3_xattn_maa_x': _L3_xattn_in['maa_x'], 'L3_xattn_maa_w1': _L3_xattn_in['maa_w1'], 'L3_xattn_maa_w2': _L3_xattn_in['maa_w2'], 'L3_xattn_maa_stack': _L3_xattn_in['maa_stack'], 'L3_xattn_time_decay': _L3_xattn_in['time_decay'], 'L3_xattn_td_w1': _L3_xattn_in['td_w1'], 'L3_xattn_td_w2': _L3_xattn_in['td_w2'], 'L3_xattn_u': _L3_xattn_in['u'], 'L3_xattn_Wr': _L3_xattn_in['Wr'], 'L3_xattn_Wk': _L3_xattn_in['Wk'], 'L3_xattn_Wv': _L3_xattn_in['Wv'], 'L3_xattn_Wg': _L3_xattn_in['Wg'], 'L3_xattn_Wo': _L3_xattn_in['Wo'], 'L3_xattn_gn_w': _L3_xattn_in['gn_w'], 'L3_xattn_gn_b': _L3_xattn_in['gn_b'], 'L3_xattn_ffn_maa_k': _L3_xattn_in['ffn_maa_k'], 'L3_xattn_ffn_maa_r': _L3_xattn_in['ffn_maa_r'], 'L3_xattn_Wfk': _L3_xattn_in['Wfk'], 'L3_xattn_Wfr': _L3_xattn_in['Wfr'], 'L3_xattn_Wfv': _L3_xattn_in['Wfv']}

def reference(x, ctx_2048, mask_1x1xSxS2_fc1, mask_Bx1xSxS2_ff1, L0_xattn_w_q, L0_xattn_w_k, L0_xattn_w_v, L0_xattn_w_o, L0_xattn_alpha, L1_xattn_Wqkv0, L1_xattn_Wqkv1, L1_xattn_Winj0, L1_xattn_Winj1, L1_xattn_Wo, L1_xattn_bo, L1_xattn_r_w_bias, L2_xattn_ln1_s, L2_xattn_ln1_b, L2_xattn_w_qkv, L2_xattn_b_qkv, L2_xattn_w_ao, L2_xattn_b_ao, L2_xattn_ln2_s, L2_xattn_ln2_b, L2_xattn_w_q, L2_xattn_b_q, L2_xattn_w_kv, L2_xattn_b_kv, L2_xattn_w_co, L2_xattn_b_co, L2_xattn_ln3_s, L2_xattn_ln3_b, L2_xattn_w1, L2_xattn_b1, L2_xattn_w2, L2_xattn_b2, L3_xattn_ln1_w, L3_xattn_ln1_b, L3_xattn_ln2_w, L3_xattn_ln2_b, L3_xattn_maa_x, L3_xattn_maa_w1, L3_xattn_maa_w2, L3_xattn_maa_stack, L3_xattn_time_decay, L3_xattn_td_w1, L3_xattn_td_w2, L3_xattn_u, L3_xattn_Wr, L3_xattn_Wk, L3_xattn_Wv, L3_xattn_Wg, L3_xattn_Wo, L3_xattn_gn_w, L3_xattn_gn_b, L3_xattn_ffn_maa_k, L3_xattn_ffn_maa_r, L3_xattn_Wfk, L3_xattn_Wfr, L3_xattn_Wfv):
    import jax
    import jax.numpy as jnp

    def _L0_xattn_ref(h_english, h_lojban, w_q, w_k, w_v, w_o, alpha):
        import jax, jax.numpy as jnp
        import numpy as np
        H = 512
        B, L, S = (4, 1024, 10)
        h = h_english.shape[-1]
        q = jnp.einsum('blh,oh->blo', h_english, w_q)
        k = jnp.einsum('bsh,oh->bso', h_lojban, w_k)
        v = jnp.einsum('bsh,oh->bso', h_lojban, w_v)
        scores = jnp.einsum('blh,bsh->bls', q, k) / jnp.sqrt(jnp.float32(h))
        probs = jax.nn.softmax(scores, axis=-1)
        context = jnp.einsum('bls,bsh->blh', probs, v)
        delta = jnp.einsum('blh,oh->blo', context, w_o)
        return h_english + alpha * delta

    def _L1_xattn_ref(z1ss, u1ss, Wqkv0, Wqkv1, Winj0, Winj1, Wo, bo, r_w_bias):
        import jax, jax.numpy as jnp
        import numpy as np
        D_MODEL = 256
        N_HEAD = 16
        D_HEAD = 64
        IDX_LIST = [256, 512]
        SCALE = 1.0 / D_HEAD ** 0.5
        LN_EPS = 1e-05
        bsz, d_model, qlen = z1ss.shape
        bounds = [0] + IDX_LIST
        Wq_list, Wi_list = ([Wqkv0, Wqkv1], [Winj0, Winj1])
        chunks = []
        for i in range(len(IDX_LIST)):
            s, e = (bounds[i], bounds[i + 1])
            h = jnp.einsum('od,bdl->bol', Wq_list[i], z1ss[:, :, s:e])
            h = h + jnp.einsum('od,bdl->bol', Wi_list[i], u1ss[:, :, s:e])
            chunks.append(h)
        w_heads = jnp.concatenate(chunks, axis=2)
        q, k, v = jnp.split(w_heads, 3, axis=1)
        q = q[:, :, -qlen:]
        klen = k.shape[2]
        q = q.reshape(bsz, N_HEAD, D_HEAD, qlen)
        k = k.reshape(bsz, N_HEAD, D_HEAD, klen)
        v = v.reshape(bsz, N_HEAD, D_HEAD, klen)
        rq = q + r_w_bias[None, :, :, None]
        score = jnp.einsum('bndi,bndj->bnij', rq, k) * SCALE
        prob = jax.nn.softmax(score, axis=-1)
        attn_vec = jnp.einsum('bnij,bndj->bndi', prob, v)
        attn_vec = attn_vec.reshape(bsz, N_HEAD * D_HEAD, qlen)
        attn_out = jnp.einsum('od,bdl->bol', Wo, attn_vec) + bo[None, :, None]
        x = attn_out + z1ss
        m = jnp.mean(x, axis=1, keepdims=True)
        var = jnp.var(x, axis=1, keepdims=True)
        return (x - m) * jax.lax.rsqrt(var + LN_EPS)

    def _L2_xattn_ref(hidden_states, encoder_states, ltor_mask, cross_mask, ln1_s, ln1_b, w_qkv, b_qkv, w_ao, b_ao, ln2_s, ln2_b, w_q, b_q, w_kv, b_kv, w_co, b_co, ln3_s, ln3_b, w1, b1, w2, b2):
        import jax, jax.numpy as jnp
        import numpy as np
        H = 512
        NH = 16
        HD = H // NH
        EPS = 1e-05

        def gelu(x):
            return 0.5 * x * (1.0 + jnp.tanh(0.7978845608028654 * x * (1.0 + 0.044715 * x * x)))

        def layernorm(x, scale, bias):
            m = jnp.mean(x, axis=-1, keepdims=True)
            v = jnp.mean(jnp.square(x - m), axis=-1, keepdims=True)
            return (x - m) * jax.lax.rsqrt(v + EPS) * scale + bias

        def split_heads(x):
            b, s, _ = x.shape
            return x.reshape(b, s, NH, HD).transpose(0, 2, 1, 3)

        def merge_heads(x):
            b, nh, s, hd = x.shape
            return x.transpose(0, 2, 1, 3).reshape(b, s, nh * hd)

        def attention(q, k, v, mask):
            scores = jnp.einsum('bhqd,bhkd->bhqk', q, k) / jnp.sqrt(jnp.float32(HD))
            scores = scores * mask - 10000.0 * (1.0 - mask)
            probs = jax.nn.softmax(scores, axis=-1)
            return jnp.einsum('bhqk,bhkd->bhqd', probs, v)
        ln_out = layernorm(hidden_states, ln1_s, ln1_b)
        qkv = ln_out @ w_qkv + b_qkv
        q, k, v = jnp.split(qkv, 3, axis=-1)
        ctx = merge_heads(attention(split_heads(q), split_heads(k), split_heads(v), ltor_mask))
        attn_out = ctx @ w_ao + b_ao
        x = hidden_states + attn_out
        ln_out = layernorm(x, ln2_s, ln2_b)
        q = ln_out @ w_q + b_q
        kv = encoder_states @ w_kv + b_kv
        k, v = jnp.split(kv, 2, axis=-1)
        ctx = merge_heads(attention(split_heads(q), split_heads(k), split_heads(v), cross_mask))
        cross_out = ctx @ w_co + b_co
        x = x + cross_out
        ln_out = layernorm(x, ln3_s, ln3_b)
        mlp_out = gelu(ln_out @ w1 + b1) @ w2 + b2
        return x + mlp_out

    def _L3_xattn_ref(x, state, ln1_w, ln1_b, ln2_w, ln2_b, maa_x, maa_w1, maa_w2, maa_stack, time_decay, td_w1, td_w2, u, Wr, Wk, Wv, Wg, Wo, gn_w, gn_b, ffn_maa_k, ffn_maa_r, Wfk, Wfr, Wfv):
        import jax, jax.numpy as jnp
        import numpy as np
        E, H, L, B = (512, 32, 256, 4)
        S = E // H
        DM, DD = (32, 64)

        def _ln(x, w, b, eps=1e-05):
            m = x.mean(-1, keepdims=True)
            v = ((x - m) ** 2).mean(-1, keepdims=True)
            return (x - m) / jnp.sqrt(v + eps) * w + b

        def _block(x, state, ln1_w, ln1_b, ln2_w, ln2_b, maa_x, maa_w1, maa_w2, maa_stack, time_decay, td_w1, td_w2, u, Wr, Wk, Wv, Wg, Wo, gn_w, gn_b, ffn_maa_k, ffn_maa_r, Wfk, Wfr, Wfv):
            b, l, e = x.shape
            h = u.shape[0]
            s_ = e // h
            xa = _ln(x, ln1_w, ln1_b)
            sx = jnp.concatenate([state[:, 1:2] - xa[:, :1], xa[:, :-1] - xa[:, 1:]], axis=1)
            xxx = jnp.tanh((xa + sx * maa_x) @ maa_w1).reshape(b, l, 5, DM)
            xxx = jnp.einsum('blfd,fde->blfe', xxx, maa_w2)
            xm = xa[:, :, None] + sx[:, :, None] * (maa_stack + xxx)
            xk, xw, xv, xr, xg = (xm[:, :, j] for j in range(5))
            w = jnp.exp(-jnp.exp(time_decay + jnp.tanh(xw @ td_w1) @ td_w2)).reshape(b, l, h, s_)
            r = (xr @ Wr.T).reshape(b, l, h, s_)
            k = (xk @ Wk.T).reshape(b, l, h, s_)
            v = (xv @ Wv.T).reshape(b, l, h, s_)
            g = jax.nn.silu(xg @ Wg.T)
            s0 = state[:, 2:2 + s_].reshape(b, h, s_, s_)

            def step(s, rkvw):
                r_t, k_t, v_t, w_t = rkvw
                a = k_t[..., :, None] * v_t[..., None, :]
                out = jnp.einsum('bhi,bhij->bhj', r_t, u * a + s)
                s = a + w_t[..., :, None] * s
                return (s, out)
            rkvw = tuple((jnp.moveaxis(t, 1, 0) for t in (r, k, v, w)))
            _, out = jax.lax.scan(step, s0, rkvw)
            out = jnp.moveaxis(out, 0, 1).reshape(b, l, e)
            og = out.reshape(b, l, h, s_)
            m = og.mean(-1, keepdims=True)
            va = ((og - m) ** 2).mean(-1, keepdims=True)
            og = ((og - m) / jnp.sqrt(va + 1e-05)).reshape(b, l, e) * gn_w + gn_b
            x1 = x + og * g @ Wo.T
            xc = _ln(x1, ln2_w, ln2_b)
            sx2 = jnp.concatenate([state[:, 0:1] - xc[:, :1], xc[:, :-1] - xc[:, 1:]], axis=1)
            xk2 = xc + sx2 * ffn_maa_k
            xr2 = xc + sx2 * ffn_maa_r
            rr = jax.nn.sigmoid(xr2 @ Wfr.T)
            kk = jnp.square(jax.nn.relu(xk2 @ Wfk.T))
            return x1 + rr * (kk @ Wfv.T)
        return _block(x, state, ln1_w, ln1_b, ln2_w, ln2_b, maa_x, maa_w1, maa_w2, maa_stack, time_decay, td_w1, td_w2, u, Wr, Wk, Wv, Wg, Wo, gn_w, gn_b, ffn_maa_k, ffn_maa_r, Wfk, Wfr, Wfv)
    x = _L0_xattn_ref(x, ctx_2048, L0_xattn_w_q, L0_xattn_w_k, L0_xattn_w_v, L0_xattn_w_o, L0_xattn_alpha)
    x = _L1_xattn_ref(x, ctx_2048, L1_xattn_Wqkv0, L1_xattn_Wqkv1, L1_xattn_Winj0, L1_xattn_Winj1, L1_xattn_Wo, L1_xattn_bo, L1_xattn_r_w_bias)
    x = _L2_xattn_ref(x, ctx_2048, mask_1x1xSxS2_fc1, mask_Bx1xSxS2_ff1, L2_xattn_ln1_s, L2_xattn_ln1_b, L2_xattn_w_qkv, L2_xattn_b_qkv, L2_xattn_w_ao, L2_xattn_b_ao, L2_xattn_ln2_s, L2_xattn_ln2_b, L2_xattn_w_q, L2_xattn_b_q, L2_xattn_w_kv, L2_xattn_b_kv, L2_xattn_w_co, L2_xattn_b_co, L2_xattn_ln3_s, L2_xattn_ln3_b, L2_xattn_w1, L2_xattn_b1, L2_xattn_w2, L2_xattn_b2)
    x = _L3_xattn_ref(x, ctx_2048, L3_xattn_ln1_w, L3_xattn_ln1_b, L3_xattn_ln2_w, L3_xattn_ln2_b, L3_xattn_maa_x, L3_xattn_maa_w1, L3_xattn_maa_w2, L3_xattn_maa_stack, L3_xattn_time_decay, L3_xattn_td_w1, L3_xattn_td_w2, L3_xattn_u, L3_xattn_Wr, L3_xattn_Wk, L3_xattn_Wv, L3_xattn_Wg, L3_xattn_Wo, L3_xattn_gn_w, L3_xattn_gn_b, L3_xattn_ffn_maa_k, L3_xattn_ffn_maa_r, L3_xattn_Wfk, L3_xattn_Wfr, L3_xattn_Wfv)
    return x

_drawn_inputs = setup_inputs


def setup_inputs(seed=0):
    import zlib

    import numpy as np

    out = dict(_drawn_inputs(seed))
    spreads = {'L2_xattn_ln1_s': (1.0, 0.6),
     'L2_xattn_ln1_b': (0.0, 0.405),
     'L2_xattn_b_qkv': (0.0, 0.1),
     'L2_xattn_b_ao': (0.0, 0.1),
     'L2_xattn_ln2_s': (1.0, 0.6),
     'L2_xattn_ln2_b': (0.0, 0.8),
     'L2_xattn_b_q': (0.0, 2.0),
     'L2_xattn_b_kv': (0.0, 0.1),
     'L2_xattn_b_co': (0.0, 0.1),
     'L2_xattn_ln3_s': (1.0, 0.2),
     'L2_xattn_ln3_b': (0.0, 0.324),
     'L2_xattn_b1': (0.0, 0.1),
     'L2_xattn_b2': (0.0, 0.1),
     'L3_xattn_ln1_w': (1.0, 0.2),
     'L3_xattn_ln1_b': (0.0, 0.291),
     'L3_xattn_ln2_w': (1.0, 0.6),
     'L3_xattn_ln2_b': (0.0, 0.8),
     'L3_xattn_gn_w': (1.0, 0.6),
     'L3_xattn_gn_b': (0.0, 0.762)}
    factors = {'L0_xattn_w_q': 2.793,
     'L0_xattn_w_k': 2.837,
     'L0_xattn_w_v': 2.803,
     'L0_xattn_w_o': 2.805,
     'L1_xattn_Wqkv0': 7.834,
     'L1_xattn_Wqkv1': 7.864,
     'L1_xattn_Winj0': 6.787,
     'L1_xattn_Winj1': 6.733,
     'L1_xattn_Wo': 3.984,
     'L1_xattn_bo': 23.56,
     'L1_xattn_r_w_bias': 8.0,
     'L2_xattn_w_q': 7.063,
     'L3_xattn_maa_x': 8.0,
     'L3_xattn_maa_w1': 3.009,
     'L3_xattn_maa_w2': 3.047,
     'L3_xattn_td_w1': 8.0,
     'L3_xattn_td_w2': 8.0,
     'L3_xattn_u': 2.995,
     'L3_xattn_ffn_maa_k': 5.671,
     'L3_xattn_ffn_maa_r': 8.0,
     'L3_xattn_Wfr': 3.922}
    for name, (base, spread) in spreads.items():
        noise = np.random.default_rng([zlib.crc32(name.encode()), seed]).standard_normal(out[name].shape)
        drawn = base * np.exp(spread * noise) if base else spread * noise
        out[name] = jnp.asarray(drawn.astype(out[name].dtype))
    for name, factor in factors.items():
        out[name] = (out[name] * factor).astype(out[name].dtype)
    return out
```

```python
from contextlib import ExitStack

import concourse.bass as bass
from concourse import mybir

P = 128
ALU = mybir.AluOpType
ACT = mybir.ActivationFunctionType
AXIS = mybir.AxisListType
F32 = mybir.dt.float32

BATCH, TOK, FEAT = 8, 256, 512
TT, FT = TOK // P, FEAT // P


class Semaphores:

    def __init__(self, nc):
        self.nc, self.taken = nc, []

    def allocate(self, name):
        self.taken.append(self.nc.alloc_semaphore(name=name))
        return self.taken[-1]

    def clear(self):
        self.nc.clear_and_free_semaphores(self.taken)
        self.taken = []
        self.nc.all_engine_barrier()


def at(g, per_pass, k, unit=1):
    return (g * per_pass + k + 1) * unit


def open_loop(eng, sems):
    for s, count in sems:
        eng.sem_inc(s, count)


def make_identity(pool, ident, sem):
    pool.memset(ident[:, :], 0.0).then_inc(sem, 1)
    pool.wait_ge(sem, 1)
    pool.affine_select(out=ident[:, :], in_=ident[:, :], compare_op=ALU.not_equal, fill=1.0, base=0,
                       pattern=[[-1, P]], channel_multiplier=1).then_inc(sem, 1)


def context_attention(nc, semaphores, x, xT, cT, w_q, w_k, w_v, w_oT, alpha, x1):
    PAIRS = BATCH // 2
    SCALE = float(FEAT) ** -0.5
    with ExitStack() as ctx:
        def sb(name, shape):
            return ctx.enter_context(nc.sbuf_tensor("l0_" + name, shape, F32))

        def ps(name, shape):
            return ctx.enter_context(nc.psum_tensor("l0_" + name, shape, F32))

        loop_sems = []

        def sem(name, credit=0):
            s = semaphores.allocate("l0_" + name)
            if credit:
                loop_sems.append((s, credit))
            return s

        def slots(name, credit=1):
            return [sem(f"{name}{u}", credit) for u in range(2)]

        wq, wk, wv, wo = (sb(n, [P, FT, FEAT]) for n in ("wq", "wk", "wv", "wo"))
        qk, vo = sb("qk", [P, FT, FEAT]), sb("vo", [P, FT, FEAT])
        ident = sb("ident", [P, P])
        alpha_col = sb("alpha_col", [P, 1])
        xt = [sb(f"xt{u}", [P, FT, TOK]) for u in range(2)]
        ct = [sb(f"ct{u}", [P, FT, TOK]) for u in range(2)]
        xn = [sb(f"xn{u}", [P, TT, FEAT]) for u in range(2)]
        yt = [sb(f"yt{u}", [P, FT, TOK]) for u in range(2)]
        cv = [sb(f"cv{u}", [P, TT, FEAT]) for u in range(2)]
        pr = [sb(f"pr{u}", [P, TT, TOK]) for u in range(2)]
        prT = [sb(f"prT{u}", [P, TT, TOK]) for u in range(2)]
        res = [sb(f"res{u}", [P, TT, FEAT]) for u in range(2)]
        top = [sb(f"top{u}", [P, TT]) for u in range(2)]
        shift = [sb(f"shift{u}", [P, TT]) for u in range(2)]
        mass = [sb(f"mass{u}", [P, TT]) for u in range(2)]
        gain = [sb(f"gain{u}", [P, TT]) for u in range(2)]

        ps_y = ps("ps_y", [P, FT, TOK])
        ps_cv = ps("ps_cv", [P, TT, FEAT])
        ps_s = ps("ps_s", [P, TT, TOK])
        ps_t = ps("ps_t", [P, TT, TOK])
        ps_d = ps("ps_d", [P, TT, FEAT])

        ident_made, w_loaded, alpha_loaded = sem("ident_made"), sem("w_loaded"), sem("alpha_loaded")
        wv_loaded = sem("wv_loaded")
        qk_summed, qk_kept, vo_summed, vo_kept = sem("qk_summed"), sem("qk_kept"), sem("vo_summed"), sem("vo_kept")
        loaded = slots("loaded", 48)
        stored = slots("stored", 16)
        y_summed = slots("y_summed")
        y_kept = slots("y_kept")
        cv_summed = slots("cv_summed")
        cv_kept = slots("cv_kept")
        scored = slots("scored")
        shifted = slots("shifted")
        probs_made = slots("probs_made")
        turned = slots("turned")
        turned_kept = slots("turned_kept")
        gained = slots("gained")
        delta_summed = slots("delta_summed")
        added = slots("added")
        inverted, topped = slots("inverted"), slots("topped")

        block = ctx.enter_context(nc.Block())

        @block.sync
        def _(sp):
            open_loop(sp, loop_sems)
            for w, src in ((wq, w_q), (wk, w_k)):
                sp.dma_start(w[:, :, :], src.rearrange("(t p) n -> p t n", p=P)).then_inc(w_loaded, 16)
            for w, src in ((wv, w_v), (wo, w_oT)):
                sp.dma_start(w[:, :, :], src.rearrange("(t p) n -> p t n", p=P)).then_inc(wv_loaded, 16)
            sp.dma_start(alpha_col[:, :], alpha.to_broadcast([P, 1])).then_inc(alpha_loaded, 16)
            with sp.Fori(1, PAIRS + 1) as g:
                for u in range(2):
                    b = 2 * g - 2 + u
                    sp.wait_ge(scored[u], g)
                    sp.wait_ge(added[u], g)
                    sp.dma_start(xt[u][:, :, :], xT[bass.ds(b, 1), :, :].rearrange("o (t p) n -> p (o t) n", p=P)).then_inc(loaded[u], 16)
                    sp.dma_start(ct[u][:, :, :], cT[bass.ds(b, 1), :, :].rearrange("o (t p) n -> p (o t) n", p=P)).then_inc(loaded[u], 16)
                    sp.dma_start(xn[u][:, :, :], x[bass.ds(b, 1), :, :].rearrange("o (t p) n -> p (o t) n", p=P)).then_inc(loaded[u], 16)

        @block.gpsimd
        def _(pool):
            make_identity(pool, ident, ident_made)

        @block.tensor
        def _(pe):
            pe.wait_ge(w_loaded, 32)
            for m in range(FT):
                for t in range(FT):
                    mm = pe.matmul(ps_y[:, 2 * (m % 2):2 * (m % 2) + 2, :] if m < 2 else ps_cv[:, m - 2, :],
                                   wq[:, t, m * P:(m + 1) * P], wk[:, t, :], start=(t == 0), stop=(t == FT - 1))
                mm.then_inc(qk_summed, 1)
            pe.wait_ge(wv_loaded, 32)
            pe.wait_ge(qk_kept, FT)
            for m in range(FT):
                for t in range(FT):
                    mm = pe.matmul(ps_y[:, 2 * (m % 2):2 * (m % 2) + 2, :] if m < 2 else ps_cv[:, m - 2, :],
                                   wv[:, t, m * P:(m + 1) * P], wo[:, t, :], start=(t == 0), stop=(t == FT - 1))
                mm.then_inc(vo_summed, 1)
            pe.wait_ge(vo_kept, FT)
            pe.wait_ge(ident_made, 2)
            with pe.Fori(1, PAIRS + 1) as g:
                def project_queries(u):
                    pe.wait_ge(loaded[u], 48 * g + 48)
                    if u == 1:
                        pe.wait_ge(y_kept[0], g + 1)
                    for m in range(FT):
                        for t in range(FT):
                            mm = pe.matmul(ps_y[:, m, :], qk[:, t, m * P:(m + 1) * P], xt[u][:, t, :],
                                           start=(t == 0), stop=(t == FT - 1))
                    mm.then_inc(y_summed[u], 1)

                def project_values(u):
                    if u == 1:
                        pe.wait_ge(cv_kept[0], g + 1)
                    for m in range(TT):
                        for t in range(FT):
                            mm = pe.matmul(ps_cv[:, m, :], ct[u][:, t, m * P:(m + 1) * P], vo[:, t, :],
                                           start=(t == 0), stop=(t == FT - 1))
                    mm.then_inc(cv_summed[u], 1)

                def score(u):
                    pe.wait_ge(y_kept[u], g + 1)
                    if u == 1:
                        pe.wait_ge(probs_made[0], g + 1)
                    for m in range(TT):
                        for t in range(FT):
                            mm = pe.matmul(ps_s[:, m, :], yt[u][:, t, m * P:(m + 1) * P], ct[u][:, t, :],
                                           start=(t == 0), stop=(t == FT - 1))
                    mm.then_inc(scored[u], 1)

                def turn(u):
                    pe.wait_ge(probs_made[u], g + 1)
                    if u == 1:
                        pe.wait_ge(turned_kept[0], g + 1)
                    for m in range(TT):
                        for t in range(TT):
                            mm = pe.transpose(ps_t[:, t, m * P:(m + 1) * P], pr[u][:, m, t * P:(t + 1) * P], ident[:, :])
                    mm.then_inc(turned[u], 1)

                def mix(u):
                    pe.wait_ge(turned_kept[u], g + 1)
                    pe.wait_ge(cv_kept[u], g + 1)
                    if u == 1:
                        pe.wait_ge(added[0], g + 1)
                    else:
                        pe.wait_ge(added[1], g)
                    for m in range(TT):
                        for t in range(TT):
                            mm = pe.matmul(ps_d[:, m, :], prT[u][:, t, m * P:(m + 1) * P], cv[u][:, t, :],
                                           start=(t == 0), stop=(t == TT - 1))
                    mm.then_inc(delta_summed[u], 1)

                project_queries(0)
                project_values(0)
                project_queries(1)
                score(0)
                project_values(1)
                turn(0)
                score(1)
                mix(0)
                turn(1)
                mix(1)

        @block.scalar
        def _(act):
            for m in range(FT):
                act.wait_ge(qk_summed, m + 1)
                act.activation(qk[:, m, :], ps_y[:, 2 * m:2 * m + 2, :].rearrange("p a b -> p (a b)") if m < 2 else ps_cv[:, m - 2, :],
                               ACT.Copy).then_inc(qk_kept, 1)
            for m in range(FT):
                act.wait_ge(vo_summed, m + 1)
                act.activation(vo[:, m, :], ps_y[:, 2 * m:2 * m + 2, :].rearrange("p a b -> p (a b)") if m < 2 else ps_cv[:, m - 2, :],
                               ACT.Copy).then_inc(vo_kept, 1)
            with act.Fori(1, PAIRS + 1) as g:
                def keep_queries(u):
                    act.wait_ge(y_summed[u], g + 1)
                    act.activation(yt[u][:, :, :], ps_y[:, :, :], ACT.Copy).then_inc(y_kept[u], 1)

                def exponentials(u):
                    act.wait_ge(shifted[u], g + 1)
                    act.wait_ge(turned[u], g)
                    act.wait_ge(gained[u], g)
                    for m in range(TT):
                        ins = act.activation(pr[u][:, m, :], ps_s[:, m, :], ACT.Exp, bias=shift[u][:, m:m + 1],
                                             scale=SCALE, accum_out=mass[u][:, m:m + 1])
                    ins.then_inc(probs_made[u], 1)

                def store(u):
                    act.wait_ge(added[u], g + 1)
                    act.dma_start(x1[bass.ds(2 * g - 2 + u, 1), :, :].rearrange("o (t p) n -> p (o t) n", p=P),
                                  res[u][:, :, :]).then_inc(stored[u], 16)

                keep_queries(0)
                keep_queries(1)
                exponentials(0)
                exponentials(1)
                store(0)
                store(1)
            for u in range(2):
                act.wait_ge(stored[u], 16 * (PAIRS + 1))

        @block.vector
        def _(dve):
            dve.wait_ge(alpha_loaded, 16)
            with dve.Fori(1, PAIRS + 1) as g:
                def keep_values(u):
                    dve.wait_ge(cv_summed[u], g + 1)
                    dve.tensor_copy(cv[u][:, :, :], ps_cv[:, :, :]).then_inc(cv_kept[u], 1)

                def row_max(u):
                    dve.wait_ge(scored[u], g + 1)
                    dve.wait_ge(probs_made[u], g)
                    dve.tensor_reduce(top[u][:, :], ps_s[:, :, :], AXIS.X, ALU.max, negate=True).then_inc(topped[u], 1)
                    dve.wait_ge(topped[u], g + 1)
                    dve.tensor_scalar(shift[u][:, :], top[u][:, :], SCALE, None, ALU.mult).then_inc(shifted[u], 1)

                def keep_turned(u):
                    dve.wait_ge(turned[u], g + 1)
                    dve.wait_ge(probs_made[u], g + 1)
                    dve.tensor_copy(prT[u][:, :, :], ps_t[:, :, :]).then_inc(turned_kept[u], 1)
                    dve.reciprocal(gain[u][:, :], mass[u][:, :]).then_inc(inverted[u], 1)
                    dve.wait_ge(inverted[u], g + 1)
                    dve.tensor_scalar(gain[u][:, :], gain[u][:, :], alpha_col[:, 0:1], None, ALU.mult).then_inc(gained[u], 1)

                def add(u):
                    dve.wait_ge(delta_summed[u], g + 1)
                    dve.wait_ge(gained[u], g + 1)
                    dve.wait_ge(stored[u], 16 * g)
                    for m in range(TT):
                        ins = dve.scalar_tensor_tensor(out=res[u][:, m, :], in0=ps_d[:, m, :], scalar=gain[u][:, m:m + 1],
                                                       in1=xn[u][:, m, :], op0=ALU.mult, op1=ALU.add)
                    ins.then_inc(added[u], 1)

                keep_values(0)
                row_max(0)
                keep_values(1)
                keep_turned(0)
                row_max(1)
                add(0)
                keep_turned(1)
                add(1)


def channel_attention(nc, semaphores, z, c, w_qkv0T, w_inj0T, w_qkv1T, w_inj1T, w_oT, bo, q_bias, out):
    HEADS, DH = 16, 64
    INNER = HEADS * DH
    HP = HEADS // 2
    QT = FEAT // P
    STEPS = HP * QT
    PV_LAG = QT + 1
    SCALE = DH ** -0.5
    CT = TOK // P
    with ExitStack() as ctx:
        def sb(name, shape):
            return ctx.enter_context(nc.sbuf_tensor("l1_" + name, shape, F32))

        def ps(name, shape):
            return ctx.enter_context(nc.psum_tensor("l1_" + name, shape, F32))

        loop_sems = []

        def sem(name, credit=0):
            s = semaphores.allocate("l1_" + name)
            if credit:
                loop_sems.append((s, credit))
            return s

        w = [sb(f"w{i}", [P, CT, 3 * INNER]) for i in range(4)]
        wo = sb("wo", [P, HP, TOK])
        ident, mean_of = sb("ident", [P, P]), sb("mean_of", [P, P])
        bo_col, qb_col, qb_scaled = sb("bo_col", [P, CT]), sb("qb_col", [P, HP]), sb("qb_scaled", [P, HP])
        zt, ut, zres = sb("zt", [P, CT, FEAT]), sb("ut", [P, CT, FEAT]), sb("zres", [P, CT, FEAT])
        q = [sb(f"q{i}", [P, FEAT]) for i in range(2)]
        k = [sb(f"k{i}", [P, FEAT]) for i in range(2)]
        vo = sb("vo", [P, HP, QT, P])
        pr = [sb(f"pr{i}", [P, 2, FEAT]) for i in range(2)]
        pT = [[sb(f"pT{i}{h}", [P, QT, FEAT]) for h in range(2)] for i in range(2)]
        shift = [sb(f"shift{i}", [P, 2]) for i in range(2)]
        mass = [sb(f"mass{i}", [P, 2]) for i in range(2)]
        inv = [sb(f"inv{i}", [P, 2]) for i in range(2)]
        xr = pT[0][0][:, 0:CT, :]
        sq = pT[0][0][:, CT:2 * CT, :]
        rstd = pT[0][1][:, 0, :]
        res = sb("res", [P, CT, FEAT])

        ps_q, ps_k = ps("ps_q", [P, FEAT]), ps("ps_k", [P, FEAT])
        ps_s = ps("ps_s", [P, 2, FEAT])
        ps_t = [ps(f"ps_t{h}", [P, QT, P]) for h in range(2)]
        ps_o = [ps(f"ps_o{i}", [P, FEAT]) for i in range(2)]

        consts_made, ident_made = sem("consts_made"), sem("ident_made")
        v_w_loaded, qk_w_loaded, o_w_loaded, cols_loaded = (sem(n) for n in ("v_w_loaded", "qk_w_loaded", "o_w_loaded", "cols_loaded"))
        zu_loaded, zres_loaded, stored = sem("zu_loaded", 32), sem("zres_loaded", 16), sem("stored", 16)
        v_summed, v_kept_act, v_kept_dve = sem("v_summed", 8), sem("v_kept_act", 4), sem("v_kept_dve", 4)
        q_summed, k_summed, q_kept, k_kept = (sem(n, HP) for n in ("q_summed", "k_summed", "q_kept", "k_kept"))
        scored, shifted, exped, inverted, scaled, turned, kept_t0, kept_t1 = (
            sem(n, STEPS) for n in ("scored", "shifted", "exped", "inverted", "scaled", "turned", "kept_t0", "kept_t1"))
        o_summed, o_kept = sem("o_summed", HP), sem("o_kept", HP)
        attn_summed, added, means_summed, centred, squared, vars_summed, rooted, normed = (
            sem(n, 1) for n in ("attn_summed", "added", "means_summed", "centred", "squared", "vars_summed", "rooted", "normed"))
        inv_var = sem("inv_var", 2)

        block = ctx.enter_context(nc.Block())

        @block.sync
        def _(sp):
            open_loop(sp, loop_sems)
            w_dram = [a.rearrange("(t p) n -> p t n", p=P) for a in (w_qkv0T, w_inj0T, w_qkv1T, w_inj1T)]
            for lo, hi, s in ((2 * INNER, 3 * INNER, v_w_loaded), (0, 2 * INNER, qk_w_loaded)):
                for i in range(4):
                    sp.dma_start(w[i][:, :, lo:hi], w_dram[i][:, :, lo:hi]).then_inc(s, 16)
            sp.dma_start(bo_col[:, :], bo).then_inc(cols_loaded, 16)
            sp.dma_start(qb_col[:, :], q_bias).then_inc(cols_loaded, 16)
            sp.dma_start(wo[:, :, :], w_oT.rearrange("(t p) n -> p t n", p=P)).then_inc(o_w_loaded, 16)
            with sp.Fori(1, BATCH + 1) as g:
                def rows(a):
                    return a[bass.ds(g - 1, 1), :, :].rearrange("o (t p) n -> p (o t) n", p=P)

                sp.wait_ge(k_summed, at(g, HP, -1))
                sp.wait_ge(q_summed, at(g, HP, -1))
                sp.dma_start(zt[:, :, :], rows(z)).then_inc(zu_loaded, 16)
                sp.dma_start(ut[:, :, :], rows(c)).then_inc(zu_loaded, 16)
                sp.wait_ge(added, at(g, 1, -1))
                sp.dma_start(zres[:, :, :], rows(z)).then_inc(zres_loaded, 16)

        @block.tensor
        def _(pe):
            pe.wait_ge(ident_made, 2)
            pe.wait_ge(consts_made, 2)
            with pe.Fori(1, BATCH + 1) as g:
                def project(pair, part, half):
                    bank, kept, summed = (ps_q, q_kept, q_summed) if part == 0 else (ps_k, k_kept, k_summed)
                    if half == 0:
                        pe.wait_ge(kept, at(g, HP, pair - 1))
                    cols = slice(part * INNER + pair * P, part * INNER + (pair + 1) * P)
                    here = slice(half * TOK, (half + 1) * TOK)
                    terms = [(w[2 * half + i], src, t) for i, src in enumerate((zt, ut)) for t in range(CT)]
                    for i, (wt, src, t) in enumerate(terms):
                        mm = pe.matmul(bank[:, here], wt[:, t, cols], src[:, t, here],
                                       start=(i == 0), stop=(i == len(terms) - 1), skip_group_check=True)
                    if half == 1:
                        mm.then_inc(summed, 1)

                def score(n):
                    pair = n // QT
                    if n % QT == 0:
                        pe.wait_ge(q_kept, at(g, HP, pair))
                        pe.wait_ge(k_kept, at(g, HP, pair))
                    pe.wait_ge(exped, at(g, STEPS, n - 1))
                    for h in range(2):
                        rows = slice(h * DH, (h + 1) * DH)
                        mm = pe.matmul(ps_s[:, h, :], q[pair % 2][rows, (n % QT) * P:(n % QT + 1) * P],
                                       k[pair % 2][rows, :], start=True, stop=True)
                    mm.then_inc(scored, 1)

                def turn(n):
                    pe.wait_ge(scaled, at(g, STEPS, n))
                    pe.wait_ge(kept_t0, at(g, STEPS, n - 1))
                    pe.wait_ge(kept_t1, at(g, STEPS, n - 1))
                    for h in range(2):
                        for t in range(QT):
                            mm = pe.transpose(ps_t[h][:, t, :], pr[n % 2][:, h, t * P:(t + 1) * P], ident[:, :])
                    mm.then_inc(turned, 1)

                def mix(n):
                    pair, t = n // QT, n % QT
                    if t == 0:
                        pe.wait_ge(kept_t0, at(g, STEPS, n + QT - 1))
                        pe.wait_ge(kept_t1, at(g, STEPS, n + QT - 1))
                        pe.wait_ge(o_kept, at(g, HP, pair - 2))
                    for h in range(2):
                        rows = slice(h * DH, (h + 1) * DH)
                        mm = pe.matmul(ps_o[pair % 2][rows, :], vo[:, pair, t, rows], pT[pair % 2][h][:, t, :],
                                       start=(t == 0), stop=(t == QT - 1))
                    if t == QT - 1:
                        mm.then_inc(o_summed, 1)

                pe.wait_ge(zu_loaded, at(g, 2, 1, 16))
                pe.wait_ge(v_w_loaded, 64)
                v_banks = [ps_t[0][:, :, :], ps_t[1][:, :, :], ps_o[0][:, :], ps_o[1][:, :]]
                for e in range(8):
                    lt, chunk = e // 2, e % 2
                    if e >= 4:
                        pe.wait_ge((v_kept_act, v_kept_dve)[e % 2], at(g, 4, e // 2 - 2))
                    elif e == 0:
                        pe.wait_ge(attn_summed, at(g, 1, -1))
                    terms = [(w[2 * (lt // 2) + i], src, t) for i, src in enumerate((zt, ut)) for t in range(CT)]
                    for i, (wt, src, t) in enumerate(terms):
                        mm = pe.matmul(v_banks[e % 4], src[:, t, lt * P:(lt + 1) * P],
                                       wt[:, t, 2 * INNER + chunk * FEAT:2 * INNER + (chunk + 1) * FEAT],
                                       start=(i == 0), stop=(i == len(terms) - 1))
                    mm.then_inc(v_summed, 1)
                pe.wait_ge(qk_w_loaded, 64)
                pe.wait_ge(added, at(g, 1, -1))
                for part in range(2):
                    for half in range(2):
                        project(0, part, half)
                pe.wait_ge(normed, at(g, 1, -1))
                pe.wait_ge(v_kept_act, at(g, 4, 3))
                pe.wait_ge(v_kept_dve, at(g, 4, 3))
                for n in range(STEPS + PV_LAG):
                    if n < STEPS:
                        score(n)
                        if n // QT + 1 < HP:
                            project(n // QT + 1, n % QT // 2, n % 2)
                    if 1 <= n <= STEPS:
                        turn(n - 1)
                    if n >= PV_LAG:
                        mix(n - PV_LAG)
                pe.wait_ge(o_w_loaded, 16)
                pe.wait_ge(o_kept, at(g, HP, HP - 1))
                pe.wait_ge(q_kept, at(g, HP, HP - 1))
                pe.wait_ge(k_kept, at(g, HP, HP - 1))
                for m, bank in enumerate((ps_q, ps_k)):
                    for t in range(HP):
                        mm = pe.matmul(bank[:, :], wo[:, t, m * P:(m + 1) * P],
                                       vo[:, t, :, :], start=(t == 0), stop=(t == HP - 1))
                mm.then_inc(attn_summed, 1)
                pe.wait_ge(added, at(g, 1, 0))
                for t in range(CT):
                    mm = pe.matmul(ps_s[:, 0, :], mean_of[:, :], xr[:, t, :], start=(t == 0), stop=(t == CT - 1))
                mm.then_inc(means_summed, 1)
                pe.wait_ge(squared, at(g, 1, 0))
                for t in range(CT):
                    mm = pe.matmul(ps_s[:, 1, :], mean_of[:, :], sq[:, t, :], start=(t == 0), stop=(t == CT - 1))
                mm.then_inc(vars_summed, 1)

        @block.scalar
        def _(act):
            act.wait_ge(consts_made, 2)
            with act.Fori(1, BATCH + 1) as g:
                def keep_values(e):
                    act.wait_ge(v_summed, at(g, 8, e))
                    lt, chunk = e // 2, e % 2
                    act.activation(vo[:, chunk * 4:(chunk + 1) * 4, lt, :],
                                   (ps_t[0][:, :, :] if e % 4 == 0 else ps_o[0][:, :].rearrange("p (a b) -> p a b", b=P)),
                                   ACT.Copy).then_inc(v_kept_act, 1)

                def keep_queries(pair):
                    act.wait_ge(q_summed, at(g, HP, pair))
                    act.wait_ge(scored, at(g, STEPS, (pair - 1) * QT - 1))
                    act.activation(q[pair % 2][:, :], ps_q[:, :], ACT.Identity, bias=qb_scaled[:, pair:pair + 1],
                                   scale=SCALE).then_inc(q_kept, 1)

                def exponentials(n):
                    act.wait_ge(shifted, at(g, STEPS, n))
                    act.wait_ge(turned, at(g, STEPS, n - 2))
                    act.wait_ge(inverted, at(g, STEPS, n - 2))
                    for h in range(2):
                        ins = act.activation(pr[n % 2][:, h, :], ps_s[:, h, :], ACT.Exp, bias=shift[n % 2][:, h:h + 1],
                                             accum_out=mass[n % 2][:, h:h + 1])
                    ins.then_inc(exped, 1)

                def keep_turned(n):
                    pair, t = n // QT, n % QT
                    act.wait_ge(turned, at(g, STEPS, n))
                    if t == 0:
                        act.wait_ge(o_summed, at(g, HP, pair - 2))
                    act.activation(pT[pair % 2][0][:, :, t * P:(t + 1) * P], ps_t[0][:, :, :], ACT.Copy).then_inc(kept_t0, 1)

                def keep_output(pair):
                    act.wait_ge(o_summed, at(g, HP, pair))
                    act.activation(vo[:, pair, :, :].rearrange("p a b -> p (a b)"), ps_o[pair % 2][:, :], ACT.Copy).then_inc(o_kept, 1)

                for e in range(0, 8, 2):
                    keep_values(e)
                keep_queries(0)
                for n in range(STEPS + PV_LAG):
                    if n < STEPS:
                        exponentials(n)
                        if n % QT == 1 and n // QT + 1 < HP:
                            keep_queries(n // QT + 1)
                    if 1 <= n <= STEPS:
                        keep_turned(n - 1)
                    if n >= PV_LAG and (n - PV_LAG) % QT == QT - 1:
                        keep_output((n - PV_LAG) // QT)
                act.wait_ge(centred, at(g, 1, 0))
                act.activation(sq, res[:, :, :], ACT.Square).then_inc(squared, 1)
                act.wait_ge(inv_var, at(g, 2, 1))
                act.activation(rstd, rstd, ACT.Sqrt).then_inc(rooted, 1)
                act.wait_ge(normed, at(g, 1, 0))
                act.dma_start(out[bass.ds(g - 1, 1), :, :].rearrange("o (t p) n -> p (o t) n", p=P),
                              res[:, :, :]).then_inc(stored, 16)
            act.wait_ge(stored, 16 * (BATCH + 1))

        @block.gpsimd
        def _(pool):
            make_identity(pool, ident, ident_made)
            with pool.Fori(1, BATCH + 1) as g:
                for n in range(STEPS):
                    pool.wait_ge(inverted, at(g, STEPS, n))
                    pool.tensor_tensor(pr[n % 2][:, :, :], pr[n % 2][:, :, :],
                                       inv[n % 2][:, :].unsqueeze(2).to_broadcast([P, 2, FEAT]), ALU.mult).then_inc(scaled, 1)

        @block.vector
        def _(dve):
            dve.memset(mean_of[:, :], 1.0 / TOK).then_inc(consts_made, 1)
            dve.wait_ge(cols_loaded, 32)
            dve.tensor_scalar(qb_scaled[:, :], qb_col[:, :], SCALE, None, ALU.mult).then_inc(consts_made, 1)
            with dve.Fori(1, BATCH + 1) as g:
                def keep_values(e):
                    dve.wait_ge(v_summed, at(g, 8, e))
                    lt, chunk = e // 2, e % 2
                    dve.tensor_copy(vo[:, chunk * 4:(chunk + 1) * 4, lt, :],
                                    (ps_t[1][:, :, :] if e % 4 == 1 else ps_o[1][:, :].rearrange("p (a b) -> p a b", b=P))
                                    ).then_inc(v_kept_dve, 1)

                def keep_keys(pair):
                    dve.wait_ge(k_summed, at(g, HP, pair))
                    dve.wait_ge(scored, at(g, STEPS, (pair - 1) * QT - 1))
                    dve.tensor_copy(k[pair % 2][:, :], ps_k[:, :]).then_inc(k_kept, 1)

                def shifts(n):
                    dve.wait_ge(scored, at(g, STEPS, n))
                    dve.wait_ge(exped, at(g, STEPS, n - 2))
                    dve.tensor_reduce(shift[n % 2][:, :], ps_s[:, :, :], AXIS.X, ALU.max, negate=True).then_inc(shifted, 1)

                def inverses(n):
                    dve.wait_ge(exped, at(g, STEPS, n))
                    dve.wait_ge(scaled, at(g, STEPS, n - 2))
                    dve.reciprocal(inv[n % 2][:, :], mass[n % 2][:, :]).then_inc(inverted, 1)

                def keep_turned(n):
                    pair, t = n // QT, n % QT
                    dve.wait_ge(turned, at(g, STEPS, n))
                    if t == 0:
                        dve.wait_ge(o_summed, at(g, HP, pair - 2))
                    dve.tensor_copy(pT[pair % 2][1][:, :, t * P:(t + 1) * P], ps_t[1][:, :, :]).then_inc(kept_t1, 1)

                for e in range(1, 8, 2):
                    keep_values(e)
                keep_keys(0)
                for n in range(STEPS + 1):
                    if n < STEPS:
                        shifts(n)
                        inverses(n)
                    if n >= 1:
                        keep_turned(n - 1)
                    if n % QT == QT - 1 and n // QT + 1 < HP:
                        keep_keys(n // QT + 1)
                dve.wait_ge(attn_summed, at(g, 1, 0))
                dve.wait_ge(zres_loaded, at(g, 1, 0, 16))
                dve.wait_ge(stored, at(g, 1, -1, 16))
                for m, bank in enumerate((ps_q, ps_k)):
                    ins = dve.scalar_tensor_tensor(out=xr[:, m, :], in0=bank[:, :], scalar=bo_col[:, m:m + 1],
                                                   in1=zres[:, m, :], op0=ALU.add, op1=ALU.add)
                ins.then_inc(added, 1)
                dve.wait_ge(means_summed, at(g, 1, 0))
                for m in range(CT):
                    ins = dve.tensor_tensor(res[:, m, :], xr[:, m, :], ps_s[:, 0, :], ALU.subtract)
                ins.then_inc(centred, 1)
                dve.wait_ge(vars_summed, at(g, 1, 0))
                dve.tensor_scalar(rstd, ps_s[:, 1, :], 1e-5, None, ALU.add).then_inc(inv_var, 1)
                dve.wait_ge(inv_var, at(g, 2, 0))
                dve.reciprocal(rstd, rstd).then_inc(inv_var, 1)
                dve.wait_ge(rooted, at(g, 1, 0))
                for m in range(CT):
                    ins = dve.tensor_tensor(res[:, m, :], res[:, m, :], rstd, ALU.mult)
                ins.then_inc(normed, 1)


def token_attention(nc, semaphores, tag, x, cT, mask, mask_batches, ln_cols, wq_d, wk_d, wv_d, wo_d, qk_cols, rows, out):
    HEADS, DH = 16, 32
    STEPS = HEADS // 2
    TILE_HEADS = P // DH
    RING = 4
    PASSES = BATCH // 2
    SCALE = DH ** -0.5
    CROSS = cT is not None
    ORDER = ("K0", "K1", "T0", "T1", "Q0", "Q1", "V0", "V1") if CROSS else ("T0", "T1", "Q0", "Q1", "K0", "K1", "V0", "V1")
    FILL = dict(zip((0, 1, 2, 3, 4, 5, 8, 10) if CROSS else (1, 2, 3, 4, 5, 6, 8, 10), ORDER))
    LOADS = 3 if CROSS else 2
    TURN_LAG, MIX_LAG = 2, 3
    LAST = STEPS + MIX_LAG
    with ExitStack() as ctx:
        def sb(name, shape):
            return ctx.enter_context(nc.sbuf_tensor(f"{tag}_{name}", shape, F32))

        def ps(name, shape):
            return ctx.enter_context(nc.psum_tensor(f"{tag}_{name}", shape, F32))

        loop_sems = []

        def sem(name, per_batch=0):
            s = semaphores.allocate(f"{tag}_{name}")
            if per_batch:
                loop_sems.append((s, 2 * per_batch))
            return s

        wq, wk, wv, wo = (sb(n, [P, FT, FEAT]) for n in ("wq", "wk", "wv", "wo"))
        ln_sb, qk_sb = sb("ln_cols", [P, 2, FT]), sb("qk_cols", [P, 2, FT])
        rows_sb = sb("rows", [P, 2, FEAT])
        ident = sb("ident", [P, P])
        half_power = sb("half_power", [P, TT])
        xs = [sb(f"xs{u}", [P, TT, FEAT]) for u in range(2)]
        cs = [sb(f"cs{u}", [P, FT, TOK]) for u in range(2)] if CROSS else None
        mk = [sb(f"mk{u}", [P, TT, TOK]) for u in range(2)]
        ma = [sb(f"ma{u}", [P, TT, TOK]) for u in range(2)]
        stats, moments, var_eps, rstd = sb("stats", [P, TT, 6]), sb("moments", [P, TT, 2]), sb("var_eps", [P, TT]), sb("rstd", [P, TT])
        xn = sb("xn", [P, TT, FEAT])
        lnT = sb("lnT", [P, FT, TOK])
        qT = [sb(f"qT{u}", [P, FT, TOK]) for u in range(2)]
        kT = [sb(f"kT{u}", [P, FT, TOK]) for u in range(2)]
        v = [sb(f"v{u}", [P, TT, FEAT]) for u in range(2)]
        pr = [sb(f"pr{i}", [P, 2, TT, TOK]) for i in range(RING)]
        pT = [sb(f"pT{i}", [P, 2, TT, TOK]) for i in range(2)]
        shift, mass, inv = ([sb(f"{n}{i}", [P, 2, TT]) for i in range(RING)] for n in ("shift", "mass", "inv"))
        ctxT = sb("ctxT", [P, FT, TOK])
        xb = sb("xb", [P, TT, FEAT])
        res = sb("res", [P, TT, FEAT])

        ps_s = [ps(f"ps_s{i}", [P, 2, TT, TOK]) for i in range(2)]
        ps_t = ps("ps_t", [P, 2, TT, TOK])
        ps_o = ps("ps_o", [P, TOK])
        ps_p = ps("ps_p", [P, 2, TOK])

        w_loaded, ident_made, const_made = sem("w_loaded"), sem("ident_made"), sem("const_made")
        loaded, stored = [sem(f"loaded{u}") for u in range(2)], sem("stored", 16)
        counted, normalised, biased, mask_split = sem("counted", 4), sem("normalised", 1), sem("biased", 1), sem("mask_split", 2)
        powered = sem("powered", 1)
        filled, fill_kept = sem("filled", 8), sem("fill_kept", 8)
        scored, masked_mul, masked, shifted, exped, inverted, normed, turned, turned_kept = (
            sem(n, STEPS) for n in ("scored", "masked_mul", "masked", "shifted", "exped", "inverted", "normed", "turned", "turned_kept"))
        mixed, mixed_kept = sem("mixed", FT), sem("mixed_kept", FT)
        out_summed, added = sem("out_summed", 1), sem("added", 1)

        block = ctx.enter_context(nc.Block())

        def each_pass(eng, before, batch):
            before(1, -1)
            with eng.Fori(1, PASSES) as g:
                batch(g, 0, False)
                batch(g, 1, False)
            batch(PASSES, 0, False)
            batch(PASSES, 1, True)

        def all_loaded(g, u):
            return (g + (u + 1) // 2) * LOADS * 16

        def fill_at(unit):
            return ORDER.index(unit)

        @block.sync
        def _(sp):
            open_loop(sp, loop_sems)

            def load(g, u, last=False):
                if last:
                    return
                b, s = 2 * (g - 1) + u + 1, (u + 1) % 2
                index = bass.ds(b, 1) if not isinstance(b, int) else slice(b, b + 1)

                def tiles(a, at_index=index):
                    return a[at_index, :, :].rearrange("o (t p) n -> p (o t) n", p=P)

                sp.wait_ge(added, at(g, 2, u - 1))
                sp.wait_ge(biased, at(g, 2, u - 1))
                sp.dma_start(xs[s][:, :, :], tiles(x)).then_inc(loaded[s], 16)
                sp.wait_ge(masked, at(g, 2 * STEPS, u * STEPS - 1))
                sp.dma_start(mk[s][:, :, :], tiles(mask, index if mask_batches > 1 else slice(0, 1))).then_inc(loaded[s], 16)
                if CROSS:
                    sp.wait_ge(filled, at(g, 16, u * 8 - 1))
                    sp.dma_start(cs[s][:, :, :], tiles(cT)).then_inc(loaded[s], 16)

            load(1, -1)
            for t, src in ((wk, wk_d), (wq, wq_d), (wv, wv_d), (wo, wo_d)):
                sp.dma_start(t[:, :, :], src.rearrange("(t p) n -> p t n", p=P)).then_inc(w_loaded, 16)
            sp.dma_start(ln_sb[:, :, :], ln_cols).then_inc(w_loaded, 16)
            sp.dma_start(qk_sb[:, :, :], qk_cols).then_inc(w_loaded, 16)
            for i, row in enumerate(rows):
                sp.dma_start(rows_sb[:, i, :], row.to_broadcast([P, FEAT])).then_inc(w_loaded, 16)
            W_DONE = 16 * 8

            each_pass(sp, lambda g, u: None, load)

        W_DONE = 16 * 8

        @block.gpsimd
        def _(pool):
            make_identity(pool, ident, ident_made)
            pool.memset(half_power[:, :], -0.5).then_inc(const_made, 1)
            pool.wait_ge(w_loaded, W_DONE)
            pool.wait_ge(const_made, 1)

            def prepare(g, u):
                pool.wait_ge(counted, at(g, 8, (u + 1) * 4 + 3))
                pool.wait_ge(normalised, at(g, 2, u))
                pool.tensor_tensor(rstd[:, :], var_eps[:, :], half_power[:, :], ALU.pow).then_inc(powered, 1)

            def batch(g, u, last):
                if not last:
                    prepare(g, u)
                for n in range(STEPS):
                    pool.wait_ge(masked_mul, at(g, 2 * STEPS, u * STEPS + n))
                    ins = pool.tensor_tensor(pr[n % RING][:, :, :, :].rearrange("p h t k -> p h (t k)"),
                                             pr[n % RING][:, :, :, :].rearrange("p h t k -> p h (t k)"),
                                             ma[u][:, :, :].rearrange("p t k -> p (t k)").unsqueeze(1).to_broadcast([P, 2, TT * TOK]),
                                             ALU.add)
                    ins.then_inc(masked, 1)
                    if n == 3:
                        pool.wait_ge(added, at(g, 2, u - 1))
                        pool.tensor_tensor(xb[:, :, :], xs[u][:, :, :], rows_sb[:, 1, :].unsqueeze(1).to_broadcast([P, TT, FEAT]),
                                           ALU.add).then_inc(biased, 1)

            each_pass(pool, prepare, batch)

        @block.tensor
        def _(pe):
            pe.wait_ge(ident_made, 2)
            pe.wait_ge(w_loaded, W_DONE)

            def fill(g, u, unit):
                s, i = (u + 1) % 2, fill_at(unit)
                base = (u + 1) * 8
                pe.wait_ge(fill_kept, at(g, 16, base + i - 1))
                src = cs[s] if CROSS and unit[0] in "KV" else lnT
                if unit[0] == "T":
                    if unit == "T0":
                        pe.wait_ge(normalised, at(g, 2, u + 1))
                    for j in range(2):
                        f = 2 * int(unit[1]) + j
                        for m in range(TT):
                            mm = pe.transpose(ps_p[:, j, m * P:(m + 1) * P], xn[:, m, f * P:(f + 1) * P], ident[:, :])
                else:
                    if src is lnT:
                        pe.wait_ge(fill_kept, at(g, 16, base + fill_at("T1")))
                    else:
                        pe.wait_ge(loaded[(u + 1) % 2], all_loaded(g, u))
                    if unit[0] == "V":
                        m = int(unit[1])
                        for t in range(FT):
                            mm = pe.matmul(ps_p[:, :, :], src[:, t, m * P:(m + 1) * P], wv[:, t, :],
                                           start=(t == 0), stop=(t == FT - 1))
                    else:
                        w = wq if unit[0] == "Q" else wk
                        for j in range(2):
                            f = 2 * int(unit[1]) + j
                            for t in range(FT):
                                mm = pe.matmul(ps_p[:, j, :], w[:, t, f * P:(f + 1) * P], src[:, t, :],
                                               start=(t == 0), stop=(t == FT - 1))
                mm.then_inc(filled, 1)

            def before(g, u):
                for unit in ORDER:
                    fill(g, u, unit)

            def batch(g, u, last):
                e = u * STEPS
                for n in range(LAST):
                    if n < STEPS:
                        if n == 0:
                            pe.wait_ge(fill_kept, at(g, 16, u * 8 + 7))
                        pe.wait_ge(masked_mul, at(g, 2 * STEPS, e + n - 2))
                        for i in range(2):
                            h = 2 * n + i
                            r = slice(h % TILE_HEADS * DH, (h % TILE_HEADS + 1) * DH)
                            for m in range(TT):
                                mm = pe.matmul(ps_s[n % 2][:, i, m, :], qT[u][r, h // TILE_HEADS, m * P:(m + 1) * P],
                                               kT[u][r, h // TILE_HEADS, :], start=True, stop=True)
                        mm.then_inc(scored, 1)
                    if n in FILL and not last:
                        fill(g, u, FILL[n])
                    if 0 <= n - TURN_LAG < STEPS:
                        k = n - TURN_LAG
                        pe.wait_ge(normed, at(g, 2 * STEPS, e + k))
                        pe.wait_ge(turned_kept, at(g, 2 * STEPS, e + k - 1))
                        if k == 0:
                            pe.wait_ge(added, at(g, 2, u - 1))
                        for i in range(2):
                            for t in range(TT):
                                for m in range(TT):
                                    mm = pe.transpose(ps_t[:, i, t, m * P:(m + 1) * P],
                                                      pr[k % RING][:, i, m, t * P:(t + 1) * P], ident[:, :])
                        mm.then_inc(turned, 1)
                    if n >= MIX_LAG:
                        k = n - MIX_LAG
                        pe.wait_ge(turned_kept, at(g, 2 * STEPS, e + k))
                        if k % 2 == 0:
                            pe.wait_ge(mixed_kept, at(g, 2 * FT, u * FT + k // 2 - 1))
                        for i in range(2):
                            h = 2 * k + i
                            r = slice(h % TILE_HEADS * DH, (h % TILE_HEADS + 1) * DH)
                            for t in range(TT):
                                mm = pe.matmul(ps_o[r, :], v[u][:, t, h * DH:(h + 1) * DH], pT[k % 2][:, i, t, :],
                                               start=(t == 0), stop=(t == TT - 1))
                        if k % 2 == 1:
                            mm.then_inc(mixed, 1)
                pe.wait_ge(mixed_kept, at(g, 2 * FT, u * FT + FT - 1))
                for m in range(TT):
                    for t in range(FT):
                        mm = pe.matmul(ps_t[:, m, :, :], ctxT[:, t, m * P:(m + 1) * P], wo[:, t, :],
                                       start=(t == 0), stop=(t == FT - 1))
                mm.then_inc(out_summed, 1)

            each_pass(pe, before, batch)

        @block.scalar
        def _(act):
            act.wait_ge(w_loaded, W_DONE)

            def keep_fill(g, u, unit):
                if unit[0] == "V":
                    return
                s, i = (u + 1) % 2, fill_at(unit)
                act.wait_ge(filled, at(g, 16, (u + 1) * 8 + i))
                for j in range(2):
                    f = 2 * int(unit[1]) + j
                    if unit[0] == "T":
                        ins = act.activation(lnT[:, f, :], ps_p[:, j, :], ACT.Identity, bias=ln_sb[:, 1, f:f + 1],
                                             scale=ln_sb[:, 0, f:f + 1])
                    else:
                        ins = act.activation((qT if unit[0] == "Q" else kT)[s][:, f, :], ps_p[:, j, :], ACT.Identity,
                                             bias=qk_sb[:, "QK".index(unit[0]), f:f + 1])
                ins.then_inc(fill_kept, 1)

            def before(g, u):
                for unit in ORDER:
                    keep_fill(g, u, unit)

            def batch(g, u, last):
                e = u * STEPS
                for n in range(LAST):
                    if 1 <= n <= STEPS:
                        k = n - 1
                        act.wait_ge(shifted, at(g, 2 * STEPS, e + k))
                        act.wait_ge(inverted, at(g, 2 * STEPS, e + k - RING))
                        for i in range(2):
                            for m in range(TT):
                                tile = pr[k % RING][:, i, m, :]
                                ins = act.activation(tile, tile, ACT.Exp, bias=shift[k % RING][:, i, m:m + 1],
                                                     accum_out=mass[k % RING][:, i, m:m + 1])
                        ins.then_inc(exped, 1)
                    if n in FILL and not last:
                        keep_fill(g, u, FILL[n])
                    if 0 <= n - TURN_LAG < STEPS:
                        k = n - TURN_LAG
                        act.wait_ge(turned, at(g, 2 * STEPS, e + k))
                        if k >= 2 and k % 2 == 1:
                            pass
                        act.wait_ge(mixed, at(g, 2 * FT, u * FT + (k - 2) // 2))
                        act.activation(pT[k % 2][:, :, :, :], ps_t[:, :, :, :], ACT.Copy).then_inc(turned_kept, 1)
                    if n >= MIX_LAG and (n - MIX_LAG) % 2 == 1:
                        f = (n - MIX_LAG) // 2
                        act.wait_ge(mixed, at(g, 2 * FT, u * FT + f))
                        if f == 0:
                            act.wait_ge(out_summed, at(g, 2, u - 1))
                        act.activation(ctxT[:, f, :], ps_o[:, :], ACT.Copy).then_inc(mixed_kept, 1)
                b = 2 * (g - 1) + u
                act.wait_ge(added, at(g, 2, u))
                act.dma_start(out[bass.ds(b, 1) if not isinstance(b, int) else slice(b, b + 1), :, :]
                              .rearrange("o (t p) n -> p (o t) n", p=P), res[:, :, :]).then_inc(stored, 16)

            each_pass(act, before, batch)
            act.wait_ge(stored, 16 * (BATCH + 2))

        @block.vector
        def _(dve):
            dve.wait_ge(w_loaded, W_DONE)

            def statistics(g, u):
                s = (u + 1) % 2
                dve.wait_ge(loaded[(u + 1) % 2], all_loaded(g, u))
                for m in range(TT):
                    ins = dve.bn_stats(stats[:, m, :], xs[s][:, m, :])
                ins.then_inc(counted, 1)
                dve.wait_ge(masked, at(g, 2 * STEPS, u * STEPS - 1))
                dve.tensor_scalar(ma[s][:, :, :], mk[s][:, :, :], 1e4, -1e4, ALU.mult, ALU.add).then_inc(mask_split, 1)
                dve.wait_ge(counted, at(g, 8, (u + 1) * 4))
                dve.wait_ge(mask_split, at(g, 4, (u + 1) * 2))
                dve.tensor_scalar(mk[s][:, :, :], mk[s][:, :, :], SCALE, None, ALU.mult).then_inc(mask_split, 1)
                for m in range(TT):
                    ins = dve.bn_aggr(moments[:, m, :], stats[:, m, :])
                ins.then_inc(counted, 1)
                dve.wait_ge(counted, at(g, 8, (u + 1) * 4 + 1))
                dve.wait_ge(powered, at(g, 2, u))
                dve.tensor_scalar(var_eps[:, :], moments[:, :, 1], 1e-5, None, ALU.add).then_inc(counted, 2)

            def normalise(g, u):
                s = (u + 1) % 2
                dve.wait_ge(powered, at(g, 2, u + 1))
                dve.wait_ge(filled, at(g, 16, u * 8 + fill_at("T1")))
                for m in range(TT):
                    ins = dve.tensor_scalar(xn[:, m, :], xs[s][:, m, :], moments[:, m, 0:1], rstd[:, m:m + 1],
                                            ALU.subtract, ALU.mult)
                ins.then_inc(normalised, 1)

            def keep_values(g, u, unit):
                i, m = fill_at(unit), int(unit[1])
                dve.wait_ge(filled, at(g, 16, (u + 1) * 8 + i))
                dve.tensor_tensor(v[(u + 1) % 2][:, m, :], ps_p[:, :, :].rearrange("p a b -> p (a b)"), rows_sb[:, 0, :],
                                  ALU.add).then_inc(fill_kept, 1)

            def before(g, u):
                statistics(g, u)
                normalise(g, u)
                keep_values(g, u, "V0")
                keep_values(g, u, "V1")

            def batch(g, u, last):
                e = u * STEPS
                dve.wait_ge(mask_split, at(g, 4, u * 2 + 1))
                if not last:
                    statistics(g, u)
                for n in range(LAST):
                    if 0 <= n - TURN_LAG < STEPS:
                        k = n - TURN_LAG
                        dve.wait_ge(exped, at(g, 2 * STEPS, e + k))
                        dve.reciprocal(inv[k % RING][:, :, :], mass[k % RING][:, :, :]).then_inc(inverted, 1)
                        dve.wait_ge(inverted, at(g, 2 * STEPS, e + k))
                        for i in range(2):
                            for m in range(TT):
                                tile = pr[k % RING][:, i, m, :]
                                ins = dve.tensor_scalar(tile, tile, inv[k % RING][:, i, m:m + 1], None, ALU.mult)
                        ins.then_inc(normed, 1)
                    if n < STEPS:
                        dve.wait_ge(scored, at(g, 2 * STEPS, e + n))
                        dve.wait_ge(turned, at(g, 2 * STEPS, e + n - RING))
                        dve.tensor_tensor(pr[n % RING][:, :, :, :].rearrange("p h t k -> p h (t k)"),
                                          ps_s[n % 2][:, :, :, :].rearrange("p h t k -> p h (t k)"),
                                          mk[u][:, :, :].rearrange("p t k -> p (t k)").unsqueeze(1).to_broadcast([P, 2, TT * TOK]),
                                          ALU.mult).then_inc(masked_mul, 1)
                    if n == 0 and not last:
                        normalise(g, u)
                    if 1 <= n <= STEPS:
                        k = n - 1
                        dve.wait_ge(masked, at(g, 2 * STEPS, e + k))
                        dve.wait_ge(exped, at(g, 2 * STEPS, e + k - RING))
                        dve.tensor_reduce(shift[k % RING][:, :, :], pr[k % RING][:, :, :, :], AXIS.X, ALU.max,
                                          negate=True).then_inc(shifted, 1)
                    if n in FILL and not last and FILL[n][0] == "V":
                        keep_values(g, u, FILL[n])
                dve.wait_ge(out_summed, at(g, 2, u))
                dve.wait_ge(biased, at(g, 2, u))
                dve.wait_ge(stored, at(g, 2, u - 1, 16))
                dve.tensor_tensor(res[:, :, :], ps_t[:, :, :, :].rearrange("p m a b -> p m (a b)"), xb[:, :, :],
                                  ALU.add).then_inc(added, 1)

            each_pass(dve, before, batch)


def token_mlp(nc, semaphores, x, w1_d, w2_d, ln_cols, b1, b2, out):
    HID = 4 * FEAT
    CHUNKS = HID // (2 * P)
    RING = 4
    PASSES = BATCH // 2
    Y_LAG = 2
    TURN_STEPS = (4, 6)
    with ExitStack() as ctx:
        def sb(name, shape):
            return ctx.enter_context(nc.sbuf_tensor("mlp_" + name, shape, F32))

        def ps(name, shape):
            return ctx.enter_context(nc.psum_tensor("mlp_" + name, shape, F32))

        loop_sems = []

        def sem(name, per_batch=0):
            s = semaphores.allocate("mlp_" + name)
            if per_batch:
                loop_sems.append((s, 2 * per_batch))
            return s

        w1, w2 = sb("w1", [P, FT, HID]), sb("w2", [P, 2 * CHUNKS, FEAT])
        ln_sb, b1_sb, b2_row = sb("ln_cols", [P, 2, FT]), sb("b1", [P, 2 * CHUNKS]), sb("b2", [P, FEAT])
        ident, half_power = sb("ident", [P, P]), sb("half_power", [P, TT])
        xs = [sb(f"xs{u}", [P, TT, FEAT]) for u in range(2)]
        stats, moments, var_eps, rstd = sb("stats", [P, TT, 6]), sb("moments", [P, TT, 2]), sb("var_eps", [P, TT]), sb("rstd", [P, TT])
        xn = sb("xn", [P, TT, FEAT])
        lnT = [sb(f"lnT{u}", [P, FT, TOK]) for u in range(2)]
        pre, cube, hid = ([sb(f"{n}{i}", [P, 2, TOK]) for i in range(RING)] for n in ("pre", "cube", "hid"))
        xb, res = sb("xb", [P, TT, FEAT]), sb("res", [P, TT, FEAT])

        ps_h = [ps(f"ps_h{i}", [P, 2, TOK]) for i in range(2)]
        ps_y = ps("ps_y", [P, TT, FEAT])
        ps_t = [ps(f"ps_t{i}", [P, 2, TOK]) for i in range(2)]

        w1_loaded, w2_loaded, cols_loaded, ident_made, const_made = (sem(n) for n in ("w1_loaded", "w2_loaded", "cols_loaded", "ident_made", "const_made"))
        loaded, stored = [sem(f"loaded{u}") for u in range(2)], sem("stored", 16)
        counted, powered, normalised, biased = sem("counted", 4), sem("powered", 1), sem("normalised", 1), sem("biased", 1)
        turned, turned_kept = sem("turned", 2), sem("turned_kept", 2)
        h_summed, h_kept, squared, squared1, cubed, bent, gelled = (
            sem(n, CHUNKS) for n in ("h_summed", "h_kept", "squared", "squared1", "cubed", "bent", "gelled"))
        y_used, added = sem("y_used", CHUNKS), sem("added", 1)

        block = ctx.enter_context(nc.Block())

        def each_pass(eng, before, batch):
            before(1, -1)
            with eng.Fori(1, PASSES) as g:
                batch(g, 0, False)
                batch(g, 1, False)
            batch(PASSES, 0, False)
            batch(PASSES, 1, True)

        def rows_of(a, b):
            index = bass.ds(b, 1) if not isinstance(b, int) else slice(b, b + 1)
            return a[index, :, :].rearrange("o (t p) n -> p (o t) n", p=P)

        @block.sync
        def _(sp):
            open_loop(sp, loop_sems)

            def load(g, u, last=False):
                if last:
                    return
                sp.wait_ge(added, at(g, 2, u - 1))
                sp.wait_ge(biased, at(g, 2, u - 1))
                sp.dma_start(xs[(u + 1) % 2][:, :, :], rows_of(x, 2 * (g - 1) + u + 1)).then_inc(loaded[(u + 1) % 2], 16)

            load(1, -1)
            sp.dma_start(ln_sb[:, :, :], ln_cols).then_inc(cols_loaded, 16)
            sp.dma_start(b1_sb[:, :], b1).then_inc(cols_loaded, 16)
            sp.dma_start(b2_row[:, :], b2.to_broadcast([P, FEAT])).then_inc(cols_loaded, 16)
            for t in range(FT):
                sp.dma_start(w1[:, t, :], w1_d[t * P:(t + 1) * P, :]).then_inc(w1_loaded, 16)
            sp.dma_start(w2[:, :, :], w2_d.rearrange("(t p) n -> p t n", p=P)).then_inc(w2_loaded, 16)
            each_pass(sp, lambda g, u: None, load)

        @block.gpsimd
        def _(pool):
            make_identity(pool, ident, ident_made)
            pool.memset(half_power[:, :], -0.5).then_inc(const_made, 1)
            pool.wait_ge(cols_loaded, 48)
            pool.wait_ge(const_made, 1)

            def prepare(g, u):
                pool.wait_ge(counted, at(g, 8, (u + 1) * 4 + 3))
                pool.wait_ge(normalised, at(g, 2, u))
                pool.tensor_tensor(rstd[:, :], var_eps[:, :], half_power[:, :], ALU.pow).then_inc(powered, 1)

            def batch(g, u, last):
                e = u * CHUNKS
                for n in range(CHUNKS):
                    if n == 1:
                        pool.wait_ge(added, at(g, 2, u - 1))
                        pool.tensor_tensor(xb[:, :, :], xs[u][:, :, :], b2_row[:, :].unsqueeze(1).to_broadcast([P, TT, FEAT]),
                                           ALU.add).then_inc(biased, 1)
                    pool.wait_ge(squared1, at(g, 2 * CHUNKS, e + n))
                    pool.tensor_tensor(cube[n % RING][:, :, :], cube[n % RING][:, :, :], pre[n % RING][:, :, :],
                                       ALU.mult).then_inc(cubed, 1)
                    if n == 2 and not last:
                        prepare(g, u)

            each_pass(pool, prepare, batch)

        @block.tensor
        def _(pe):
            pe.wait_ge(ident_made, 2)

            def turn(g, u, i):
                pe.wait_ge(turned_kept, at(g, 4, u * 2 + i))
                pe.wait_ge(normalised, at(g, 2, u + 1))
                for j in range(2):
                    f = 2 * i + j
                    for m in range(TT):
                        mm = pe.transpose(ps_t[i][:, j, m * P:(m + 1) * P], xn[:, m, f * P:(f + 1) * P], ident[:, :])
                mm.then_inc(turned, 1)

            def before(g, u):
                turn(g, u, 0)
                turn(g, u, 1)
                pe.wait_ge(w1_loaded, 16 * FT)

            def batch(g, u, last):
                e = u * CHUNKS
                pe.wait_ge(turned_kept, at(g, 4, u * 2 + 1))
                for n in range(CHUNKS + Y_LAG):
                    if n < CHUNKS:
                        pe.wait_ge(squared, at(g, 2 * CHUNKS, e + n - 2))
                        for j in range(2):
                            f = 2 * n + j
                            for t in range(FT):
                                mm = pe.matmul(ps_h[n % 2][:, j, :], w1[:, t, f * P:(f + 1) * P], lnT[u][:, t, :],
                                               start=(t == 0), stop=(t == FT - 1))
                        mm.then_inc(h_summed, 1)
                    if n in TURN_STEPS and not last:
                        turn(g, u, TURN_STEPS.index(n))
                    if n >= Y_LAG:
                        k = n - Y_LAG
                        pe.wait_ge(gelled, at(g, 2 * CHUNKS, e + k))
                        if k == 0:
                            pe.wait_ge(added, at(g, 2, u - 1))
                            pe.wait_ge(w2_loaded, 16)
                        for j in range(2):
                            f = 2 * k + j
                            for m in range(TT):
                                mm = pe.matmul(ps_y[:, m, :], hid[k % RING][:, j, m * P:(m + 1) * P], w2[:, f, :],
                                               start=(f == 0), stop=(f == 2 * CHUNKS - 1))
                        mm.then_inc(y_used, 1)

            each_pass(pe, before, batch)

        @block.scalar
        def _(act):
            act.wait_ge(cols_loaded, 48)

            def keep_turned(g, u, i):
                act.wait_ge(turned, at(g, 4, (u + 1) * 2 + i))
                for j in range(2):
                    f = 2 * i + j
                    ins = act.activation(lnT[(u + 1) % 2][:, f, :], ps_t[i][:, j, :], ACT.Identity, bias=ln_sb[:, 1, f:f + 1],
                                         scale=ln_sb[:, 0, f:f + 1])
                ins.then_inc(turned_kept, 1)

            def before(g, u):
                keep_turned(g, u, 0)
                keep_turned(g, u, 1)

            def batch(g, u, last):
                e = u * CHUNKS
                for n in range(CHUNKS + 1):
                    if n < CHUNKS:
                        act.wait_ge(h_summed, at(g, 2 * CHUNKS, e + n))
                        act.wait_ge(gelled, at(g, 2 * CHUNKS, e + n - RING))
                        for j in range(2):
                            ins = act.activation(pre[n % RING][:, j, :], ps_h[n % 2][:, j, :], ACT.Identity,
                                                 bias=b1_sb[:, 2 * n + j:2 * n + j + 1])
                        ins.then_inc(h_kept, 1)
                        for j in range(2):
                            ins = act.activation(cube[n % RING][:, j, :], ps_h[n % 2][:, j, :], ACT.Square,
                                                 bias=b1_sb[:, 2 * n + j:2 * n + j + 1])
                        ins.then_inc(squared, 1)
                    if n >= 1:
                        k = n - 1
                        act.wait_ge(cubed, at(g, 2 * CHUNKS, e + k))
                        act.activation(cube[k % RING][:, :, :], cube[k % RING][:, :, :], ACT.Tanh,
                                       scale=0.7978845608028654).then_inc(bent, 1)
                    if n in TURN_STEPS and not last:
                        keep_turned(g, u, TURN_STEPS.index(n))
                act.wait_ge(added, at(g, 2, u))
                act.dma_start(rows_of(out, 2 * (g - 1) + u), res[:, :, :]).then_inc(stored, 16)

            each_pass(act, before, batch)
            act.wait_ge(stored, 16 * (BATCH + 2))

        @block.vector
        def _(dve):
            def statistics(g, u):
                s = (u + 1) % 2
                dve.wait_ge(loaded[s], (g + (u + 1) // 2) * 16)
                for m in range(TT):
                    ins = dve.bn_stats(stats[:, m, :], xs[s][:, m, :])
                ins.then_inc(counted, 1)

            def moment(g, u):
                dve.wait_ge(counted, at(g, 8, (u + 1) * 4))
                dve.tensor_copy(var_eps[:, :], stats[:, :, 2]).then_inc(counted, 1)
                for m in range(TT):
                    ins = dve.bn_aggr(moments[:, m, :], stats[:, m, :])
                ins.then_inc(counted, 1)
                dve.wait_ge(counted, at(g, 8, (u + 1) * 4 + 2))
                dve.tensor_scalar(var_eps[:, :], moments[:, :, 1], 1e-5, None, ALU.add).then_inc(counted, 1)

            def normalise(g, u):
                s = (u + 1) % 2
                dve.wait_ge(powered, at(g, 2, u + 1))
                dve.wait_ge(turned, at(g, 4, u * 2 + 1))
                for m in range(TT):
                    ins = dve.tensor_scalar(xn[:, m, :], xs[s][:, m, :], moments[:, m, 0:1], rstd[:, m:m + 1],
                                            ALU.subtract, ALU.mult)
                ins.then_inc(normalised, 1)

            def before(g, u):
                statistics(g, u)
                moment(g, u)
                normalise(g, u)

            def batch(g, u, last):
                e = u * CHUNKS
                for n in range(CHUNKS + 1):
                    if n < CHUNKS:
                        dve.wait_ge(squared, at(g, 2 * CHUNKS, e + n))
                        dve.tensor_scalar(cube[n % RING][:, :, :], cube[n % RING][:, :, :], 0.044715, 1.0, ALU.mult,
                                          ALU.add).then_inc(squared1, 1)
                    if n >= 1:
                        k = n - 1
                        dve.wait_ge(bent, at(g, 2 * CHUNKS, e + k))
                        dve.wait_ge(y_used, at(g, 2 * CHUNKS, e + k - RING))
                        dve.scalar_tensor_tensor(out=hid[k % RING][:, :, :], in0=cube[k % RING][:, :, :], scalar=1.0,
                                                 in1=pre[k % RING][:, :, :], op0=ALU.add, op1=ALU.mult).then_inc(gelled, 1)
                    if n == 1 and not last:
                        statistics(g, u)
                    if n == 2 and not last:
                        moment(g, u)
                    if n == 3 and not last:
                        normalise(g, u)
                dve.wait_ge(y_used, at(g, 2 * CHUNKS, e + CHUNKS - 1))
                dve.wait_ge(biased, at(g, 2, u))
                dve.wait_ge(stored, at(g, 2, u - 1, 16))
                dve.scalar_tensor_tensor(out=res[:, :, :], in0=ps_y[:, :, :], scalar=0.5, in1=xb[:, :, :],
                                         op0=ALU.mult, op1=ALU.add).then_inc(added, 1)

            each_pass(dve, before, batch)


def recurrent_block(nc, semaphores, x, state, w, cols, maa_w1, maa_w2, td_w1, td_w2, select, spread, head_sum, group_mean, out):
    GROUP = 16
    MIX = 32
    DECAY = td_w1.shape[1]
    WEIGHTS = ("r", "k", "v", "g", "o", "fk", "fr", "fv")
    A_UNITS = ("T0", "T1", "XX", "Mw0", "Mw1", "Mk0", "Mk1", "D1", "K0", "D20", "D21", "K1", "Mv0", "Mv1", "V0", "V1",
               "Mr0", "Mr1", "R0", "R1", "Mg0", "Mg1", "G0", "G1")
    Z_UNITS = ("C0", "C1", "E0", "E1", "Q0", "Q1", "O0", "O1", "T0", "T1", "FK0", "FK1", "FR0", "FR1", "FV0", "FV1")
    MIXED = "wkvrg"
    NA, NZ = len(A_UNITS), len(Z_UNITS)
    SCHEDULE = (
        "A:LS A:LN A:T0 A:T1", "Z:E0 Z:E1 A:SX", "A:XX Z:Q0 Z:Q1 A:Mw0 A:Mw1", "A:Mk0 A:Mk1 A:D1 Z:N1",
        "A:K0 A:D20 A:D21 Z:N2", "A:K1 A:Mv0 A:Mv1 Z:N3", "Z:O0 A:V0 Z:O1", "Z:LS A:V1 Z:LN",
        "A:Mr0 Z:T0 A:Mr1 Z:T1", "A:R0 Z:X", "A:R1 Z:FK0", "Z:FK1 A:Mg0 A:Mg1", "Z:FR0 A:G0", "Z:FR1", "C:P A:G1 Z:FV0",
        "Z:FV1 C:C0 C:C1")
    STEPS = GROUP
    with ExitStack() as ctx:
        def sb(name, shape):
            return ctx.enter_context(nc.sbuf_tensor("rec_" + name, shape, F32))

        def ps(name, shape):
            return ctx.enter_context(nc.psum_tensor("rec_" + name, shape, F32))

        loop_sems = []

        def sem(name, per_batch=0):
            s = semaphores.allocate("rec_" + name)
            if per_batch:
                loop_sems.append((s, 2 * per_batch))
            return s

        def of(b, per_batch, k, unit=1):
            return at(b + 2, per_batch, k, unit)

        wt = {n: sb("w_" + n, [P, FT, FEAT]) for n in WEIGHTS}
        m1 = sb("m1", [P, FT, 5 * MIX])
        m2a, m2b = sb("m2a", [P, FEAT]), sb("m2b", [MIX, FEAT])
        t1, t2 = sb("t1", [P, FT, DECAY]), sb("t2", [DECAY, FEAT])
        sel, spr, ones = sb("sel", [P, GROUP, P]), sb("spr", [P, (2 * GROUP - 1) * (P // GROUP)]), sb("ones", [P, P])
        mean_of = sb("mean_of", [P, P])
        NC = 16
        col = sb("cols", [P, NC, FT])
        LN1_W, LN1_B, LN2_W, LN2_B, MAA_X, DECAY0, U, GN_W, GN_B, FFN_K, FFN_R, STACK = range(12)
        ident, half_power = sb("ident", [P, P]), sb("half_power", [P, TT])

        xin, xn = sb("xin", [P, TT, FEAT]), sb("xn", [P, TT, FEAT])
        stats, moments, var_eps, rstd = ([sb(f"{n}{i}", sh) for i in "az"] for n, sh in
                                         (("stats", [P, TT, 6]), ("moments", [P, TT, 2]), ("var_eps", [P, TT]), ("rstd", [P, TT])))
        st = [sb(f"st{u}", [P, FT, 2 + GROUP]) for u in range(2)]
        edge = sb("edge", [P, FT, 2])
        xaT, sx = sb("xaT", [P, FT, TOK + 1]), sb("sx", [P, FT, TOK])
        xm = [sb(f"xm{i}", [P, FT, TOK]) for i in range(2)]
        xxT, xx4, tdT = sb("xxT", [P, TOK]), sb("xx4", [MIX, TOK]), sb("tdT", [DECAY, TOK])
        rT, kT, vT, g2 = ([sb(f"{n}{u}", [P, FT, TOK]) for u in range(2)] for n in ("rT", "kT", "vT", "g2"))
        wE = [sb(f"wE{u}", [P, FT, TOK + 1]) for u in range(2)]
        kvE = [sb(f"kvE{i}", [P, FT, TOK + 1]) for i in range(2)]
        sE = [sb(f"sE{i}", [P, FT, TOK + 1]) for i in range(2)]
        rs = [sb(f"rs{i}", [P, FT, TOK]) for i in range(2)]
        og, sq = sb("og", [P, FT, TOK]), sb("sq", [P, FT, TOK])
        xres = sb("xres", [P, TT, FEAT])
        xcT, sx2, xk2, xr2 = sb("xcT", [P, FT, TOK + 1]), sb("sx2", [P, FT, TOK]), sb("xk2", [P, FT, TOK]), sb("xr2", [P, FT, TOK])
        kk, ruk = og, xr2
        sq_rows = sq[:, :, :].rearrange("p (m a) n -> p m (a n)", m=TT)

        ps_v = [ps(f"ps_v{i}", [P, FT, TOK]) for i in range(2)]
        ps_acc = ps("ps_acc", [P, FT, TOK])
        ps_a, ps_z = ps("ps_a", [P, 2, TOK]), ps("ps_z", [P, 2, TOK])

        w_loaded, ident_made, const_made = sem("w_loaded"), sem("ident_made"), sem("const_made")
        x_loaded, st_loaded, z_loaded, stored = sem("x_loaded"), sem("st_loaded"), sem("z_loaded"), sem("stored", 16)
        a_filled, a_kept, z_filled, z_kept = sem("a_filled", NA), sem("a_kept", NA), sem("z_filled", NZ), sem("z_kept", NZ)
        counted = [sem(f"counted_{i}", 4) for i in "az"]
        powered = [sem(f"powered_{i}", 1) for i in "az"]
        normalised = [sem(f"normalised_{i}", 1) for i in "az"]
        shifted, mixed_x, mixtures, decayed, g_bent = sem("shifted", 1), sem("mixed_x", 1), sem("mixtures", 5), sem("decayed", 1), sem("g_bent", 2)
        spread_v, kv_made, seeded, scanned, rs_made, summed = (
            sem(n, STEPS) for n in ("spread_v", "kv_made", "seeded", "scanned", "rs_made", "summed"))
        ruk_made, og_made = sem("ruk_made", 2), sem("og_made", 1)
        squared, inverted, rooted, og_scaled, og_affine, gated = (
            sem("squared", 2), sem("inverted", 2), sem("rooted", 1), sem("og_scaled", 1), sem("og_affine", 1), sem("gated", 1))
        shifted2, mixed2, kk_made, res_made = sem("shifted2", 1), sem("mixed2", 2), sem("kk_made", 1), sem("res_made", 2)
        W_LOADS = len(WEIGHTS) + 10

        block = ctx.enter_context(nc.Block())

        def run(eng, step, a_unit, z_unit, c_unit, body_end=None):
            names = " ".join(SCHEDULE).split()

            def body(b, s, with_z, with_a):
                for j in range(STEPS):
                    step(b, s, j)
                    for name in SCHEDULE[j].split():
                        stage, unit = name.split(":")
                        if stage == "A" and with_a:
                            a_unit(b + 1, 1 - s, unit)
                        elif stage == "Z" and with_z:
                            z_unit(b - 1, 1 - s, unit)
                        elif stage == "C":
                            c_unit(b, s, unit)
                step(b, s, STEPS)
                if body_end:
                    body_end(b, s)

            for name in names:
                if name.startswith("A:"):
                    a_unit(0, 0, name[2:])
            body(0, 0, False, True)
            with eng.Fori(1, BATCH // 2) as p:
                body(2 * p - 1, 1, True, True)
                body(2 * p, 0, True, True)
            body(BATCH - 1, 1, True, False)
            for name in names:
                if name.startswith("Z:"):
                    z_unit(BATCH - 1, 1, name[2:])

        def batch_of(a, b):
            return a[bass.ds(b, 1) if not isinstance(b, int) else slice(b, b + 1)]

        def token_rows(a, b):
            return batch_of(a, b).rearrange("o (t p) n -> p (o t) n", p=P)

        def feature_rows(a, b):
            return batch_of(a, b).rearrange("o p t n -> p (o t) n")

        def a_at(unit):
            return A_UNITS.index(unit)

        def z_at(unit):
            return Z_UNITS.index(unit)

        NOTHING = lambda *_: None

        @block.sync
        def _(sp):
            open_loop(sp, loop_sems)

            def load_x(b):
                sp.wait_ge(normalised[0], of(b - 1, 1, 0))
                sp.dma_start(xin[:, :, :], token_rows(x, b)).then_inc(x_loaded, 16)

            def load_st(b, s):
                sp.wait_ge(og_made, of(b - 2, 1, 0))
                sp.dma_start(st[s][:, :, :], feature_rows(state, b)).then_inc(st_loaded, 16)

            def load_z(b):
                sp.wait_ge(stored, of(b - 1, 1, 0, 16))
                sp.wait_ge(z_kept, of(b - 1, NZ, z_at("T0")))
                sp.dma_start(xres[:, :, :], token_rows(x, b)).then_inc(z_loaded, 16)
                sp.dma_start(edge[:, :, :], feature_rows(state, b)[:, :, 0:2]).then_inc(z_loaded, 16)

            def store(b):
                sp.wait_ge(res_made, of(b, 2, 1))
                sp.dma_start(token_rows(out, b), xres[:, :, :]).then_inc(stored, 16)

            load_x(0)
            load_st(0, 0)
            sp.dma_start(col[:, :, :], cols).then_inc(w_loaded, 16)
            sp.dma_start(m1[:, :, :], maa_w1.rearrange("(t p) n -> p t n", p=P)).then_inc(w_loaded, 16)
            sp.dma_start(m2a[:, :], maa_w2[0:P, :]).then_inc(w_loaded, 16)
            sp.dma_start(m2b[:, :], maa_w2[P:P + MIX, :]).then_inc(w_loaded, 16)
            sp.dma_start(t1[:, :, :], td_w1.rearrange("(t p) n -> p t n", p=P)).then_inc(w_loaded, 16)
            sp.dma_start(t2[:, :], td_w2).then_inc(w_loaded, 16)
            sp.dma_start(sel[:, :, :], select).then_inc(w_loaded, 16)
            sp.dma_start(spr[:, :], spread).then_inc(w_loaded, 16)
            sp.dma_start(ones[:, :], head_sum).then_inc(w_loaded, 16)
            sp.dma_start(mean_of[:, :], group_mean).then_inc(w_loaded, 16)
            for n in WEIGHTS:
                sp.dma_start(wt[n][:, :, :], w[n].rearrange("(t p) n -> p t n", p=P)).then_inc(w_loaded, 16)
            load_x(1)
            load_st(1, 1)
            load_x(2)
            load_st(2, 0)

            def body(b, s, ahead=True):
                load_z(b - 1)
                if ahead:
                    load_x(b + 2)
                store(b - 1)
                if ahead:
                    load_st(b + 2, s)

            for b in range(1, BATCH):
                body(b, b % 2, b + 2 < BATCH)
            load_z(BATCH - 1)
            store(BATCH - 1)
            sp.wait_ge(stored, 16 * (BATCH + 2))

        @block.gpsimd
        def _(pool):
            make_identity(pool, ident, ident_made)
            pool.memset(half_power[:, :], -0.5).then_inc(const_made, 1)
            pool.memset(wE[0][:, :, 0], 0.0).then_inc(const_made, 1)
            pool.memset(wE[1][:, :, 0], 0.0).then_inc(const_made, 1)
            pool.wait_ge(w_loaded, 16 * W_LOADS)
            pool.wait_ge(const_made, 3)

            def power(i, b):
                pool.wait_ge(counted[i], of(b, 4, 3))
                pool.wait_ge(normalised[i], of(b - 1, 1, 0))
                pool.tensor_tensor(rstd[i][:, :], var_eps[i][:, :], half_power[:, :], ALU.pow).then_inc(powered[i], 1)

            def a_unit(b, s, unit):
                if unit == "LS":
                    power(0, b)
                elif unit[0] == "M" and unit[2] == "1":
                    o = MIXED.index(unit[1])
                    pool.wait_ge(a_kept, of(b, NA, a_at(unit)))
                    pool.tensor_tensor(xm[(o + 1) % 2][:, :, :], xm[(o + 1) % 2][:, :, :], xaT[:, :, 1:TOK + 1],
                                       ALU.add).then_inc(mixtures, 1)

            def z_unit(b, s, unit):
                if unit == "N1":
                    pool.wait_ge(rooted, of(b, 1, 0))
                    pool.tensor_tensor(og[:, :, :], og[:, :, :], sq[:, :, :], ALU.mult).then_inc(og_scaled, 1)
                elif unit == "LS":
                    power(1, b)
                elif unit == "X":
                    pool.wait_ge(z_kept, of(b, NZ, z_at("T1")))
                    pool.wait_ge(mixed2, of(b - 1, 2, 1))
                    pool.tensor_tensor(sx2[:, :, :], xcT[:, :, 0:TOK], xcT[:, :, 1:TOK + 1], ALU.subtract).then_inc(shifted2, 1)
                elif unit == "FK1":
                    pool.wait_ge(z_kept, of(b, NZ, z_at("FK1")))
                    pool.tensor_tensor(kk[:, :, :], kk[:, :, :], kk[:, :, :], ALU.mult).then_inc(kk_made, 1)

            def c_unit(b, s, unit):
                if unit == "P":
                    pool.wait_ge(a_kept, of(b, NA, a_at("R1")))
                    pool.wait_ge(z_filled, of(b - 1, NZ, z_at("FR1")))
                    pool.tensor_tensor(ruk[:, :, :], rT[s][:, :, :], kT[s][:, :, :], ALU.mult).then_inc(ruk_made, 1)
                    pool.wait_ge(ruk_made, of(b, 2, 0))
                    pool.tensor_tensor(ruk[:, :, :], ruk[:, :, :], col[:, U, :].unsqueeze(2).to_broadcast([P, FT, TOK]),
                                       ALU.mult).then_inc(ruk_made, 1)

            def step(b, s, j):
                if j == STEPS:
                    return
                if j == 0:
                    pool.wait_ge(a_kept, of(b, NA, a_at("R1")))
                pool.wait_ge(scanned, of(b, STEPS, j))
                pool.wait_ge(summed, of(b, STEPS, j - 2))
                pool.tensor_tensor(rs[j % 2][:, :, :], sE[j % 2][:, :, 0:TOK], rT[s][:, :, :], ALU.mult).then_inc(rs_made, 1)

            run(pool, step, a_unit, z_unit, c_unit)

        @block.tensor
        def _(pe):
            pe.wait_ge(ident_made, 2)
            pe.wait_ge(w_loaded, 16 * W_LOADS)

            def transpose_rows(bank, rows, half):
                for j in range(2):
                    f = 2 * half + j
                    for m in range(TT):
                        mm = pe.transpose(bank[:, j, m * P:(m + 1) * P], rows[:, m, f * P:(f + 1) * P], ident[:, :])
                return mm

            def to_features(bank, weight, src, half):
                for j in range(2):
                    f = 2 * half + j
                    for t in range(FT):
                        mm = pe.matmul(bank[:, j, :], weight[:, t, f * P:(f + 1) * P], src[:, t, :],
                                       start=(t == 0), stop=(t == FT - 1))
                return mm

            def to_tokens(bank, weight, src, m):
                for t in range(FT):
                    mm = pe.matmul(bank[:, :, :], src[:, t, m * P:(m + 1) * P], weight[:, t, :],
                                   start=(t == 0), stop=(t == FT - 1))
                return mm

            def a_unit(b, s, unit):
                if unit in ("LS", "LN", "SX"):
                    return
                pe.wait_ge(a_kept, of(b, NA, a_at(unit) - 1))
                half = int(unit[-1]) if unit[-1] in "01" else 0
                if unit[0] == "T":
                    pe.wait_ge(normalised[0], of(b, 1, 0))
                    mm = transpose_rows(ps_a, xn, half)
                elif unit == "XX":
                    pe.wait_ge(mixed_x, of(b, 1, 0))
                    for j, rows in enumerate((P, MIX)):
                        for t in range(FT):
                            mm = pe.matmul(ps_a[0:rows, j, :], m1[:, t, j * P:j * P + rows], xm[0][:, t, :],
                                           start=(t == 0), stop=(t == FT - 1))
                elif unit[0] == "M":
                    f = "kwvrg".index(unit[1])
                    if unit == "Mw0":
                        pe.wait_ge(a_kept, of(b, NA, a_at("XX")))
                    r = slice(f * MIX, (f + 1) * MIX) if f < 4 else slice(0, MIX)
                    w2, xx = (m2a, xxT) if f < 4 else (m2b, xx4)
                    for j in range(2):
                        c = 2 * half + j
                        mm = pe.matmul(ps_a[:, j, :], w2[r, c * P:(c + 1) * P], xx[r, :], start=True, stop=True)
                elif unit == "D1":
                    pe.wait_ge(mixtures, of(b, 5, 0))
                    for t in range(FT):
                        mm = pe.matmul(ps_a[0:DECAY, 0, :], t1[:, t, :], xm[1][:, t, :], start=(t == 0), stop=(t == FT - 1))
                elif unit[:2] == "D2":
                    pe.wait_ge(a_kept, of(b, NA, a_at("D1")))
                    for j in range(2):
                        c = 2 * half + j
                        mm = pe.matmul(ps_a[:, j, :], t2[:, c * P:(c + 1) * P], tdT[:, :], start=True, stop=True)
                else:
                    o = MIXED.index(unit[0].lower())
                    pe.wait_ge(mixtures, of(b, 5, o))
                    mm = to_features(ps_a, wt[unit[0].lower()], xm[(o + 1) % 2], half)
                mm.then_inc(a_filled, 1)

            def z_unit(b, s, unit):
                if unit not in Z_UNITS:
                    return
                pe.wait_ge(z_kept, of(b, NZ, z_at(unit) - 1))
                half = int(unit[-1])
                if unit[0] == "E":
                    pe.wait_ge(og_made, of(b, 1, 0))
                    mm = pe.matmul(ps_z[:, :, :], mean_of[:, :], og[:, 2 * half:2 * half + 2, :], start=True, stop=True)
                elif unit[0] == "Q":
                    pe.wait_ge(squared, of(b, 2, half))
                    mm = pe.matmul(ps_z[:, :, :], mean_of[:, :], sq[:, 2 * half:2 * half + 2, :], start=True, stop=True)
                elif unit[0] == "O":
                    pe.wait_ge(gated, of(b, 1, 0))
                    mm = to_tokens(ps_z, wt["o"], og, half)
                elif unit[0] == "T":
                    pe.wait_ge(normalised[1], of(b, 1, 0))
                    mm = transpose_rows(ps_z, sq_rows, half)
                elif unit[:2] == "FK":
                    pe.wait_ge(mixed2, of(b, 2, 0))
                    mm = to_features(ps_z, wt["fk"], xk2, half)
                elif unit[:2] == "FR":
                    pe.wait_ge(mixed2, of(b, 2, 1))
                    mm = to_tokens(ps_z, wt["fr"], xr2, half)
                elif unit[:2] == "FV":
                    pe.wait_ge(kk_made, of(b, 1, 0))
                    mm = to_tokens(ps_z, wt["fv"], kk, half)
                mm.then_inc(z_filled, 1)

            def c_unit(b, s, unit):
                if unit == "P":
                    return
                half = int(unit[1])
                pe.wait_ge(z_kept, of(b - 1, NZ, NZ - 1) if half == 0 else of(b, NZ, 0))
                pe.wait_ge(ruk_made, of(b, 2, 1))
                pe.matmul(ps_z[:, :, :], ones[:, :], ruk[:, 2 * half:2 * half + 2, :], start=True, stop=True).then_inc(z_filled, 1)

            def step(b, s, j):
                if j >= 1:
                    pe.wait_ge(rs_made, of(b, STEPS, j - 1))
                    if j == 1:
                        pe.wait_ge(og_made, of(b - 1, 1, 0))
                    i = (GROUP - j) * (P // GROUP)
                    for half in range(2):
                        mm = pe.matmul(ps_acc[:, 2 * half:2 * half + 2, :], spr[:, i:i + P],
                                       rs[(j - 1) % 2][:, 2 * half:2 * half + 2, :], start=(j == 1), stop=(j == STEPS))
                    mm.then_inc(summed, 1)
                if j < STEPS:
                    if j == 0:
                        pe.wait_ge(a_kept, of(b, NA, a_at("V1")))
                    pe.wait_ge(kv_made, of(b, STEPS, j - 2))
                    for half in range(2):
                        mm = pe.matmul(ps_v[j % 2][:, 2 * half:2 * half + 2, :], sel[:, j, :], vT[s][:, 2 * half:2 * half + 2, :],
                                       start=True, stop=True)
                    mm.then_inc(spread_v, 1)

            run(pe, step, a_unit, z_unit, c_unit)

        @block.scalar
        def _(act):
            act.wait_ge(w_loaded, 16 * W_LOADS)

            def a_unit(b, s, unit):
                if unit in ("LS", "LN", "SX") or unit[0] == "M":
                    return
                half = int(unit[-1]) if unit[-1] in "01" else 0
                if unit == "T0":
                    act.wait_ge(og_made, of(b - 2, 1, 0))
                    act.wait_ge(mixtures, of(b - 1, 5, 4))
                elif unit == "T1":
                    act.wait_ge(st_loaded, (b + 1) * 16)
                    act.activation(xaT[:, :, 0], st[s][:, :, 1], ACT.Copy)
                act.wait_ge(a_filled, of(b, NA, a_at(unit)))
                if unit[0] == "T":
                    for j in range(2):
                        c = 2 * half + j
                        ins = act.activation(xaT[:, c, 1:TOK + 1], ps_a[:, j, :], ACT.Identity, bias=col[:, LN1_B, c:c + 1],
                                             scale=col[:, LN1_W, c:c + 1])
                elif unit == "XX":
                    act.activation(xxT[:, :], ps_a[:, 0, :], ACT.Tanh)
                    ins = act.activation(xx4[:, :], ps_a[0:MIX, 1, :], ACT.Tanh)
                elif unit == "D1":
                    ins = act.activation(tdT[:, :], ps_a[0:DECAY, 0, :], ACT.Tanh)
                elif unit[:2] == "D2":
                    for j in range(2):
                        c = 2 * half + j
                        ins = act.activation(wE[s][:, c, 1:TOK + 1], ps_a[:, j, :], ACT.Exp, bias=col[:, DECAY0, c:c + 1])
                elif unit[0] == "G":
                    if half == 0:
                        act.wait_ge(gated, of(b - 2, 1, 0))
                    act.activation(g2[s][:, 2 * half:2 * half + 2, :], ps_a[:, :, :], ACT.Tanh, scale=0.5).then_inc(g_bent, 1)
                    return
                else:
                    dst = {"R": rT, "K": kT, "V": vT}[unit[0]][s]
                    ins = act.activation(dst[:, 2 * half:2 * half + 2, :], ps_a[:, :, :], ACT.Copy)
                ins.then_inc(a_kept, 1)
                if unit == "D21":
                    act.wait_ge(a_kept, of(b, NA, a_at("D21")))
                    act.activation(wE[s][:, :, 1:TOK + 1], wE[s][:, :, 1:TOK + 1], ACT.Exp, scale=-1.0).then_inc(decayed, 1)

            def z_unit(b, s, unit):
                if unit[0] == "E":
                    half = int(unit[1])
                    act.wait_ge(z_kept, of(b, NZ, z_at(unit)))
                    act.wait_ge(res_made, of(b - 1, 2, 1))
                    act.activation(sq[:, 2 * half:2 * half + 2, :], og[:, 2 * half:2 * half + 2, :], ACT.Square).then_inc(squared, 1)
                elif unit == "N1":
                    act.wait_ge(inverted, of(b, 2, 1))
                    act.activation(sq[:, :, :], sq[:, :, :], ACT.Sqrt).then_inc(rooted, 1)
                elif unit == "N2":
                    act.wait_ge(og_scaled, of(b, 1, 0))
                    for c in range(FT):
                        ins = act.activation(og[:, c, :], og[:, c, :], ACT.Identity, bias=col[:, GN_B, c:c + 1],
                                             scale=col[:, GN_W, c:c + 1])
                    ins.then_inc(og_affine, 1)
                elif unit[0] == "T":
                    half = int(unit[1])
                    if half == 0:
                        act.wait_ge(mixed2, of(b - 1, 2, 1))
                        act.wait_ge(z_loaded, (b + 1) * 32)
                        act.activation(xcT[:, :, 0], edge[:, :, 0], ACT.Copy)
                    act.wait_ge(z_filled, of(b, NZ, z_at(unit)))
                    for j in range(2):
                        c = 2 * half + j
                        ins = act.activation(xcT[:, c, 1:TOK + 1], ps_z[:, j, :], ACT.Identity, bias=col[:, LN2_B, c:c + 1],
                                             scale=col[:, LN2_W, c:c + 1])
                    ins.then_inc(z_kept, 1)
                elif unit[:2] == "FK":
                    half = int(unit[2])
                    act.wait_ge(z_filled, of(b, NZ, z_at(unit)))
                    act.activation(kk[:, 2 * half:2 * half + 2, :], ps_z[:, :, :], ACT.Relu).then_inc(z_kept, 1)
                elif unit[:2] == "FR":
                    m = int(unit[2])
                    act.wait_ge(z_filled, of(b, NZ, z_at(unit)))
                    act.activation(sq_rows[:, m, :], ps_z[:, :, :].rearrange("p a n -> p (a n)"), ACT.Tanh, scale=0.5).then_inc(z_kept, 1)

            def step(b, s, j):
                if j < STEPS:
                    act.wait_ge(scanned, of(b, STEPS, j - 2))
                    act.activation(kvE[j % 2][:, :, 0], st[s][:, :, 2 + j], ACT.Copy).then_inc(seeded, 1)

            run(act, step, a_unit, z_unit, NOTHING)

        @block.vector
        def _(dve):
            dve.wait_ge(w_loaded, 16 * W_LOADS)
            dve.wait_ge(const_made, 3)

            def statistics(i, b, rows):
                for m in range(TT):
                    ins = dve.bn_stats(stats[i][:, m, :], rows[:, m, :])
                ins.then_inc(counted[i], 1)
                dve.wait_ge(counted[i], of(b, 4, 0))
                dve.tensor_copy(var_eps[i][:, :], stats[i][:, :, 2]).then_inc(counted[i], 1)
                for m in range(TT):
                    ins = dve.bn_aggr(moments[i][:, m, :], stats[i][:, m, :])
                ins.then_inc(counted[i], 1)
                dve.wait_ge(counted[i], of(b, 4, 2))
                dve.tensor_scalar(var_eps[i][:, :], moments[i][:, :, 1], 1e-5, None, ALU.add).then_inc(counted[i], 1)

            def normalise(i, b, dst, rows):
                dve.wait_ge(powered[i], of(b, 1, 0))
                for m in range(TT):
                    ins = dve.tensor_scalar(dst[:, m, :], rows[:, m, :], moments[i][:, m, 0:1], rstd[i][:, m:m + 1],
                                            ALU.subtract, ALU.mult)
                ins.then_inc(normalised[i], 1)

            def a_unit(b, s, unit):
                if unit == "LS":
                    dve.wait_ge(x_loaded, (b + 1) * 16)
                    statistics(0, b, xin)
                elif unit == "LN":
                    dve.wait_ge(a_filled, of(b - 1, NA, a_at("T1")))
                    normalise(0, b, xn, xin)
                elif unit == "SX":
                    dve.wait_ge(a_kept, of(b, NA, a_at("T1")))
                    dve.tensor_tensor(sx[:, :, :], xaT[:, :, 0:TOK], xaT[:, :, 1:TOK + 1], ALU.subtract).then_inc(shifted, 1)
                    dve.wait_ge(shifted, of(b, 1, 0))
                    dve.wait_ge(a_filled, of(b - 1, NA, a_at("R1")))
                    for c in range(FT):
                        ins = dve.scalar_tensor_tensor(out=xm[0][:, c, :], in0=sx[:, c, :], scalar=col[:, MAA_X, c:c + 1],
                                                       in1=xaT[:, c, 1:TOK + 1], op0=ALU.mult, op1=ALU.add)
                    ins.then_inc(mixed_x, 1)
                elif unit[0] == "M":
                    half, o, f = int(unit[2]), MIXED.index(unit[1]), "kwvrg".index(unit[1])
                    dve.wait_ge(a_filled, of(b, NA, a_at(unit)))
                    if half == 0:
                        reader = (a_at("G1") - NA, a_at("XX"), a_at("D1"), a_at("K1"), a_at("V1"))[o]
                        dve.wait_ge(a_filled, of(b, NA, reader))
                    for j in range(2):
                        c = 2 * half + j
                        ins = dve.scalar_tensor_tensor(out=xm[(o + 1) % 2][:, c, :], in0=ps_a[:, j, :],
                                                       scalar=col[:, STACK + f, c:c + 1], in1=sx[:, c, :],
                                                       op0=ALU.add, op1=ALU.mult)
                    ins.then_inc(a_kept, 1)
                elif unit[0] == "G":
                    half = int(unit[1])
                    dve.wait_ge(g_bent, of(b, 2, half))
                    tile = g2[s][:, 2 * half:2 * half + 2, :]
                    dve.scalar_tensor_tensor(out=tile, in0=tile, scalar=1.0, in1=ps_a[:, :, :], op0=ALU.add,
                                             op1=ALU.mult).then_inc(a_kept, 1)

            def z_unit(b, s, unit):
                half = int(unit[-1]) if unit[-1] in "01" else 0
                here = slice(2 * half, 2 * half + 2)
                if unit in Z_UNITS and unit[0] != "T" and unit[:2] not in ("FK", "FR"):
                    dve.wait_ge(z_filled, of(b, NZ, z_at(unit)))
                if unit[0] == "E":
                    dve.tensor_tensor(og[:, here, :], og[:, here, :], ps_z[:, :, :], ALU.subtract).then_inc(z_kept, 1)
                elif unit[0] == "Q":
                    dve.tensor_scalar(sq[:, here, :], ps_z[:, :, :], 1e-5, None, ALU.add).then_inc(z_kept, 1)
                    dve.wait_ge(z_kept, of(b, NZ, z_at(unit)))
                    dve.reciprocal(sq[:, here, :], sq[:, here, :]).then_inc(inverted, 1)
                elif unit == "N3":
                    dve.wait_ge(og_affine, of(b, 1, 0))
                    dve.wait_ge(a_kept, of(b, NA, a_at("G1")))
                    dve.scalar_tensor_tensor(out=og[:, :, :], in0=og[:, :, :], scalar=0.5, in1=g2[s][:, :, :], op0=ALU.mult,
                                             op1=ALU.mult).then_inc(gated, 1)
                elif unit[0] == "O":
                    if half == 0:
                        dve.wait_ge(z_loaded, (b + 1) * 32)
                    dve.tensor_tensor(xres[:, half, :], ps_z[:, :, :].rearrange("p a n -> p (a n)"), xres[:, half, :],
                                      ALU.add).then_inc(z_kept, 1)
                elif unit == "LS":
                    dve.wait_ge(z_kept, of(b, NZ, z_at("O1")))
                    statistics(1, b, xres)
                elif unit == "LN":
                    normalise(1, b, sq_rows, xres)
                elif unit == "X":
                    dve.wait_ge(shifted2, of(b, 1, 0))
                    for dst, which in ((xk2, FFN_K), (xr2, FFN_R)):
                        for c in range(FT):
                            ins = dve.scalar_tensor_tensor(out=dst[:, c, :], in0=sx2[:, c, :], scalar=col[:, which, c:c + 1],
                                                           in1=xcT[:, c, 1:TOK + 1], op0=ALU.mult, op1=ALU.add)
                        ins.then_inc(mixed2, 1)
                elif unit[:2] == "FV":
                    row = sq_rows[:, half, :]
                    dve.scalar_tensor_tensor(out=row, in0=row, scalar=1.0, in1=ps_z[:, :, :].rearrange("p a n -> p (a n)"),
                                             op0=ALU.add, op1=ALU.mult).then_inc(z_kept, 1)
                    dve.wait_ge(z_kept, of(b, NZ, z_at(unit)))
                    dve.scalar_tensor_tensor(out=xres[:, half, :], in0=row, scalar=0.5, in1=xres[:, half, :], op0=ALU.mult,
                                             op1=ALU.add).then_inc(res_made, 1)

            def c_unit(b, s, unit):
                if unit == "P":
                    return
                half = int(unit[1])
                here = slice(2 * half, 2 * half + 2)
                dve.wait_ge(z_filled, of(b, NZ, half))
                dve.tensor_tensor(og[:, here, :], ps_z[:, :, :], vT[s][:, here, :], ALU.mult).then_inc(z_kept, 1)

            def step(b, s, j):
                if j < STEPS:
                    dve.wait_ge(spread_v, of(b, STEPS, j))
                    if j == 0:
                        dve.wait_ge(a_kept, of(b, NA, a_at("K1")))
                        dve.wait_ge(decayed, of(b, 1, 0))
                    dve.tensor_tensor(kvE[j % 2][:, :, 1:TOK + 1], ps_v[j % 2][:, :, :], kT[s][:, :, :], ALU.mult).then_inc(kv_made, 1)
                    dve.wait_ge(seeded, of(b, STEPS, j))
                    dve.wait_ge(kv_made, of(b, STEPS, j))
                    dve.wait_ge(rs_made, of(b, STEPS, j - 2))
                    dve.tensor_tensor_scan(sE[j % 2][:, :, :].rearrange("p c t -> p (c t)"),
                                           wE[s][:, :, :].rearrange("p c t -> p (c t)"),
                                           kvE[j % 2][:, :, :].rearrange("p c t -> p (c t)"), 0.0, ALU.mult, ALU.add
                                           ).then_inc(scanned, 1)
                else:
                    dve.wait_ge(summed, of(b, STEPS, STEPS - 1))
                    dve.wait_ge(z_kept, of(b, NZ, 1))
                    dve.tensor_tensor(og[:, :, :], ps_acc[:, :, :], og[:, :, :], ALU.add).then_inc(og_made, 1)

            run(dve, step, a_unit, z_unit, c_unit)


def build(nc, semaphores, ap, out):
    def between(name):
        return nc.dram_tensor(name, (BATCH, TOK, FEAT), F32, kind="Internal").ap()

    x1, x2, x3, x4, x5 = (between(f"x{i}") for i in range(1, 6))
    context_attention(nc, semaphores, ap["x"], ap["xT"], ap["cT"], ap["L0_xattn_w_q"], ap["L0_xattn_w_k"], ap["L0_xattn_w_v"],
                      ap["L0_w_oT"], ap["L0_xattn_alpha"], x1)
    semaphores.clear()
    channel_attention(nc, semaphores, x1, ap["c"], *(ap["L1_" + n] for n in ("Wqkv0T", "Winj0T", "Wqkv1T", "Winj1T", "WoT", "bo", "q_bias")), x2)
    semaphores.clear()
    w = ap["L2_xattn_w_qkv"]
    token_attention(nc, semaphores, "self", x2, None, ap["mask_self"], 1, ap["L2_ln1"], w[:, 0:FEAT], w[:, FEAT:2 * FEAT],
                    w[:, 2 * FEAT:3 * FEAT], ap["L2_xattn_w_ao"], ap["L2_qk1"], (ap["L2_bv1"], ap["L2_bo1"]), x3)
    semaphores.clear()
    w = ap["L2_xattn_w_kv"]
    token_attention(nc, semaphores, "cross", x3, ap["cT"], ap["mask_cross"], BATCH, ap["L2_ln2"], ap["L2_xattn_w_q"], w[:, 0:FEAT],
                    w[:, FEAT:2 * FEAT], ap["L2_xattn_w_co"], ap["L2_qk2"], (ap["L2_bv2"], ap["L2_bo2"]), x4)
    semaphores.clear()
    token_mlp(nc, semaphores, x4, ap["L2_xattn_w1"], ap["L2_xattn_w2"], ap["L2_ln3"], ap["L2_b1"], ap["L2_b2"], x5)
    semaphores.clear()
    weights = {n: ap[f"L3_W{n}T"] for n in ("r", "k", "v", "g", "o", "fk", "fr", "fv")}
    recurrent_block(nc, semaphores, x5, ap["L3_state"], weights, *(ap["L3_" + n] for n in
                    ("cols", "maa_w1", "maa_w2", "td_w1", "td_w2", "select", "spread", "head_sum", "group_mean")), out)


def lay_out(np, a):
    out = {}

    def put(name, array):
        out[name] = np.ascontiguousarray(array)

    put("x", a["x"])
    put("c", a["ctx_2048"])
    put("cT", a["ctx_2048"].transpose(0, 2, 1))
    if "L0_xattn_w_q" in a:
        put("xT", a["x"].transpose(0, 2, 1))
        for n in ("w_q", "w_k", "w_v"):
            put("L0_xattn_" + n, a["L0_xattn_" + n])
        put("L0_w_oT", a["L0_xattn_w_o"].T)
        put("L0_xattn_alpha", a["L0_xattn_alpha"].reshape(1, 1))
    if "L2_xattn_w_ao" in a:
        def col(v):
            return v.reshape(-1, P).T

        d = {n[len("L2_xattn_"):]: v for n, v in a.items() if n.startswith("L2_xattn_")}
        put("mask_self", a["mask_1x1xSxS2_fc1"][:, 0])
        put("mask_cross", a["mask_Bx1xSxS2_ff1"][:, 0])
        for n in ("w_qkv", "w_ao", "w_q", "w_kv", "w_co", "w1", "w2"):
            put("L2_xattn_" + n, d[n])
        for n in ("ln1", "ln2", "ln3"):
            put("L2_" + n, np.stack([col(d[n + "_s"]), col(d[n + "_b"])], 1))
        put("L2_qk1", np.stack([col(d["b_qkv"][:FEAT]), col(d["b_qkv"][FEAT:2 * FEAT])], 1))
        put("L2_qk2", np.stack([col(d["b_q"]), col(d["b_kv"][:FEAT])], 1))
        put("L2_bv1", d["b_qkv"][2 * FEAT:].reshape(1, FEAT))
        put("L2_bv2", d["b_kv"][FEAT:].reshape(1, FEAT))
        put("L2_bo1", d["b_ao"].reshape(1, FEAT))
        put("L2_bo2", d["b_co"].reshape(1, FEAT))
        put("L2_b1", col(d["b1"]))
        put("L2_b2", d["b2"].reshape(1, FEAT))
    if "L1_xattn_Wo" in a:
        for n in ("Wqkv0", "Winj0", "Wqkv1", "Winj1", "Wo"):
            put("L1_" + n + "T", a["L1_xattn_" + n].T)
        put("L1_bo", a["L1_xattn_bo"].reshape(TT, P).T)
        put("L1_q_bias", a["L1_xattn_r_w_bias"].reshape(-1, P).T)
    if "L3_xattn_Wr" in a:
        d = {n[len("L3_xattn_"):]: v for n, v in a.items() if n.startswith("L3_xattn_")}
        group, heads = 16, P // 16
        by_feature = np.arange(FEAT).reshape(FT, heads, group).transpose(0, 2, 1).reshape(-1)
        for n in ("Wr", "Wk", "Wfk", "Wfr", "Wfv"):
            put("L3_" + n + "T", d[n].T)
        for n in ("Wv", "Wg"):
            put("L3_" + n + "T", d[n].T[:, by_feature])
        put("L3_WoT", d["Wo"].T[by_feature])
        for n in ("maa_w1", "td_w1", "td_w2"):
            put("L3_" + n, d[n])
        put("L3_maa_w2", d["maa_w2"].reshape(-1, FEAT))
        vectors = [d[n].reshape(-1) for n in ("ln1_w", "ln1_b", "ln2_w", "ln2_b", "maa_x", "time_decay", "u")]
        vectors += [d[n][by_feature] for n in ("gn_w", "gn_b")]
        vectors += [d[n] for n in ("ffn_maa_k", "ffn_maa_r")] + list(d["maa_stack"][0])
        put("L3_cols", np.stack([v.reshape(-1, P).T for v in vectors], 1))
        c = a["ctx_2048"]
        edges = c[:, 0:2].transpose(0, 2, 1).reshape(BATCH, FT, P, 2)
        first = c[:, 2:2 + group].reshape(BATCH, FT, P, group)
        put("L3_state", np.concatenate([edges, first], 3).transpose(0, 2, 1, 3))
        p, m = np.arange(P)[:, None], np.arange(P)[None, :]
        put("L3_head_sum", (p // group == m % heads).astype(np.float32))
        put("L3_group_mean", ((p % heads == m % heads) / group).astype(np.float32))
        put("L3_select", np.stack([(p // heads == j) & (p % heads == m // group) for j in range(group)], 1).astype(np.float32))
        window = np.arange((2 * group - 1) * heads)[None, :]
        put("L3_spread", ((window // heads == group - 1) & (window % heads == p // group)).astype(np.float32))
    return out


def kernel(**inputs):
    import numpy as _np
    import concourse.bacc as _bacc
    from concourse import mybir as _mybir
    from concourse.bass_utils import run_bass_kernel_spmd as _run

    arrays = lay_out(_np, {n: _np.asarray(a) for n, a in inputs.items()})
    nc = _bacc.Bacc("TRN2", target_bir_lowering=False, num_devices=1)
    ap = {n: nc.dram_tensor("in_" + n, a.shape, _mybir.dt.from_np(a.dtype), kind="ExternalInput").ap()
          for n, a in arrays.items()}
    out = nc.dram_tensor("out", (BATCH, TOK, FEAT), _mybir.dt.float32, kind="ExternalOutput").ap()
    build(nc, Semaphores(nc), ap, out)
    r = _run(nc, [{"in_" + n: a for n, a in arrays.items()}], core_ids=[0])
    return r.results[0]["out"]
```

```python
from contextlib import ExitStack

import concourse.bass as bass
from concourse import mybir

P = 128
ALU = mybir.AluOpType
ACT = mybir.ActivationFunctionType
AXIS = mybir.AxisListType
F32 = mybir.dt.float32
F32R = mybir.dt.float32r

BATCH, TOK, FEAT = 8, 256, 512
TT, FT = TOK // P, FEAT // P


class Semaphores:

    def __init__(self, nc):
        self.nc, self.taken = nc, []

    def allocate(self, name):
        self.taken.append(self.nc.alloc_semaphore(name=name))
        return self.taken[-1]

    def clear(self):
        self.nc.clear_and_free_semaphores(self.taken)
        self.taken = []
        self.nc.all_engine_barrier()


def at(g, per_pass, k, unit=1):
    return (g * per_pass + k + 1) * unit


def open_loop(eng, sems):
    for s, count in sems:
        eng.sem_inc(s, count)


def make_identity(pool, ident, sem):
    pool.memset(ident[:, :], 0.0).then_inc(sem, 1)
    pool.wait_ge(sem, 1)
    pool.affine_select(out=ident[:, :], in_=ident[:, :], compare_op=ALU.not_equal, fill=1.0, base=0,
                       pattern=[[-1, P]], channel_multiplier=1).then_inc(sem, 1)


def context_attention(nc, semaphores, x, xT, cT, w_q, w_k, w_v, w_oT, alpha, x1):
    PAIRS = BATCH // 2
    SCALE = float(FEAT) ** -0.5
    with ExitStack() as ctx:
        def sb(name, shape):
            return ctx.enter_context(nc.sbuf_tensor("l0_" + name, shape, F32))

        def ps(name, shape):
            return ctx.enter_context(nc.psum_tensor("l0_" + name, shape, F32))

        loop_sems = []

        def sem(name, credit=0):
            s = semaphores.allocate("l0_" + name)
            if credit:
                loop_sems.append((s, credit))
            return s

        def slots(name, credit=1):
            return [sem(f"{name}{u}", credit) for u in range(2)]

        wq, wk, wv, wo = (sb(n, [P, FT, FEAT]) for n in ("wq", "wk", "wv", "wo"))
        qk, vo = sb("qk", [P, FT, FEAT]), sb("vo", [P, FT, FEAT])
        ident = sb("ident", [P, P])
        alpha_col = sb("alpha_col", [P, 1])
        xt = [sb(f"xt{u}", [P, FT, TOK]) for u in range(2)]
        ct = [sb(f"ct{u}", [P, FT, TOK]) for u in range(2)]
        xn = [sb(f"xn{u}", [P, TT, FEAT]) for u in range(2)]
        yt = [sb(f"yt{u}", [P, FT, TOK]) for u in range(2)]
        cv = [sb(f"cv{u}", [P, TT, FEAT]) for u in range(2)]
        pr = [sb(f"pr{u}", [P, TT, TOK]) for u in range(2)]
        prT = [sb(f"prT{u}", [P, TT, TOK]) for u in range(2)]
        res = [sb(f"res{u}", [P, TT, FEAT]) for u in range(2)]
        top = [sb(f"top{u}", [P, TT]) for u in range(2)]
        shift = [sb(f"shift{u}", [P, TT]) for u in range(2)]
        mass = [sb(f"mass{u}", [P, TT]) for u in range(2)]
        gain = [sb(f"gain{u}", [P, TT]) for u in range(2)]

        ps_y = ps("ps_y", [P, FT, TOK])
        ps_cv = ps("ps_cv", [P, TT, FEAT])
        ps_s = ps("ps_s", [P, TT, TOK])
        ps_t = ps("ps_t", [P, TT, TOK])
        ps_d = ps("ps_d", [P, TT, FEAT])

        ident_made, w_loaded, alpha_loaded = sem("ident_made"), sem("w_loaded"), sem("alpha_loaded")
        wv_loaded = sem("wv_loaded")
        qk_summed, qk_kept, vo_summed, vo_kept = sem("qk_summed"), sem("qk_kept"), sem("vo_summed"), sem("vo_kept")
        loaded = slots("loaded", 48)
        stored = slots("stored", 16)
        y_summed = slots("y_summed")
        y_kept = slots("y_kept")
        cv_summed = slots("cv_summed")
        cv_kept = slots("cv_kept")
        scored = slots("scored")
        shifted = slots("shifted")
        probs_made = slots("probs_made")
        turned = slots("turned")
        turned_kept = slots("turned_kept")
        gained = slots("gained")
        delta_summed = slots("delta_summed")
        added = slots("added")
        inverted, topped = slots("inverted"), slots("topped")

        block = ctx.enter_context(nc.Block())

        @block.sync
        def _(sp):
            open_loop(sp, loop_sems)
            for w, src in ((wq, w_q), (wk, w_k)):
                sp.dma_start(w[:, :, :], src.rearrange("(t p) n -> p t n", p=P)).then_inc(w_loaded, 16)
            for w, src in ((wv, w_v), (wo, w_oT)):
                sp.dma_start(w[:, :, :], src.rearrange("(t p) n -> p t n", p=P)).then_inc(wv_loaded, 16)
            sp.dma_start(alpha_col[:, :], alpha.to_broadcast([P, 1])).then_inc(alpha_loaded, 16)
            with sp.Fori(1, PAIRS + 1) as g:
                for u in range(2):
                    b = 2 * g - 2 + u
                    sp.wait_ge(scored[u], g)
                    sp.wait_ge(added[u], g)
                    sp.dma_start(xt[u][:, :, :], xT[bass.ds(b, 1), :, :].rearrange("o (t p) n -> p (o t) n", p=P)).then_inc(loaded[u], 16)
                    sp.dma_start(ct[u][:, :, :], cT[bass.ds(b, 1), :, :].rearrange("o (t p) n -> p (o t) n", p=P)).then_inc(loaded[u], 16)
                    sp.dma_start(xn[u][:, :, :], x[bass.ds(b, 1), :, :].rearrange("o (t p) n -> p (o t) n", p=P)).then_inc(loaded[u], 16)

        @block.gpsimd
        def _(pool):
            make_identity(pool, ident, ident_made)

        @block.tensor
        def _(pe):
            pe.wait_ge(w_loaded, 32)
            for m in range(FT):
                for t in range(FT):
                    mm = pe.matmul(ps_y[:, 2 * (m % 2):2 * (m % 2) + 2, :] if m < 2 else ps_cv[:, m - 2, :],
                                   wq[:, t, m * P:(m + 1) * P], wk[:, t, :], start=(t == 0), stop=(t == FT - 1))
                mm.then_inc(qk_summed, 1)
            pe.wait_ge(wv_loaded, 32)
            pe.wait_ge(qk_kept, FT)
            for m in range(FT):
                for t in range(FT):
                    mm = pe.matmul(ps_y[:, 2 * (m % 2):2 * (m % 2) + 2, :] if m < 2 else ps_cv[:, m - 2, :],
                                   wv[:, t, m * P:(m + 1) * P], wo[:, t, :], start=(t == 0), stop=(t == FT - 1))
                mm.then_inc(vo_summed, 1)
            pe.wait_ge(vo_kept, FT)
            pe.wait_ge(ident_made, 2)
            with pe.Fori(1, PAIRS + 1) as g:
                def project_queries(u):
                    pe.wait_ge(loaded[u], 48 * g + 48)
                    if u == 1:
                        pe.wait_ge(y_kept[0], g + 1)
                    for m in range(FT):
                        for t in range(FT):
                            mm = pe.matmul(ps_y[:, m, :], qk[:, t, m * P:(m + 1) * P], xt[u][:, t, :],
                                           start=(t == 0), stop=(t == FT - 1))
                    mm.then_inc(y_summed[u], 1)

                def project_values(u):
                    if u == 1:
                        pe.wait_ge(cv_kept[0], g + 1)
                    for m in range(TT):
                        for t in range(FT):
                            mm = pe.matmul(ps_cv[:, m, :], ct[u][:, t, m * P:(m + 1) * P], vo[:, t, :],
                                           start=(t == 0), stop=(t == FT - 1))
                    mm.then_inc(cv_summed[u], 1)

                def score(u):
                    pe.wait_ge(y_kept[u], g + 1)
                    if u == 1:
                        pe.wait_ge(probs_made[0], g + 1)
                    for m in range(TT):
                        for t in range(FT):
                            mm = pe.matmul(ps_s[:, m, :], yt[u][:, t, m * P:(m + 1) * P], ct[u][:, t, :],
                                           start=(t == 0), stop=(t == FT - 1))
                    mm.then_inc(scored[u], 1)

                def turn(u):
                    pe.wait_ge(probs_made[u], g + 1)
                    if u == 1:
                        pe.wait_ge(turned_kept[0], g + 1)
                    for m in range(TT):
                        for t in range(TT):
                            mm = pe.transpose(ps_t[:, t, m * P:(m + 1) * P], pr[u][:, m, t * P:(t + 1) * P], ident[:, :])
                    mm.then_inc(turned[u], 1)

                def mix(u):
                    pe.wait_ge(turned_kept[u], g + 1)
                    pe.wait_ge(cv_kept[u], g + 1)
                    if u == 1:
                        pe.wait_ge(added[0], g + 1)
                    else:
                        pe.wait_ge(added[1], g)
                    for m in range(TT):
                        for t in range(TT):
                            mm = pe.matmul(ps_d[:, m, :], prT[u][:, t, m * P:(m + 1) * P], cv[u][:, t, :],
                                           start=(t == 0), stop=(t == TT - 1))
                    mm.then_inc(delta_summed[u], 1)

                project_queries(0)
                project_values(0)
                project_queries(1)
                score(0)
                project_values(1)
                turn(0)
                score(1)
                mix(0)
                turn(1)
                mix(1)

        @block.scalar
        def _(act):
            for m in range(FT):
                act.wait_ge(qk_summed, m + 1)
                act.activation(qk[:, m, :], ps_y[:, 2 * m:2 * m + 2, :].rearrange("p a b -> p (a b)") if m < 2 else ps_cv[:, m - 2, :],
                               ACT.Copy).then_inc(qk_kept, 1)
            for m in range(FT):
                act.wait_ge(vo_summed, m + 1)
                act.activation(vo[:, m, :], ps_y[:, 2 * m:2 * m + 2, :].rearrange("p a b -> p (a b)") if m < 2 else ps_cv[:, m - 2, :],
                               ACT.Copy).then_inc(vo_kept, 1)
            with act.Fori(1, PAIRS + 1) as g:
                def keep_queries(u):
                    act.wait_ge(y_summed[u], g + 1)
                    act.activation(yt[u][:, :, :], ps_y[:, :, :], ACT.Copy).then_inc(y_kept[u], 1)

                def exponentials(u):
                    act.wait_ge(shifted[u], g + 1)
                    act.wait_ge(turned[u], g)
                    act.wait_ge(gained[u], g)
                    for m in range(TT):
                        ins = act.activation(pr[u][:, m, :], ps_s[:, m, :], ACT.Exp, bias=shift[u][:, m:m + 1],
                                             scale=SCALE, accum_out=mass[u][:, m:m + 1])
                    ins.then_inc(probs_made[u], 1)

                def store(u):
                    act.wait_ge(added[u], g + 1)
                    act.dma_start(x1[bass.ds(2 * g - 2 + u, 1), :, :].rearrange("o (t p) n -> p (o t) n", p=P),
                                  res[u][:, :, :]).then_inc(stored[u], 16)

                keep_queries(0)
                keep_queries(1)
                exponentials(0)
                exponentials(1)
                store(0)
                store(1)
            for u in range(2):
                act.wait_ge(stored[u], 16 * (PAIRS + 1))

        @block.vector
        def _(dve):
            dve.wait_ge(alpha_loaded, 16)
            with dve.Fori(1, PAIRS + 1) as g:
                def keep_values(u):
                    dve.wait_ge(cv_summed[u], g + 1)
                    dve.tensor_copy(cv[u][:, :, :], ps_cv[:, :, :]).then_inc(cv_kept[u], 1)

                def row_max(u):
                    dve.wait_ge(scored[u], g + 1)
                    dve.wait_ge(probs_made[u], g)
                    dve.tensor_reduce(top[u][:, :], ps_s[:, :, :], AXIS.X, ALU.max, negate=True).then_inc(topped[u], 1)
                    dve.wait_ge(topped[u], g + 1)
                    dve.tensor_scalar(shift[u][:, :], top[u][:, :], SCALE, None, ALU.mult).then_inc(shifted[u], 1)

                def keep_turned(u):
                    dve.wait_ge(turned[u], g + 1)
                    dve.wait_ge(probs_made[u], g + 1)
                    dve.tensor_copy(prT[u][:, :, :], ps_t[:, :, :]).then_inc(turned_kept[u], 1)
                    dve.reciprocal(gain[u][:, :], mass[u][:, :]).then_inc(inverted[u], 1)
                    dve.wait_ge(inverted[u], g + 1)
                    dve.tensor_scalar(gain[u][:, :], gain[u][:, :], alpha_col[:, 0:1], None, ALU.mult).then_inc(gained[u], 1)

                def add(u):
                    dve.wait_ge(delta_summed[u], g + 1)
                    dve.wait_ge(gained[u], g + 1)
                    dve.wait_ge(stored[u], 16 * g)
                    for m in range(TT):
                        ins = dve.scalar_tensor_tensor(out=res[u][:, m, :], in0=ps_d[:, m, :], scalar=gain[u][:, m:m + 1],
                                                       in1=xn[u][:, m, :], op0=ALU.mult, op1=ALU.add)
                    ins.then_inc(added[u], 1)

                keep_values(0)
                row_max(0)
                keep_values(1)
                keep_turned(0)
                row_max(1)
                add(0)
                keep_turned(1)
                add(1)


def channel_attention(nc, semaphores, z, c, w_qkv0T, w_inj0T, w_qkv1T, w_inj1T, w_oT, bo, q_bias, out):
    HEADS, DH = 16, 64
    INNER = HEADS * DH
    HP = HEADS // 2
    QT = FEAT // P
    STEPS = 2 * HEADS
    TILES = 2 * STEPS
    PROJECT_AHEAD = 2
    TURN_LAG, MIX_LAG = 2, 3
    OUTPUT_FROM = STEPS - 5
    SCALE = DH ** -0.5
    CT = TOK // P
    with ExitStack() as ctx:
        def sb(name, shape, dtype=F32):
            return ctx.enter_context(nc.sbuf_tensor("l1_" + name, shape, dtype))

        def ps(name, shape):
            return ctx.enter_context(nc.psum_tensor("l1_" + name, shape, F32))

        loop_sems = []

        def sem(name, credit=0):
            s = semaphores.allocate("l1_" + name)
            if credit:
                loop_sems.append((s, credit))
            return s

        w = [sb(f"w{i}", [P, CT, 3 * INNER]) for i in range(4)]
        wo_hi, wo_lo = sb("wo_hi", [P, HP, TOK], F32R), sb("wo_lo", [P, HP, TOK], F32R)
        ident, mean_of = sb("ident", [P, P]), sb("mean_of", [P, P])
        one = sb("one", [P, 1])
        bo_col, qb_col = sb("bo_col", [P, CT]), sb("qb_col", [P, HP])
        zt, ut, zres = sb("zt", [P, CT, FEAT]), sb("ut", [P, CT, FEAT]), sb("zres", [P, CT, FEAT])
        q = [sb(f"q{i}", [P, 2, FEAT], F32R) for i in range(2)]
        k = [sb(f"k{i}", [P, 2, FEAT], F32R) for i in range(2)]
        k_lo = [sb(f"k_lo{i}", [P, FEAT], F32R) for i in range(2)]
        vo = sb("vo", [P, HEADS, QT, 2 * DH], F32R)
        pr = sb("pr", [P, TURN_LAG + 1, 2, FEAT])
        p_hi = [sb(f"p_hi{i}", [P, QT, 2 * P], F32R) for i in range(2)]
        p_lo = [sb(f"p_lo{i}", [P, QT, 2 * P], F32R) for i in range(2)]
        shift, mass, inv = sb("shift", [P, 4]), sb("mass", [P, 4]), sb("inv", [P, 4])
        o_sum = sb("o_sum", [P, FEAT])
        wo_raw = pr[:, 0:2, :, :].rearrange("p a b n -> p (a b n)")
        xr, sq, rstd = pr[:, 0, :, :], pr[:, 1, :, :], pr[:, 1, 0, :]

        ps_q, ps_k = ps("ps_q", [P, FEAT]), ps("ps_k", [P, FEAT])
        ps_s = ps("ps_s", [P, 2, FEAT])
        ps_t = [ps(f"ps_t{h}", [P, QT, P]) for h in range(2)]
        ps_o = [ps(f"ps_o{i}", [P, FEAT]) for i in range(2)]

        mean_made, ident_made, wo_split = sem("mean_made"), sem("ident_made"), sem("wo_split")
        v_w_loaded, qk_w_loaded, o_w_loaded, cols_loaded = (sem(n) for n in ("v_w_loaded", "qk_w_loaded", "o_w_loaded", "cols_loaded"))
        zu_loaded, zres_loaded, stored = sem("zu_loaded", 32), sem("zres_loaded", 16), sem("stored", 16)
        v_summed, v_hi_kept, v_kept = sem("v_summed", 8), sem("v_hi_kept", 8), sem("v_kept", 8)
        q_summed, k_summed, q_hi_kept, k_hi_kept, q_kept, k_lo_kept = (
            sem(n, HP) for n in ("q_summed", "k_summed", "q_hi_kept", "k_hi_kept", "q_kept", "k_lo_kept"))
        k_mirrored = sem("k_mirrored", 2 * HP)
        scored, shifted, exped, inverted, scaled, turned, p_hi_kept, p_kept = (
            sem(n, TILES) for n in ("scored", "shifted", "exped", "inverted", "scaled", "turned", "p_hi_kept", "p_kept"))
        mixed, o_moved, o_summed, o_split = sem("mixed", STEPS), sem("o_moved", HEADS), sem("o_summed", HEADS), sem("o_split", 2 * HP)
        attn_summed, added, means_summed, centred, squared, vars_summed, rooted, normed = (
            sem(n, 1) for n in ("attn_summed", "added", "means_summed", "centred", "squared", "vars_summed", "rooted", "normed"))
        inv_var = sem("inv_var", 2)

        block = ctx.enter_context(nc.Block())

        def own(h):
            return slice(h * DH, (h + 1) * DH)

        def batch_rows(a, g):
            batch = slice(g - 1, g) if isinstance(g, int) else bass.ds(g - 1, 1)
            return a[batch, :, :].rearrange("o (t p) n -> p (o t) n", p=P)

        def run(eng, body, after_value, norm_parts):
            def one_pass(g, with_norm):
                if with_norm and -1 in norm_parts:
                    norm_parts[-1](g - 1)
                for e in range(8):
                    after_value(g, e)
                    if with_norm and e in norm_parts:
                        norm_parts[e](g - 1)
                body(g)

            one_pass(1, False)
            with eng.Fori(2, BATCH + 1) as g:
                one_pass(g, True)
            for e in sorted(norm_parts):
                norm_parts[e](BATCH)

        def pair_projected(n):
            pair, unit = divmod(n + PROJECT_AHEAD, QT)
            return (unit // 2, pair + 1) if n >= 0 and unit % 2 == 1 and pair + 1 < HP else (None, None)

        @block.sync
        def _(sp):
            open_loop(sp, loop_sems)
            w_dram = [a.rearrange("(t p) n -> p t n", p=P) for a in (w_qkv0T, w_inj0T, w_qkv1T, w_inj1T)]

            def load_w(lo, hi, s):
                for i in range(4):
                    sp.dma_start(w[i][:, :, lo:hi], w_dram[i][:, :, lo:hi]).then_inc(s, 16)

            def load(g):
                sp.wait_ge(k_summed, at(g, HP, -1))
                sp.wait_ge(q_summed, at(g, HP, -1))
                sp.dma_start(zt[:, :, :], batch_rows(z, g)).then_inc(zu_loaded, 16)
                sp.dma_start(ut[:, :, :], batch_rows(c, g)).then_inc(zu_loaded, 16)

            def load_zres(g):
                sp.wait_ge(stored, at(g, 1, -1, 16))
                sp.dma_start(zres[:, :, :], batch_rows(z, g)).then_inc(zres_loaded, 16)

            load_w(2 * INNER, 3 * INNER, v_w_loaded)
            load(1)
            load_w(0, 2 * INNER, qk_w_loaded)
            load_zres(1)
            with sp.Fori(2, BATCH + 1) as g:
                load(g)
                load_zres(g)

        @block.tensor
        def _(pe):
            pe.wait_ge(ident_made, 2)
            pe.wait_ge(mean_made, 1)
            pe.wait_ge(wo_split, 2)
            def body(g):
                def project(pair, part, half):
                    bank, summed = (ps_q, q_summed) if part == 0 else (ps_k, k_summed)
                    if half == 0:
                        pe.wait_ge(q_kept if part == 0 else k_lo_kept, at(g, HP, pair - 1))
                    cols = slice(part * INNER + pair * P, part * INNER + (pair + 1) * P)
                    here = slice(half * TOK, (half + 1) * TOK)
                    terms = [(w[2 * half + i], src, t) for i, src in enumerate((zt, ut)) for t in range(CT)]
                    for i, (wt, src, t) in enumerate(terms):
                        mm = pe.matmul(bank[:, here], wt[:, t, cols], src[:, t, here],
                                       start=(i == 0), stop=(i == len(terms) - 1), skip_group_check=True)
                    if half == 1:
                        mm.then_inc(summed, 1)

                def score(n):
                    pair, h, half = n // QT, n // 2 % 2, n % 2
                    if n % QT == 0:
                        pe.wait_ge(q_kept, at(g, HP, pair))
                        pe.wait_ge(k_lo_kept, at(g, HP, pair))
                        pe.wait_ge(k_mirrored, at(g, 2 * HP, 2 * pair + 1))
                    for i in range(2):
                        here = slice((2 * half + i) * P, (2 * half + i + 1) * P)
                        pe.wait_ge(exped, at(g, TILES, 2 * n + i - 2))
                        pe.matmul(ps_s[:, i, :], q[pair % 2][:, h, here], k[pair % 2][:, h, :], start=True, stop=False)
                        pe.matmul(ps_s[:, i, :], q[pair % 2][own(h), h, here], k_lo[pair % 2][own(h), :],
                                  start=False, stop=True).then_inc(scored, 1)

                def turn(n):
                    for i in range(2):
                        pe.wait_ge(scaled, at(g, TILES, 2 * n + i))
                        pe.wait_ge(p_kept, at(g, TILES, 2 * n + i - 2))
                        for t in range(QT):
                            mm = pe.transpose(ps_t[i][:, t, :], pr[:, n % (TURN_LAG + 1), i, t * P:(t + 1) * P], ident[:, :])
                        mm.then_inc(turned, 1)

                def mix(n):
                    head, half = n // 2, n % 2
                    pe.wait_ge(p_kept, at(g, TILES, 2 * n + 1))
                    if half == 0:
                        pe.wait_ge(o_summed, at(g, HEADS, head - 2))
                    for t in range(QT):
                        for part in (p_hi, p_lo):
                            mm = pe.matmul(ps_o[head % 2][:, half * 2 * P:(half + 1) * 2 * P], vo[:, head, t, :],
                                           part[n % 2][:, t, :], start=(t == 0 and part is p_hi),
                                           stop=(t == QT - 1 and part is p_lo), skip_group_check=True)
                    mm.then_inc(mixed, 1)

                pe.wait_ge(qk_w_loaded, 64)
                pe.wait_ge(added, at(g, 1, -1))
                def contract_output(t):
                    if t == 0:
                        pe.wait_ge(q_kept, at(g, HP, HP - 1))
                        pe.wait_ge(k_lo_kept, at(g, HP, HP - 1))
                    pe.wait_ge(o_split, at(g, 2 * HP, 2 * t + 1))
                    o_hi, o_lo = vo[:, 2 * t, :, :], vo[:, 2 * t + 1, :, :]
                    for m, bank in enumerate((ps_q, ps_k)):
                        here = slice(m * P, (m + 1) * P)
                        for wo, o in ((wo_lo, o_hi), (wo_hi, o_lo), (wo_hi, o_hi)):
                            mm = pe.matmul(bank[:, :], wo[:, t, here], o, start=(t == 0 and wo is wo_lo),
                                           stop=(t == HP - 1 and wo is wo_hi and o is o_hi), skip_group_check=True)
                    return mm

                for m in range(QT + PROJECT_AHEAD):
                    project(m // QT, m % QT // 2, m % 2)
                pe.wait_ge(v_kept, at(g, 8, 7))
                pe.wait_ge(normed, at(g, 1, -1))
                for n in range(STEPS + MIX_LAG):
                    if TURN_LAG <= n < STEPS + TURN_LAG:
                        turn(n - TURN_LAG)
                    if n < STEPS:
                        score(n)
                    if n < STEPS:
                        pair, unit = divmod(n + PROJECT_AHEAD, QT)
                        if pair + 1 < HP:
                            project(pair + 1, unit // 2, unit % 2)
                    if 0 <= n - OUTPUT_FROM < HP - 1:
                        contract_output(n - OUTPUT_FROM)
                    if n >= MIX_LAG:
                        mix(n - MIX_LAG)
                contract_output(HP - 1).then_inc(attn_summed, 1)

            def values(g, e):
                if e == 0:
                    pe.wait_ge(zu_loaded, at(g, 2, 1, 16))
                    pe.wait_ge(v_w_loaded, 64)
                if e >= 4:
                    pe.wait_ge(v_kept, at(g, 8, e - 4))
                lt, chunk = e // 2, e % 2
                terms = [(w[2 * (lt // 2) + i], src, t) for i, src in enumerate((zt, ut)) for t in range(CT)]
                bank = (ps_t[0][:, :, :], ps_t[1][:, :, :], ps_o[0][:, :], ps_o[1][:, :])[e % 4]
                for i, (wt, src, t) in enumerate(terms):
                    mm = pe.matmul(bank, src[:, t, lt * P:(lt + 1) * P],
                                   wt[:, t, 2 * INNER + chunk * FEAT:2 * INNER + (chunk + 1) * FEAT],
                                   start=(i == 0), stop=(i == len(terms) - 1))
                mm.then_inc(v_summed, 1)

            def means(g):
                pe.wait_ge(added, at(g, 1, 0))
                for t in range(CT):
                    mm = pe.matmul(ps_s[:, 0, :], mean_of[:, :], xr[:, t, :], start=(t == 0), stop=(t == CT - 1))
                mm.then_inc(means_summed, 1)

            def variances(g):
                pe.wait_ge(squared, at(g, 1, 0))
                for t in range(CT):
                    mm = pe.matmul(ps_s[:, 1, :], mean_of[:, :], sq[:, t, :], start=(t == 0), stop=(t == CT - 1))
                mm.then_inc(vars_summed, 1)

            run(pe, body, values, {0: means, 3: variances})

        def value_bank(e):
            bank = (ps_t[0][:, :, :], ps_t[1][:, :, :], ps_o[0][:, :], ps_o[1][:, :])[e % 4]
            return (bank.rearrange("p a b -> p (a b)") if e % 4 < 2 else bank).rearrange("p (h d) -> p h d", d=DH)

        def value_place(e, low):
            lt, chunk = e // 2, e % 2
            return vo[:, chunk * 8:(chunk + 1) * 8, lt, low * DH:(low + 1) * DH]

        @block.scalar
        def _(act):
            act.dma_start(wo_raw.rearrange("p (t n) -> p t n", n=TOK), w_oT.rearrange("(t p) n -> p t n", p=P)).then_inc(o_w_loaded, 16)
            act.dma_start(bo_col[:, :], bo).then_inc(cols_loaded, 16)
            act.dma_start(qb_col[:, :], q_bias).then_inc(cols_loaded, 16)
            act.wait_ge(o_w_loaded, 16)
            act.activation(wo_hi[:, :, :].rearrange("p t n -> p (t n)"), wo_raw, ACT.Copy).then_inc(wo_split, 1)
            act.wait_ge(cols_loaded, 32)
            def body(g):
                def queries_hi(pair):
                    act.wait_ge(q_summed, at(g, HP, pair))
                    act.wait_ge(scored, at(g, TILES, 2 * QT * (pair - 1) - 1))
                    for h in range(2):
                        ins = act.activation(q[pair % 2][own(h), h, :], ps_q[own(h), :], ACT.Identity,
                                             bias=qb_col[own(h), pair:pair + 1])
                    ins.then_inc(q_hi_kept, 1)

                def keys_hi(pair):
                    act.wait_ge(k_summed, at(g, HP, pair))
                    act.wait_ge(scored, at(g, TILES, 2 * QT * (pair - 1) - 1))
                    for h in range(2):
                        ins = act.activation(k[pair % 2][own(h), h, :], ps_k[own(h), :], ACT.Copy, scale=SCALE)
                    ins.then_inc(k_hi_kept, 1)

                def exponentials(n):
                    for i in range(2):
                        a = n % 2 * 2 + i
                        act.wait_ge(shifted, at(g, TILES, 2 * n + i))
                        act.wait_ge(turned, at(g, TILES, 2 * (n - TURN_LAG - 1) + i))
                        act.wait_ge(inverted, at(g, TILES, 2 * n + i - 4))
                        act.activation(pr[:, n % (TURN_LAG + 1), i, :], ps_s[:, i, :], ACT.Exp, bias=shift[:, a:a + 1],
                                       accum_out=mass[:, a:a + 1]).then_inc(exped, 1)

                def turned_hi(n):
                    act.wait_ge(mixed, at(g, STEPS, n - 2))
                    for i in range(2):
                        act.wait_ge(turned, at(g, TILES, 2 * n + i))
                        act.activation(p_hi[n % 2][:, :, i * P:(i + 1) * P], ps_t[i][:, :, :], ACT.Copy).then_inc(p_hi_kept, 1)

                def move_output(n):
                    if n % 2 == 1:
                        head, h = n // 2, n // 2 % 2
                        act.wait_ge(mixed, at(g, STEPS, n))
                        if h == 0:
                            act.wait_ge(o_split, at(g, 2 * HP, 2 * (head // 2) - 1))
                        act.activation(o_sum[own(h), :], ps_o[h][own(1 - h), :], ACT.Copy).then_inc(o_moved, 1)

                queries_hi(0)
                keys_hi(0)
                queries_hi(1)
                for n in range(STEPS + MIX_LAG + 1):
                    if n > MIX_LAG:
                        move_output(n - MIX_LAG - 1)
                    if TURN_LAG <= n < STEPS + TURN_LAG:
                        turned_hi(n - TURN_LAG)
                    if n < STEPS:
                        exponentials(n)
                    part, pair = pair_projected(n)
                    if pair is not None:
                        (queries_hi, keys_hi)[part](pair)

            def values_hi(g, e):
                act.wait_ge(v_summed, at(g, 8, e))
                act.activation(value_place(e, 0), value_bank(e), ACT.Copy).then_inc(v_hi_kept, 1)

            def squares(g):
                act.wait_ge(centred, at(g, 1, 0))
                act.activation(sq, zres[:, :, :], ACT.Square).then_inc(squared, 1)

            def root_and_store(g):
                act.wait_ge(inv_var, at(g, 2, 1))
                act.activation(rstd, rstd, ACT.Sqrt).then_inc(rooted, 1)
                act.wait_ge(normed, at(g, 1, 0))
                act.dma_start(batch_rows(out, g), zres[:, :, :]).then_inc(stored, 16)

            run(act, body, values_hi, {2: squares, 6: root_and_store})
            act.wait_ge(stored, 16 * (BATCH + 1))

        @block.gpsimd
        def _(pool):
            make_identity(pool, ident, ident_made)
            pool.memset(one[:, :], 1.0).then_inc(ident_made, 1)
            pool.wait_ge(ident_made, 3)
            with pool.Fori(1, BATCH + 1) as g:
                def mirror_keys(pair, n=0):
                    pool.wait_ge(scaled, at(g, TILES, 2 * n - 1))
                    pool.wait_ge(o_split, at(g, 2 * HP, 2 * max(0, (n - MIX_LAG - 1) // QT) - 1))
                    pool.wait_ge(k_hi_kept, at(g, HP, pair))
                    for h in range(2):
                        there = k[pair % 2][own(h), h, :].bitcast(F32)
                        ins = pool.tensor_tensor(k[pair % 2][own(1 - h), h, :], there, one[own(h), :].to_broadcast([DH, FEAT]), ALU.mult)
                        ins.then_inc(k_mirrored, 1)
                        pool.wait_ge(k_mirrored, at(g, 2 * HP, 2 * pair + h))

                def scale(n):
                    for i in range(2):
                        a = n % 2 * 2 + i
                        pool.wait_ge(inverted, at(g, TILES, 2 * n + i))
                        pool.tensor_tensor(pr[:, n % (TURN_LAG + 1), i, :], pr[:, n % (TURN_LAG + 1), i, :],
                                           inv[:, a:a + 1].to_broadcast([P, FEAT]), ALU.mult).then_inc(scaled, 1)

                def split_output(n):
                    if n % QT == QT - 1:
                        pair = n // QT
                        o_hi, o_lo = (vo[:, 2 * pair + i, :, :].rearrange("p a b -> p (a b)") for i in range(2))
                        pool.wait_ge(o_summed, at(g, HEADS, 2 * pair + 1))
                        pool.tensor_tensor(o_hi, o_sum[:, :], one[:, :].to_broadcast([P, FEAT]), ALU.mult).then_inc(o_split, 1)
                        pool.wait_ge(o_split, at(g, 2 * HP, 2 * pair))
                        pool.tensor_tensor(o_lo, o_sum[:, :], o_hi.bitcast(F32), ALU.subtract).then_inc(o_split, 1)

                mirror_keys(0)
                for n in range(STEPS + MIX_LAG + 1):
                    part, pair = pair_projected(n - 1)
                    if part == 1:
                        mirror_keys(pair, n)
                    if n < STEPS:
                        scale(n)
                    if n > MIX_LAG:
                        split_output(n - MIX_LAG - 1)

        @block.vector
        def _(dve):
            dve.memset(mean_of[:, :], 1.0 / TOK).then_inc(mean_made, 1)
            dve.wait_ge(wo_split, 1)
            dve.wait_ge(cols_loaded, 32)
            dve.tensor_tensor(wo_lo[:, :, :].rearrange("p t n -> p (t n)"), wo_raw,
                              wo_hi[:, :, :].rearrange("p t n -> p (t n)").bitcast(F32), ALU.subtract).then_inc(wo_split, 1)
            def body(g):
                def queries_lo(pair):
                    dve.wait_ge(q_hi_kept, at(g, HP, pair))
                    for h in range(2):
                        ins = dve.scalar_tensor_tensor(out=q[pair % 2][own(1 - h), h, :], in0=ps_q[own(h), :],
                                                       scalar=qb_col[own(h), pair:pair + 1],
                                                       in1=q[pair % 2][own(h), h, :].bitcast(F32), op0=ALU.add, op1=ALU.subtract)
                    ins.then_inc(q_kept, 1)

                def keys_lo(pair):
                    dve.wait_ge(k_hi_kept, at(g, HP, pair))
                    for h in range(2):
                        ins = dve.scalar_tensor_tensor(out=k_lo[pair % 2][own(h), :], in0=ps_k[own(h), :], scalar=SCALE,
                                                       in1=k[pair % 2][own(h), h, :].bitcast(F32), op0=ALU.mult, op1=ALU.subtract)
                    ins.then_inc(k_lo_kept, 1)

                def shifts(n):
                    for i in range(2):
                        a = n % 2 * 2 + i
                        dve.wait_ge(scored, at(g, TILES, 2 * n + i))
                        dve.wait_ge(exped, at(g, TILES, 2 * n + i - 4))
                        dve.tensor_reduce(shift[:, a:a + 1], ps_s[:, i, :], AXIS.X, ALU.max, negate=True).then_inc(shifted, 1)

                def inverse(n, i):
                    a = n % 2 * 2 + i
                    dve.wait_ge(exped, at(g, TILES, 2 * n + i))
                    dve.wait_ge(scaled, at(g, TILES, 2 * n + i - 4))
                    dve.reciprocal(inv[:, a:a + 1], mass[:, a:a + 1]).then_inc(inverted, 1)

                def inverses(n):
                    for i in range(2):
                        inverse(n, i)

                def turned_lo(n):
                    for i in range(2):
                        here = slice(i * P, (i + 1) * P)
                        dve.wait_ge(p_hi_kept, at(g, TILES, 2 * n + i))
                        dve.tensor_tensor(p_lo[n % 2][:, :, here], ps_t[i][:, :, :], p_hi[n % 2][:, :, here].bitcast(F32),
                                          ALU.subtract).then_inc(p_kept, 1)

                def sum_output(n):
                    if n % 2 == 1:
                        head, h = n // 2, n // 2 % 2
                        dve.wait_ge(o_moved, at(g, HEADS, head))
                        dve.tensor_tensor(o_sum[own(h), :], ps_o[h][own(h), :], o_sum[own(h), :], ALU.add).then_inc(o_summed, 1)

                queries_lo(0)
                keys_lo(0)
                queries_lo(1)
                for n in range(STEPS + MIX_LAG + 1):
                    if n < STEPS:
                        shifts(n)
                    if TURN_LAG <= n < STEPS + TURN_LAG:
                        turned_lo(n - TURN_LAG)
                    if n < STEPS:
                        inverses(n)
                    part, pair = pair_projected(n - 1)
                    if pair is not None:
                        (queries_lo, keys_lo)[part](pair)
                    if n > MIX_LAG:
                        sum_output(n - MIX_LAG - 1)

            def values_lo(g, e):
                dve.wait_ge(v_hi_kept, at(g, 8, e))
                dve.tensor_tensor(value_place(e, 1), value_bank(e), value_place(e, 0).bitcast(F32), ALU.subtract).then_inc(v_kept, 1)

            def add(g):
                dve.wait_ge(attn_summed, at(g, 1, 0))
                dve.wait_ge(zres_loaded, at(g, 1, 0, 16))
                for m, bank in enumerate((ps_q, ps_k)):
                    ins = dve.scalar_tensor_tensor(out=xr[:, m, :], in0=bank[:, :], scalar=bo_col[:, m:m + 1],
                                                   in1=zres[:, m, :], op0=ALU.add, op1=ALU.add)
                ins.then_inc(added, 1)

            def centre(g):
                dve.wait_ge(means_summed, at(g, 1, 0))
                for m in range(CT):
                    ins = dve.tensor_tensor(zres[:, m, :], xr[:, m, :], ps_s[:, 0, :], ALU.subtract)
                ins.then_inc(centred, 1)

            def invert(g):
                dve.wait_ge(vars_summed, at(g, 1, 0))
                dve.tensor_scalar(rstd, ps_s[:, 1, :], 1e-5, None, ALU.add).then_inc(inv_var, 1)
                dve.wait_ge(inv_var, at(g, 2, 0))
                dve.reciprocal(rstd, rstd).then_inc(inv_var, 1)

            def normalise(g):
                dve.wait_ge(rooted, at(g, 1, 0))
                for m in range(CT):
                    ins = dve.tensor_tensor(zres[:, m, :], zres[:, m, :], rstd, ALU.mult)
                ins.then_inc(normed, 1)

            run(dve, body, values_lo, {-1: add, 1: centre, 5: invert, 6: normalise})

def token_attention(nc, semaphores, tag, x, cT, mask, mask_batches, ln_cols, wq_d, wk_d, wv_d, wo_d, qk_cols, rows, out):
    HEADS, DH = 16, 32
    STEPS = HEADS // 2
    TILE_HEADS = P // DH
    RING = 4
    PASSES = BATCH // 2
    SCALE = DH ** -0.5
    CROSS = cT is not None
    ORDER = ("K0", "K1", "T0", "T1", "Q0", "Q1", "V0", "V1") if CROSS else ("T0", "T1", "Q0", "Q1", "K0", "K1", "V0", "V1")
    FILL = dict(zip((0, 1, 2, 3, 4, 5, 8, 10) if CROSS else (1, 2, 3, 4, 5, 6, 8, 10), ORDER))
    LOADS = 3 if CROSS else 2
    TURN_LAG, MIX_LAG = 2, 3
    LAST = STEPS + MIX_LAG
    with ExitStack() as ctx:
        def sb(name, shape):
            return ctx.enter_context(nc.sbuf_tensor(f"{tag}_{name}", shape, F32))

        def ps(name, shape):
            return ctx.enter_context(nc.psum_tensor(f"{tag}_{name}", shape, F32))

        loop_sems = []

        def sem(name, per_batch=0):
            s = semaphores.allocate(f"{tag}_{name}")
            if per_batch:
                loop_sems.append((s, 2 * per_batch))
            return s

        wq, wk, wv, wo = (sb(n, [P, FT, FEAT]) for n in ("wq", "wk", "wv", "wo"))
        ln_sb, qk_sb = sb("ln_cols", [P, 2, FT]), sb("qk_cols", [P, 2, FT])
        rows_sb = sb("rows", [P, 2, FEAT])
        ident = sb("ident", [P, P])
        half_power = sb("half_power", [P, TT])
        xs = [sb(f"xs{u}", [P, TT, FEAT]) for u in range(2)]
        cs = [sb(f"cs{u}", [P, FT, TOK]) for u in range(2)] if CROSS else None
        mk = [sb(f"mk{u}", [P, TT, TOK]) for u in range(2)]
        ma = [sb(f"ma{u}", [P, TT, TOK]) for u in range(2)]
        stats, moments, var_eps, rstd = sb("stats", [P, TT, 6]), sb("moments", [P, TT, 2]), sb("var_eps", [P, TT]), sb("rstd", [P, TT])
        xn = sb("xn", [P, TT, FEAT])
        lnT = sb("lnT", [P, FT, TOK])
        qT = [sb(f"qT{u}", [P, FT, TOK]) for u in range(2)]
        kT = [sb(f"kT{u}", [P, FT, TOK]) for u in range(2)]
        v = [sb(f"v{u}", [P, TT, FEAT]) for u in range(2)]
        pr = [sb(f"pr{i}", [P, 2, TT, TOK]) for i in range(RING)]
        pT = [sb(f"pT{i}", [P, 2, TT, TOK]) for i in range(2)]
        shift, mass, inv = ([sb(f"{n}{i}", [P, 2, TT]) for i in range(RING)] for n in ("shift", "mass", "inv"))
        ctxT = sb("ctxT", [P, FT, TOK])
        xb = sb("xb", [P, TT, FEAT])
        res = sb("res", [P, TT, FEAT])

        ps_s = [ps(f"ps_s{i}", [P, 2, TT, TOK]) for i in range(2)]
        ps_t = ps("ps_t", [P, 2, TT, TOK])
        ps_o = ps("ps_o", [P, TOK])
        ps_p = ps("ps_p", [P, 2, TOK])

        w_loaded, ident_made, const_made = sem("w_loaded"), sem("ident_made"), sem("const_made")
        loaded, stored = [sem(f"loaded{u}") for u in range(2)], sem("stored", 16)
        counted, normalised, biased, mask_split = sem("counted", 4), sem("normalised", 1), sem("biased", 1), sem("mask_split", 2)
        powered = sem("powered", 1)
        filled, fill_kept = sem("filled", 8), sem("fill_kept", 8)
        scored, masked_mul, masked, shifted, exped, inverted, normed, turned, turned_kept = (
            sem(n, STEPS) for n in ("scored", "masked_mul", "masked", "shifted", "exped", "inverted", "normed", "turned", "turned_kept"))
        mixed, mixed_kept = sem("mixed", FT), sem("mixed_kept", FT)
        out_summed, added = sem("out_summed", 1), sem("added", 1)

        block = ctx.enter_context(nc.Block())

        def each_pass(eng, before, batch):
            before(1, -1)
            with eng.Fori(1, PASSES) as g:
                batch(g, 0, False)
                batch(g, 1, False)
            batch(PASSES, 0, False)
            batch(PASSES, 1, True)

        def all_loaded(g, u):
            return (g + (u + 1) // 2) * LOADS * 16

        def fill_at(unit):
            return ORDER.index(unit)

        @block.sync
        def _(sp):
            open_loop(sp, loop_sems)

            def load(g, u, last=False):
                if last:
                    return
                b, s = 2 * (g - 1) + u + 1, (u + 1) % 2
                index = bass.ds(b, 1) if not isinstance(b, int) else slice(b, b + 1)

                def tiles(a, at_index=index):
                    return a[at_index, :, :].rearrange("o (t p) n -> p (o t) n", p=P)

                sp.wait_ge(added, at(g, 2, u - 1))
                sp.wait_ge(biased, at(g, 2, u - 1))
                sp.dma_start(xs[s][:, :, :], tiles(x)).then_inc(loaded[s], 16)
                sp.wait_ge(masked, at(g, 2 * STEPS, u * STEPS - 1))
                sp.dma_start(mk[s][:, :, :], tiles(mask, index if mask_batches > 1 else slice(0, 1))).then_inc(loaded[s], 16)
                if CROSS:
                    sp.wait_ge(filled, at(g, 16, u * 8 - 1))
                    sp.dma_start(cs[s][:, :, :], tiles(cT)).then_inc(loaded[s], 16)

            load(1, -1)
            for t, src in ((wk, wk_d), (wq, wq_d), (wv, wv_d), (wo, wo_d)):
                sp.dma_start(t[:, :, :], src.rearrange("(t p) n -> p t n", p=P)).then_inc(w_loaded, 16)
            sp.dma_start(ln_sb[:, :, :], ln_cols).then_inc(w_loaded, 16)
            sp.dma_start(qk_sb[:, :, :], qk_cols).then_inc(w_loaded, 16)
            for i, row in enumerate(rows):
                sp.dma_start(rows_sb[:, i, :], row.to_broadcast([P, FEAT])).then_inc(w_loaded, 16)
            W_DONE = 16 * 8

            each_pass(sp, lambda g, u: None, load)

        W_DONE = 16 * 8

        @block.gpsimd
        def _(pool):
            make_identity(pool, ident, ident_made)
            pool.memset(half_power[:, :], -0.5).then_inc(const_made, 1)
            pool.wait_ge(w_loaded, W_DONE)
            pool.wait_ge(const_made, 1)

            def prepare(g, u):
                pool.wait_ge(counted, at(g, 8, (u + 1) * 4 + 3))
                pool.wait_ge(normalised, at(g, 2, u))
                pool.tensor_tensor(rstd[:, :], var_eps[:, :], half_power[:, :], ALU.pow).then_inc(powered, 1)

            def batch(g, u, last):
                if not last:
                    prepare(g, u)
                for n in range(STEPS):
                    pool.wait_ge(masked_mul, at(g, 2 * STEPS, u * STEPS + n))
                    ins = pool.tensor_tensor(pr[n % RING][:, :, :, :].rearrange("p h t k -> p h (t k)"),
                                             pr[n % RING][:, :, :, :].rearrange("p h t k -> p h (t k)"),
                                             ma[u][:, :, :].rearrange("p t k -> p (t k)").unsqueeze(1).to_broadcast([P, 2, TT * TOK]),
                                             ALU.add)
                    ins.then_inc(masked, 1)
                    if n == 3:
                        pool.wait_ge(added, at(g, 2, u - 1))
                        pool.tensor_tensor(xb[:, :, :], xs[u][:, :, :], rows_sb[:, 1, :].unsqueeze(1).to_broadcast([P, TT, FEAT]),
                                           ALU.add).then_inc(biased, 1)

            each_pass(pool, prepare, batch)

        @block.tensor
        def _(pe):
            pe.wait_ge(ident_made, 2)
            pe.wait_ge(w_loaded, W_DONE)

            def fill(g, u, unit):
                s, i = (u + 1) % 2, fill_at(unit)
                base = (u + 1) * 8
                pe.wait_ge(fill_kept, at(g, 16, base + i - 1))
                src = cs[s] if CROSS and unit[0] in "KV" else lnT
                if unit[0] == "T":
                    if unit == "T0":
                        pe.wait_ge(normalised, at(g, 2, u + 1))
                    for j in range(2):
                        f = 2 * int(unit[1]) + j
                        for m in range(TT):
                            mm = pe.transpose(ps_p[:, j, m * P:(m + 1) * P], xn[:, m, f * P:(f + 1) * P], ident[:, :])
                else:
                    if src is lnT:
                        pe.wait_ge(fill_kept, at(g, 16, base + fill_at("T1")))
                    else:
                        pe.wait_ge(loaded[(u + 1) % 2], all_loaded(g, u))
                    if unit[0] == "V":
                        m = int(unit[1])
                        for t in range(FT):
                            mm = pe.matmul(ps_p[:, :, :], src[:, t, m * P:(m + 1) * P], wv[:, t, :],
                                           start=(t == 0), stop=(t == FT - 1))
                    else:
                        w = wq if unit[0] == "Q" else wk
                        for j in range(2):
                            f = 2 * int(unit[1]) + j
                            for t in range(FT):
                                mm = pe.matmul(ps_p[:, j, :], w[:, t, f * P:(f + 1) * P], src[:, t, :],
                                               start=(t == 0), stop=(t == FT - 1))
                mm.then_inc(filled, 1)

            def before(g, u):
                for unit in ORDER:
                    fill(g, u, unit)

            def batch(g, u, last):
                e = u * STEPS
                for n in range(LAST):
                    if n < STEPS:
                        if n == 0:
                            pe.wait_ge(fill_kept, at(g, 16, u * 8 + 7))
                        pe.wait_ge(masked_mul, at(g, 2 * STEPS, e + n - 2))
                        for i in range(2):
                            h = 2 * n + i
                            r = slice(h % TILE_HEADS * DH, (h % TILE_HEADS + 1) * DH)
                            for m in range(TT):
                                mm = pe.matmul(ps_s[n % 2][:, i, m, :], qT[u][r, h // TILE_HEADS, m * P:(m + 1) * P],
                                               kT[u][r, h // TILE_HEADS, :], start=True, stop=True)
                        mm.then_inc(scored, 1)
                    if n in FILL and not last:
                        fill(g, u, FILL[n])
                    if 0 <= n - TURN_LAG < STEPS:
                        k = n - TURN_LAG
                        pe.wait_ge(normed, at(g, 2 * STEPS, e + k))
                        pe.wait_ge(turned_kept, at(g, 2 * STEPS, e + k - 1))
                        if k == 0:
                            pe.wait_ge(added, at(g, 2, u - 1))
                        for i in range(2):
                            for t in range(TT):
                                for m in range(TT):
                                    mm = pe.transpose(ps_t[:, i, t, m * P:(m + 1) * P],
                                                      pr[k % RING][:, i, m, t * P:(t + 1) * P], ident[:, :])
                        mm.then_inc(turned, 1)
                    if n >= MIX_LAG:
                        k = n - MIX_LAG
                        pe.wait_ge(turned_kept, at(g, 2 * STEPS, e + k))
                        if k % 2 == 0:
                            pe.wait_ge(mixed_kept, at(g, 2 * FT, u * FT + k // 2 - 1))
                        for i in range(2):
                            h = 2 * k + i
                            r = slice(h % TILE_HEADS * DH, (h % TILE_HEADS + 1) * DH)
                            for t in range(TT):
                                mm = pe.matmul(ps_o[r, :], v[u][:, t, h * DH:(h + 1) * DH], pT[k % 2][:, i, t, :],
                                               start=(t == 0), stop=(t == TT - 1))
                        if k % 2 == 1:
                            mm.then_inc(mixed, 1)
                pe.wait_ge(mixed_kept, at(g, 2 * FT, u * FT + FT - 1))
                for m in range(TT):
                    for t in range(FT):
                        mm = pe.matmul(ps_t[:, m, :, :], ctxT[:, t, m * P:(m + 1) * P], wo[:, t, :],
                                       start=(t == 0), stop=(t == FT - 1))
                mm.then_inc(out_summed, 1)

            each_pass(pe, before, batch)

        @block.scalar
        def _(act):
            act.wait_ge(w_loaded, W_DONE)

            def keep_fill(g, u, unit):
                if unit[0] == "V":
                    return
                s, i = (u + 1) % 2, fill_at(unit)
                act.wait_ge(filled, at(g, 16, (u + 1) * 8 + i))
                for j in range(2):
                    f = 2 * int(unit[1]) + j
                    if unit[0] == "T":
                        ins = act.activation(lnT[:, f, :], ps_p[:, j, :], ACT.Identity, bias=ln_sb[:, 1, f:f + 1],
                                             scale=ln_sb[:, 0, f:f + 1])
                    else:
                        ins = act.activation((qT if unit[0] == "Q" else kT)[s][:, f, :], ps_p[:, j, :], ACT.Identity,
                                             bias=qk_sb[:, "QK".index(unit[0]), f:f + 1])
                ins.then_inc(fill_kept, 1)

            def before(g, u):
                for unit in ORDER:
                    keep_fill(g, u, unit)

            def batch(g, u, last):
                e = u * STEPS
                for n in range(LAST):
                    if 1 <= n <= STEPS:
                        k = n - 1
                        act.wait_ge(shifted, at(g, 2 * STEPS, e + k))
                        act.wait_ge(inverted, at(g, 2 * STEPS, e + k - RING))
                        for i in range(2):
                            for m in range(TT):
                                tile = pr[k % RING][:, i, m, :]
                                ins = act.activation(tile, tile, ACT.Exp, bias=shift[k % RING][:, i, m:m + 1],
                                                     accum_out=mass[k % RING][:, i, m:m + 1])
                        ins.then_inc(exped, 1)
                    if n in FILL and not last:
                        keep_fill(g, u, FILL[n])
                    if 0 <= n - TURN_LAG < STEPS:
                        k = n - TURN_LAG
                        act.wait_ge(turned, at(g, 2 * STEPS, e + k))
                        if k >= 2 and k % 2 == 1:
                            pass
                        act.wait_ge(mixed, at(g, 2 * FT, u * FT + (k - 2) // 2))
                        act.activation(pT[k % 2][:, :, :, :], ps_t[:, :, :, :], ACT.Copy).then_inc(turned_kept, 1)
                    if n >= MIX_LAG and (n - MIX_LAG) % 2 == 1:
                        f = (n - MIX_LAG) // 2
                        act.wait_ge(mixed, at(g, 2 * FT, u * FT + f))
                        if f == 0:
                            act.wait_ge(out_summed, at(g, 2, u - 1))
                        act.activation(ctxT[:, f, :], ps_o[:, :], ACT.Copy).then_inc(mixed_kept, 1)
                b = 2 * (g - 1) + u
                act.wait_ge(added, at(g, 2, u))
                act.dma_start(out[bass.ds(b, 1) if not isinstance(b, int) else slice(b, b + 1), :, :]
                              .rearrange("o (t p) n -> p (o t) n", p=P), res[:, :, :]).then_inc(stored, 16)

            each_pass(act, before, batch)
            act.wait_ge(stored, 16 * (BATCH + 2))

        @block.vector
        def _(dve):
            dve.wait_ge(w_loaded, W_DONE)

            def statistics(g, u):
                s = (u + 1) % 2
                dve.wait_ge(loaded[(u + 1) % 2], all_loaded(g, u))
                for m in range(TT):
                    ins = dve.bn_stats(stats[:, m, :], xs[s][:, m, :])
                ins.then_inc(counted, 1)
                dve.wait_ge(masked, at(g, 2 * STEPS, u * STEPS - 1))
                dve.tensor_scalar(ma[s][:, :, :], mk[s][:, :, :], 1e4, -1e4, ALU.mult, ALU.add).then_inc(mask_split, 1)
                dve.wait_ge(counted, at(g, 8, (u + 1) * 4))
                dve.wait_ge(mask_split, at(g, 4, (u + 1) * 2))
                dve.tensor_scalar(mk[s][:, :, :], mk[s][:, :, :], SCALE, None, ALU.mult).then_inc(mask_split, 1)
                for m in range(TT):
                    ins = dve.bn_aggr(moments[:, m, :], stats[:, m, :])
                ins.then_inc(counted, 1)
                dve.wait_ge(counted, at(g, 8, (u + 1) * 4 + 1))
                dve.wait_ge(powered, at(g, 2, u))
                dve.tensor_scalar(var_eps[:, :], moments[:, :, 1], 1e-5, None, ALU.add).then_inc(counted, 2)

            def normalise(g, u):
                s = (u + 1) % 2
                dve.wait_ge(powered, at(g, 2, u + 1))
                dve.wait_ge(filled, at(g, 16, u * 8 + fill_at("T1")))
                for m in range(TT):
                    ins = dve.tensor_scalar(xn[:, m, :], xs[s][:, m, :], moments[:, m, 0:1], rstd[:, m:m + 1],
                                            ALU.subtract, ALU.mult)
                ins.then_inc(normalised, 1)

            def keep_values(g, u, unit):
                i, m = fill_at(unit), int(unit[1])
                dve.wait_ge(filled, at(g, 16, (u + 1) * 8 + i))
                dve.tensor_tensor(v[(u + 1) % 2][:, m, :], ps_p[:, :, :].rearrange("p a b -> p (a b)"), rows_sb[:, 0, :],
                                  ALU.add).then_inc(fill_kept, 1)

            def before(g, u):
                statistics(g, u)
                normalise(g, u)
                keep_values(g, u, "V0")
                keep_values(g, u, "V1")

            def batch(g, u, last):
                e = u * STEPS
                dve.wait_ge(mask_split, at(g, 4, u * 2 + 1))
                if not last:
                    statistics(g, u)
                for n in range(LAST):
                    if 0 <= n - TURN_LAG < STEPS:
                        k = n - TURN_LAG
                        dve.wait_ge(exped, at(g, 2 * STEPS, e + k))
                        dve.reciprocal(inv[k % RING][:, :, :], mass[k % RING][:, :, :]).then_inc(inverted, 1)
                        dve.wait_ge(inverted, at(g, 2 * STEPS, e + k))
                        for i in range(2):
                            for m in range(TT):
                                tile = pr[k % RING][:, i, m, :]
                                ins = dve.tensor_scalar(tile, tile, inv[k % RING][:, i, m:m + 1], None, ALU.mult)
                        ins.then_inc(normed, 1)
                    if n < STEPS:
                        dve.wait_ge(scored, at(g, 2 * STEPS, e + n))
                        dve.wait_ge(turned, at(g, 2 * STEPS, e + n - RING))
                        dve.tensor_tensor(pr[n % RING][:, :, :, :].rearrange("p h t k -> p h (t k)"),
                                          ps_s[n % 2][:, :, :, :].rearrange("p h t k -> p h (t k)"),
                                          mk[u][:, :, :].rearrange("p t k -> p (t k)").unsqueeze(1).to_broadcast([P, 2, TT * TOK]),
                                          ALU.mult).then_inc(masked_mul, 1)
                    if n == 0 and not last:
                        normalise(g, u)
                    if 1 <= n <= STEPS:
                        k = n - 1
                        dve.wait_ge(masked, at(g, 2 * STEPS, e + k))
                        dve.wait_ge(exped, at(g, 2 * STEPS, e + k - RING))
                        dve.tensor_reduce(shift[k % RING][:, :, :], pr[k % RING][:, :, :, :], AXIS.X, ALU.max,
                                          negate=True).then_inc(shifted, 1)
                    if n in FILL and not last and FILL[n][0] == "V":
                        keep_values(g, u, FILL[n])
                dve.wait_ge(out_summed, at(g, 2, u))
                dve.wait_ge(biased, at(g, 2, u))
                dve.wait_ge(stored, at(g, 2, u - 1, 16))
                dve.tensor_tensor(res[:, :, :], ps_t[:, :, :, :].rearrange("p m a b -> p m (a b)"), xb[:, :, :],
                                  ALU.add).then_inc(added, 1)

            each_pass(dve, before, batch)


def token_mlp(nc, semaphores, x, w1_d, w2_d, ln_cols, b1, b2, out):
    HID = 4 * FEAT
    CHUNKS = HID // (2 * P)
    RING = 4
    PASSES = BATCH // 2
    Y_LAG = 2
    TURN_STEPS = (4, 6)
    with ExitStack() as ctx:
        def sb(name, shape):
            return ctx.enter_context(nc.sbuf_tensor("mlp_" + name, shape, F32))

        def ps(name, shape):
            return ctx.enter_context(nc.psum_tensor("mlp_" + name, shape, F32))

        loop_sems = []

        def sem(name, per_batch=0):
            s = semaphores.allocate("mlp_" + name)
            if per_batch:
                loop_sems.append((s, 2 * per_batch))
            return s

        w1, w2 = sb("w1", [P, FT, HID]), sb("w2", [P, 2 * CHUNKS, FEAT])
        ln_sb, b1_sb, b2_row = sb("ln_cols", [P, 2, FT]), sb("b1", [P, 2 * CHUNKS]), sb("b2", [P, FEAT])
        ident, half_power = sb("ident", [P, P]), sb("half_power", [P, TT])
        xs = [sb(f"xs{u}", [P, TT, FEAT]) for u in range(2)]
        stats, moments, var_eps, rstd = sb("stats", [P, TT, 6]), sb("moments", [P, TT, 2]), sb("var_eps", [P, TT]), sb("rstd", [P, TT])
        xn = sb("xn", [P, TT, FEAT])
        lnT = [sb(f"lnT{u}", [P, FT, TOK]) for u in range(2)]
        pre, cube, hid = ([sb(f"{n}{i}", [P, 2, TOK]) for i in range(RING)] for n in ("pre", "cube", "hid"))
        xb, res = sb("xb", [P, TT, FEAT]), sb("res", [P, TT, FEAT])

        ps_h = [ps(f"ps_h{i}", [P, 2, TOK]) for i in range(2)]
        ps_y = ps("ps_y", [P, TT, FEAT])
        ps_t = [ps(f"ps_t{i}", [P, 2, TOK]) for i in range(2)]

        w1_loaded, w2_loaded, cols_loaded, ident_made, const_made = (sem(n) for n in ("w1_loaded", "w2_loaded", "cols_loaded", "ident_made", "const_made"))
        loaded, stored = [sem(f"loaded{u}") for u in range(2)], sem("stored", 16)
        counted, powered, normalised, biased = sem("counted", 4), sem("powered", 1), sem("normalised", 1), sem("biased", 1)
        turned, turned_kept = sem("turned", 2), sem("turned_kept", 2)
        h_summed, h_kept, squared, squared1, cubed, bent, gelled = (
            sem(n, CHUNKS) for n in ("h_summed", "h_kept", "squared", "squared1", "cubed", "bent", "gelled"))
        y_used, added = sem("y_used", CHUNKS), sem("added", 1)

        block = ctx.enter_context(nc.Block())

        def each_pass(eng, before, batch):
            before(1, -1)
            with eng.Fori(1, PASSES) as g:
                batch(g, 0, False)
                batch(g, 1, False)
            batch(PASSES, 0, False)
            batch(PASSES, 1, True)

        def rows_of(a, b):
            index = bass.ds(b, 1) if not isinstance(b, int) else slice(b, b + 1)
            return a[index, :, :].rearrange("o (t p) n -> p (o t) n", p=P)

        @block.sync
        def _(sp):
            open_loop(sp, loop_sems)

            def load(g, u, last=False):
                if last:
                    return
                sp.wait_ge(added, at(g, 2, u - 1))
                sp.wait_ge(biased, at(g, 2, u - 1))
                sp.dma_start(xs[(u + 1) % 2][:, :, :], rows_of(x, 2 * (g - 1) + u + 1)).then_inc(loaded[(u + 1) % 2], 16)

            load(1, -1)
            sp.dma_start(ln_sb[:, :, :], ln_cols).then_inc(cols_loaded, 16)
            sp.dma_start(b1_sb[:, :], b1).then_inc(cols_loaded, 16)
            sp.dma_start(b2_row[:, :], b2.to_broadcast([P, FEAT])).then_inc(cols_loaded, 16)
            for t in range(FT):
                sp.dma_start(w1[:, t, :], w1_d[t * P:(t + 1) * P, :]).then_inc(w1_loaded, 16)
            sp.dma_start(w2[:, :, :], w2_d.rearrange("(t p) n -> p t n", p=P)).then_inc(w2_loaded, 16)
            each_pass(sp, lambda g, u: None, load)

        @block.gpsimd
        def _(pool):
            make_identity(pool, ident, ident_made)
            pool.memset(half_power[:, :], -0.5).then_inc(const_made, 1)
            pool.wait_ge(cols_loaded, 48)
            pool.wait_ge(const_made, 1)

            def prepare(g, u):
                pool.wait_ge(counted, at(g, 8, (u + 1) * 4 + 3))
                pool.wait_ge(normalised, at(g, 2, u))
                pool.tensor_tensor(rstd[:, :], var_eps[:, :], half_power[:, :], ALU.pow).then_inc(powered, 1)

            def batch(g, u, last):
                e = u * CHUNKS
                for n in range(CHUNKS):
                    if n == 1:
                        pool.wait_ge(added, at(g, 2, u - 1))
                        pool.tensor_tensor(xb[:, :, :], xs[u][:, :, :], b2_row[:, :].unsqueeze(1).to_broadcast([P, TT, FEAT]),
                                           ALU.add).then_inc(biased, 1)
                    pool.wait_ge(squared1, at(g, 2 * CHUNKS, e + n))
                    pool.tensor_tensor(cube[n % RING][:, :, :], cube[n % RING][:, :, :], pre[n % RING][:, :, :],
                                       ALU.mult).then_inc(cubed, 1)
                    if n == 2 and not last:
                        prepare(g, u)

            each_pass(pool, prepare, batch)

        @block.tensor
        def _(pe):
            pe.wait_ge(ident_made, 2)

            def turn(g, u, i):
                pe.wait_ge(turned_kept, at(g, 4, u * 2 + i))
                pe.wait_ge(normalised, at(g, 2, u + 1))
                for j in range(2):
                    f = 2 * i + j
                    for m in range(TT):
                        mm = pe.transpose(ps_t[i][:, j, m * P:(m + 1) * P], xn[:, m, f * P:(f + 1) * P], ident[:, :])
                mm.then_inc(turned, 1)

            def before(g, u):
                turn(g, u, 0)
                turn(g, u, 1)
                pe.wait_ge(w1_loaded, 16 * FT)

            def batch(g, u, last):
                e = u * CHUNKS
                pe.wait_ge(turned_kept, at(g, 4, u * 2 + 1))
                for n in range(CHUNKS + Y_LAG):
                    if n < CHUNKS:
                        pe.wait_ge(squared, at(g, 2 * CHUNKS, e + n - 2))
                        for j in range(2):
                            f = 2 * n + j
                            for t in range(FT):
                                mm = pe.matmul(ps_h[n % 2][:, j, :], w1[:, t, f * P:(f + 1) * P], lnT[u][:, t, :],
                                               start=(t == 0), stop=(t == FT - 1))
                        mm.then_inc(h_summed, 1)
                    if n in TURN_STEPS and not last:
                        turn(g, u, TURN_STEPS.index(n))
                    if n >= Y_LAG:
                        k = n - Y_LAG
                        pe.wait_ge(gelled, at(g, 2 * CHUNKS, e + k))
                        if k == 0:
                            pe.wait_ge(added, at(g, 2, u - 1))
                            pe.wait_ge(w2_loaded, 16)
                        for j in range(2):
                            f = 2 * k + j
                            for m in range(TT):
                                mm = pe.matmul(ps_y[:, m, :], hid[k % RING][:, j, m * P:(m + 1) * P], w2[:, f, :],
                                               start=(f == 0), stop=(f == 2 * CHUNKS - 1))
                        mm.then_inc(y_used, 1)

            each_pass(pe, before, batch)

        @block.scalar
        def _(act):
            act.wait_ge(cols_loaded, 48)

            def keep_turned(g, u, i):
                act.wait_ge(turned, at(g, 4, (u + 1) * 2 + i))
                for j in range(2):
                    f = 2 * i + j
                    ins = act.activation(lnT[(u + 1) % 2][:, f, :], ps_t[i][:, j, :], ACT.Identity, bias=ln_sb[:, 1, f:f + 1],
                                         scale=ln_sb[:, 0, f:f + 1])
                ins.then_inc(turned_kept, 1)

            def before(g, u):
                keep_turned(g, u, 0)
                keep_turned(g, u, 1)

            def batch(g, u, last):
                e = u * CHUNKS
                for n in range(CHUNKS + 1):
                    if n < CHUNKS:
                        act.wait_ge(h_summed, at(g, 2 * CHUNKS, e + n))
                        act.wait_ge(gelled, at(g, 2 * CHUNKS, e + n - RING))
                        for j in range(2):
                            ins = act.activation(pre[n % RING][:, j, :], ps_h[n % 2][:, j, :], ACT.Identity,
                                                 bias=b1_sb[:, 2 * n + j:2 * n + j + 1])
                        ins.then_inc(h_kept, 1)
                        for j in range(2):
                            ins = act.activation(cube[n % RING][:, j, :], ps_h[n % 2][:, j, :], ACT.Square,
                                                 bias=b1_sb[:, 2 * n + j:2 * n + j + 1])
                        ins.then_inc(squared, 1)
                    if n >= 1:
                        k = n - 1
                        act.wait_ge(cubed, at(g, 2 * CHUNKS, e + k))
                        act.activation(cube[k % RING][:, :, :], cube[k % RING][:, :, :], ACT.Tanh,
                                       scale=0.7978845608028654).then_inc(bent, 1)
                    if n in TURN_STEPS and not last:
                        keep_turned(g, u, TURN_STEPS.index(n))
                act.wait_ge(added, at(g, 2, u))
                act.dma_start(rows_of(out, 2 * (g - 1) + u), res[:, :, :]).then_inc(stored, 16)

            each_pass(act, before, batch)
            act.wait_ge(stored, 16 * (BATCH + 2))

        @block.vector
        def _(dve):
            def statistics(g, u):
                s = (u + 1) % 2
                dve.wait_ge(loaded[s], (g + (u + 1) // 2) * 16)
                for m in range(TT):
                    ins = dve.bn_stats(stats[:, m, :], xs[s][:, m, :])
                ins.then_inc(counted, 1)

            def moment(g, u):
                dve.wait_ge(counted, at(g, 8, (u + 1) * 4))
                dve.tensor_copy(var_eps[:, :], stats[:, :, 2]).then_inc(counted, 1)
                for m in range(TT):
                    ins = dve.bn_aggr(moments[:, m, :], stats[:, m, :])
                ins.then_inc(counted, 1)
                dve.wait_ge(counted, at(g, 8, (u + 1) * 4 + 2))
                dve.tensor_scalar(var_eps[:, :], moments[:, :, 1], 1e-5, None, ALU.add).then_inc(counted, 1)

            def normalise(g, u):
                s = (u + 1) % 2
                dve.wait_ge(powered, at(g, 2, u + 1))
                dve.wait_ge(turned, at(g, 4, u * 2 + 1))
                for m in range(TT):
                    ins = dve.tensor_scalar(xn[:, m, :], xs[s][:, m, :], moments[:, m, 0:1], rstd[:, m:m + 1],
                                            ALU.subtract, ALU.mult)
                ins.then_inc(normalised, 1)

            def before(g, u):
                statistics(g, u)
                moment(g, u)
                normalise(g, u)

            def batch(g, u, last):
                e = u * CHUNKS
                for n in range(CHUNKS + 1):
                    if n < CHUNKS:
                        dve.wait_ge(squared, at(g, 2 * CHUNKS, e + n))
                        dve.tensor_scalar(cube[n % RING][:, :, :], cube[n % RING][:, :, :], 0.044715, 1.0, ALU.mult,
                                          ALU.add).then_inc(squared1, 1)
                    if n >= 1:
                        k = n - 1
                        dve.wait_ge(bent, at(g, 2 * CHUNKS, e + k))
                        dve.wait_ge(y_used, at(g, 2 * CHUNKS, e + k - RING))
                        dve.scalar_tensor_tensor(out=hid[k % RING][:, :, :], in0=cube[k % RING][:, :, :], scalar=1.0,
                                                 in1=pre[k % RING][:, :, :], op0=ALU.add, op1=ALU.mult).then_inc(gelled, 1)
                    if n == 1 and not last:
                        statistics(g, u)
                    if n == 2 and not last:
                        moment(g, u)
                    if n == 3 and not last:
                        normalise(g, u)
                dve.wait_ge(y_used, at(g, 2 * CHUNKS, e + CHUNKS - 1))
                dve.wait_ge(biased, at(g, 2, u))
                dve.wait_ge(stored, at(g, 2, u - 1, 16))
                dve.scalar_tensor_tensor(out=res[:, :, :], in0=ps_y[:, :, :], scalar=0.5, in1=xb[:, :, :],
                                         op0=ALU.mult, op1=ALU.add).then_inc(added, 1)

            each_pass(dve, before, batch)


def recurrent_block(nc, semaphores, x, state, w, cols, maa_w1, maa_w2, td_w1, td_w2, select, spread, head_sum, group_mean, out):
    GROUP = 16
    MIX = 32
    DECAY = td_w1.shape[1]
    WEIGHTS = ("r", "k", "v", "g", "o", "fk", "fr", "fv")
    A_UNITS = ("T0", "T1", "XX", "Mw0", "Mw1", "Mk0", "Mk1", "D1", "K0", "D20", "D21", "K1", "Mv0", "Mv1", "V0", "V1",
               "Mr0", "Mr1", "R0", "R1", "Mg0", "Mg1", "G0", "G1")
    Z_UNITS = ("C0", "C1", "E0", "E1", "Q0", "Q1", "O0", "O1", "T0", "T1", "FK0", "FK1", "FR0", "FR1", "FV0", "FV1")
    MIXED = "wkvrg"
    NA, NZ = len(A_UNITS), len(Z_UNITS)
    SCHEDULE = (
        "A:LS A:LN A:T0 A:T1", "Z:E0 Z:E1 A:SX", "A:XX Z:Q0 Z:Q1 A:Mw0 A:Mw1", "A:Mk0 A:Mk1 A:D1 Z:N1",
        "A:K0 A:D20 A:D21 Z:N2", "A:K1 A:Mv0 A:Mv1 Z:N3", "Z:O0 A:V0 Z:O1", "Z:LS A:V1 Z:LN",
        "A:Mr0 Z:T0 A:Mr1 Z:T1", "A:R0 Z:X", "A:R1 Z:FK0", "Z:FK1 A:Mg0 A:Mg1", "Z:FR0 A:G0", "Z:FR1", "C:P A:G1 Z:FV0",
        "Z:FV1 C:C0 C:C1")
    STEPS = GROUP
    with ExitStack() as ctx:
        def sb(name, shape):
            return ctx.enter_context(nc.sbuf_tensor("rec_" + name, shape, F32))

        def ps(name, shape):
            return ctx.enter_context(nc.psum_tensor("rec_" + name, shape, F32))

        loop_sems = []

        def sem(name, per_batch=0):
            s = semaphores.allocate("rec_" + name)
            if per_batch:
                loop_sems.append((s, 2 * per_batch))
            return s

        def of(b, per_batch, k, unit=1):
            return at(b + 2, per_batch, k, unit)

        wt = {n: sb("w_" + n, [P, FT, FEAT]) for n in WEIGHTS}
        m1 = sb("m1", [P, FT, 5 * MIX])
        m2a, m2b = sb("m2a", [P, FEAT]), sb("m2b", [MIX, FEAT])
        t1, t2 = sb("t1", [P, FT, DECAY]), sb("t2", [DECAY, FEAT])
        sel, spr, ones = sb("sel", [P, GROUP, P]), sb("spr", [P, (2 * GROUP - 1) * (P // GROUP)]), sb("ones", [P, P])
        mean_of = sb("mean_of", [P, P])
        NC = 16
        col = sb("cols", [P, NC, FT])
        LN1_W, LN1_B, LN2_W, LN2_B, MAA_X, DECAY0, U, GN_W, GN_B, FFN_K, FFN_R, STACK = range(12)
        ident, half_power = sb("ident", [P, P]), sb("half_power", [P, TT])

        xin, xn = sb("xin", [P, TT, FEAT]), sb("xn", [P, TT, FEAT])
        stats, moments, var_eps, rstd = ([sb(f"{n}{i}", sh) for i in "az"] for n, sh in
                                         (("stats", [P, TT, 6]), ("moments", [P, TT, 2]), ("var_eps", [P, TT]), ("rstd", [P, TT])))
        st = [sb(f"st{u}", [P, FT, 2 + GROUP]) for u in range(2)]
        edge = sb("edge", [P, FT, 2])
        xaT, sx = sb("xaT", [P, FT, TOK + 1]), sb("sx", [P, FT, TOK])
        xm = [sb(f"xm{i}", [P, FT, TOK]) for i in range(2)]
        xxT, xx4, tdT = sb("xxT", [P, TOK]), sb("xx4", [MIX, TOK]), sb("tdT", [DECAY, TOK])
        rT, kT, vT, g2 = ([sb(f"{n}{u}", [P, FT, TOK]) for u in range(2)] for n in ("rT", "kT", "vT", "g2"))
        wE = [sb(f"wE{u}", [P, FT, TOK + 1]) for u in range(2)]
        kvE = [sb(f"kvE{i}", [P, FT, TOK + 1]) for i in range(2)]
        sE = [sb(f"sE{i}", [P, FT, TOK + 1]) for i in range(2)]
        rs = [sb(f"rs{i}", [P, FT, TOK]) for i in range(2)]
        og, sq = sb("og", [P, FT, TOK]), sb("sq", [P, FT, TOK])
        xres = sb("xres", [P, TT, FEAT])
        xcT, sx2, xk2, xr2 = sb("xcT", [P, FT, TOK + 1]), sb("sx2", [P, FT, TOK]), sb("xk2", [P, FT, TOK]), sb("xr2", [P, FT, TOK])
        kk, ruk = og, xr2
        sq_rows = sq[:, :, :].rearrange("p (m a) n -> p m (a n)", m=TT)

        ps_v = [ps(f"ps_v{i}", [P, FT, TOK]) for i in range(2)]
        ps_acc = ps("ps_acc", [P, FT, TOK])
        ps_a, ps_z = ps("ps_a", [P, 2, TOK]), ps("ps_z", [P, 2, TOK])

        w_loaded, ident_made, const_made = sem("w_loaded"), sem("ident_made"), sem("const_made")
        x_loaded, st_loaded, z_loaded, stored = sem("x_loaded"), sem("st_loaded"), sem("z_loaded"), sem("stored", 16)
        a_filled, a_kept, z_filled, z_kept = sem("a_filled", NA), sem("a_kept", NA), sem("z_filled", NZ), sem("z_kept", NZ)
        counted = [sem(f"counted_{i}", 4) for i in "az"]
        powered = [sem(f"powered_{i}", 1) for i in "az"]
        normalised = [sem(f"normalised_{i}", 1) for i in "az"]
        shifted, mixed_x, mixtures, decayed, g_bent = sem("shifted", 1), sem("mixed_x", 1), sem("mixtures", 5), sem("decayed", 1), sem("g_bent", 2)
        spread_v, kv_made, seeded, scanned, rs_made, summed = (
            sem(n, STEPS) for n in ("spread_v", "kv_made", "seeded", "scanned", "rs_made", "summed"))
        ruk_made, og_made = sem("ruk_made", 2), sem("og_made", 1)
        squared, inverted, rooted, og_scaled, og_affine, gated = (
            sem("squared", 2), sem("inverted", 2), sem("rooted", 1), sem("og_scaled", 1), sem("og_affine", 1), sem("gated", 1))
        shifted2, mixed2, kk_made, res_made = sem("shifted2", 1), sem("mixed2", 2), sem("kk_made", 1), sem("res_made", 2)
        W_LOADS = len(WEIGHTS) + 10

        block = ctx.enter_context(nc.Block())

        def run(eng, step, a_unit, z_unit, c_unit, body_end=None):
            names = " ".join(SCHEDULE).split()

            def body(b, s, with_z, with_a):
                for j in range(STEPS):
                    step(b, s, j)
                    for name in SCHEDULE[j].split():
                        stage, unit = name.split(":")
                        if stage == "A" and with_a:
                            a_unit(b + 1, 1 - s, unit)
                        elif stage == "Z" and with_z:
                            z_unit(b - 1, 1 - s, unit)
                        elif stage == "C":
                            c_unit(b, s, unit)
                step(b, s, STEPS)
                if body_end:
                    body_end(b, s)

            for name in names:
                if name.startswith("A:"):
                    a_unit(0, 0, name[2:])
            body(0, 0, False, True)
            with eng.Fori(1, BATCH // 2) as p:
                body(2 * p - 1, 1, True, True)
                body(2 * p, 0, True, True)
            body(BATCH - 1, 1, True, False)
            for name in names:
                if name.startswith("Z:"):
                    z_unit(BATCH - 1, 1, name[2:])

        def batch_of(a, b):
            return a[bass.ds(b, 1) if not isinstance(b, int) else slice(b, b + 1)]

        def token_rows(a, b):
            return batch_of(a, b).rearrange("o (t p) n -> p (o t) n", p=P)

        def feature_rows(a, b):
            return batch_of(a, b).rearrange("o p t n -> p (o t) n")

        def a_at(unit):
            return A_UNITS.index(unit)

        def z_at(unit):
            return Z_UNITS.index(unit)

        NOTHING = lambda *_: None

        @block.sync
        def _(sp):
            open_loop(sp, loop_sems)

            def load_x(b):
                sp.wait_ge(normalised[0], of(b - 1, 1, 0))
                sp.dma_start(xin[:, :, :], token_rows(x, b)).then_inc(x_loaded, 16)

            def load_st(b, s):
                sp.wait_ge(og_made, of(b - 2, 1, 0))
                sp.dma_start(st[s][:, :, :], feature_rows(state, b)).then_inc(st_loaded, 16)

            def load_z(b):
                sp.wait_ge(stored, of(b - 1, 1, 0, 16))
                sp.wait_ge(z_kept, of(b - 1, NZ, z_at("T0")))
                sp.dma_start(xres[:, :, :], token_rows(x, b)).then_inc(z_loaded, 16)
                sp.dma_start(edge[:, :, :], feature_rows(state, b)[:, :, 0:2]).then_inc(z_loaded, 16)

            def store(b):
                sp.wait_ge(res_made, of(b, 2, 1))
                sp.dma_start(token_rows(out, b), xres[:, :, :]).then_inc(stored, 16)

            load_x(0)
            load_st(0, 0)
            sp.dma_start(col[:, :, :], cols).then_inc(w_loaded, 16)
            sp.dma_start(m1[:, :, :], maa_w1.rearrange("(t p) n -> p t n", p=P)).then_inc(w_loaded, 16)
            sp.dma_start(m2a[:, :], maa_w2[0:P, :]).then_inc(w_loaded, 16)
            sp.dma_start(m2b[:, :], maa_w2[P:P + MIX, :]).then_inc(w_loaded, 16)
            sp.dma_start(t1[:, :, :], td_w1.rearrange("(t p) n -> p t n", p=P)).then_inc(w_loaded, 16)
            sp.dma_start(t2[:, :], td_w2).then_inc(w_loaded, 16)
            sp.dma_start(sel[:, :, :], select).then_inc(w_loaded, 16)
            sp.dma_start(spr[:, :], spread).then_inc(w_loaded, 16)
            sp.dma_start(ones[:, :], head_sum).then_inc(w_loaded, 16)
            sp.dma_start(mean_of[:, :], group_mean).then_inc(w_loaded, 16)
            for n in WEIGHTS:
                sp.dma_start(wt[n][:, :, :], w[n].rearrange("(t p) n -> p t n", p=P)).then_inc(w_loaded, 16)
            load_x(1)
            load_st(1, 1)
            load_x(2)
            load_st(2, 0)

            def body(b, s, ahead=True):
                load_z(b - 1)
                if ahead:
                    load_x(b + 2)
                store(b - 1)
                if ahead:
                    load_st(b + 2, s)

            for b in range(1, BATCH):
                body(b, b % 2, b + 2 < BATCH)
            load_z(BATCH - 1)
            store(BATCH - 1)
            sp.wait_ge(stored, 16 * (BATCH + 2))

        @block.gpsimd
        def _(pool):
            make_identity(pool, ident, ident_made)
            pool.memset(half_power[:, :], -0.5).then_inc(const_made, 1)
            pool.memset(wE[0][:, :, 0], 0.0).then_inc(const_made, 1)
            pool.memset(wE[1][:, :, 0], 0.0).then_inc(const_made, 1)
            pool.wait_ge(w_loaded, 16 * W_LOADS)
            pool.wait_ge(const_made, 3)

            def power(i, b):
                pool.wait_ge(counted[i], of(b, 4, 3))
                pool.wait_ge(normalised[i], of(b - 1, 1, 0))
                pool.tensor_tensor(rstd[i][:, :], var_eps[i][:, :], half_power[:, :], ALU.pow).then_inc(powered[i], 1)

            def a_unit(b, s, unit):
                if unit == "LS":
                    power(0, b)
                elif unit[0] == "M" and unit[2] == "1":
                    o = MIXED.index(unit[1])
                    pool.wait_ge(a_kept, of(b, NA, a_at(unit)))
                    pool.tensor_tensor(xm[(o + 1) % 2][:, :, :], xm[(o + 1) % 2][:, :, :], xaT[:, :, 1:TOK + 1],
                                       ALU.add).then_inc(mixtures, 1)

            def z_unit(b, s, unit):
                if unit == "N1":
                    pool.wait_ge(rooted, of(b, 1, 0))
                    pool.tensor_tensor(og[:, :, :], og[:, :, :], sq[:, :, :], ALU.mult).then_inc(og_scaled, 1)
                elif unit == "LS":
                    power(1, b)
                elif unit == "X":
                    pool.wait_ge(z_kept, of(b, NZ, z_at("T1")))
                    pool.wait_ge(mixed2, of(b - 1, 2, 1))
                    pool.tensor_tensor(sx2[:, :, :], xcT[:, :, 0:TOK], xcT[:, :, 1:TOK + 1], ALU.subtract).then_inc(shifted2, 1)
                elif unit == "FK1":
                    pool.wait_ge(z_kept, of(b, NZ, z_at("FK1")))
                    pool.tensor_tensor(kk[:, :, :], kk[:, :, :], kk[:, :, :], ALU.mult).then_inc(kk_made, 1)

            def c_unit(b, s, unit):
                if unit == "P":
                    pool.wait_ge(a_kept, of(b, NA, a_at("R1")))
                    pool.wait_ge(z_filled, of(b - 1, NZ, z_at("FR1")))
                    pool.tensor_tensor(ruk[:, :, :], rT[s][:, :, :], kT[s][:, :, :], ALU.mult).then_inc(ruk_made, 1)
                    pool.wait_ge(ruk_made, of(b, 2, 0))
                    pool.tensor_tensor(ruk[:, :, :], ruk[:, :, :], col[:, U, :].unsqueeze(2).to_broadcast([P, FT, TOK]),
                                       ALU.mult).then_inc(ruk_made, 1)

            def step(b, s, j):
                if j == STEPS:
                    return
                if j == 0:
                    pool.wait_ge(a_kept, of(b, NA, a_at("R1")))
                pool.wait_ge(scanned, of(b, STEPS, j))
                pool.wait_ge(summed, of(b, STEPS, j - 2))
                pool.tensor_tensor(rs[j % 2][:, :, :], sE[j % 2][:, :, 0:TOK], rT[s][:, :, :], ALU.mult).then_inc(rs_made, 1)

            run(pool, step, a_unit, z_unit, c_unit)

        @block.tensor
        def _(pe):
            pe.wait_ge(ident_made, 2)
            pe.wait_ge(w_loaded, 16 * W_LOADS)

            def transpose_rows(bank, rows, half):
                for j in range(2):
                    f = 2 * half + j
                    for m in range(TT):
                        mm = pe.transpose(bank[:, j, m * P:(m + 1) * P], rows[:, m, f * P:(f + 1) * P], ident[:, :])
                return mm

            def to_features(bank, weight, src, half):
                for j in range(2):
                    f = 2 * half + j
                    for t in range(FT):
                        mm = pe.matmul(bank[:, j, :], weight[:, t, f * P:(f + 1) * P], src[:, t, :],
                                       start=(t == 0), stop=(t == FT - 1))
                return mm

            def to_tokens(bank, weight, src, m):
                for t in range(FT):
                    mm = pe.matmul(bank[:, :, :], src[:, t, m * P:(m + 1) * P], weight[:, t, :],
                                   start=(t == 0), stop=(t == FT - 1))
                return mm

            def a_unit(b, s, unit):
                if unit in ("LS", "LN", "SX"):
                    return
                pe.wait_ge(a_kept, of(b, NA, a_at(unit) - 1))
                half = int(unit[-1]) if unit[-1] in "01" else 0
                if unit[0] == "T":
                    pe.wait_ge(normalised[0], of(b, 1, 0))
                    mm = transpose_rows(ps_a, xn, half)
                elif unit == "XX":
                    pe.wait_ge(mixed_x, of(b, 1, 0))
                    for j, rows in enumerate((P, MIX)):
                        for t in range(FT):
                            mm = pe.matmul(ps_a[0:rows, j, :], m1[:, t, j * P:j * P + rows], xm[0][:, t, :],
                                           start=(t == 0), stop=(t == FT - 1))
                elif unit[0] == "M":
                    f = "kwvrg".index(unit[1])
                    if unit == "Mw0":
                        pe.wait_ge(a_kept, of(b, NA, a_at("XX")))
                    r = slice(f * MIX, (f + 1) * MIX) if f < 4 else slice(0, MIX)
                    w2, xx = (m2a, xxT) if f < 4 else (m2b, xx4)
                    for j in range(2):
                        c = 2 * half + j
                        mm = pe.matmul(ps_a[:, j, :], w2[r, c * P:(c + 1) * P], xx[r, :], start=True, stop=True)
                elif unit == "D1":
                    pe.wait_ge(mixtures, of(b, 5, 0))
                    for t in range(FT):
                        mm = pe.matmul(ps_a[0:DECAY, 0, :], t1[:, t, :], xm[1][:, t, :], start=(t == 0), stop=(t == FT - 1))
                elif unit[:2] == "D2":
                    pe.wait_ge(a_kept, of(b, NA, a_at("D1")))
                    for j in range(2):
                        c = 2 * half + j
                        mm = pe.matmul(ps_a[:, j, :], t2[:, c * P:(c + 1) * P], tdT[:, :], start=True, stop=True)
                else:
                    o = MIXED.index(unit[0].lower())
                    pe.wait_ge(mixtures, of(b, 5, o))
                    mm = to_features(ps_a, wt[unit[0].lower()], xm[(o + 1) % 2], half)
                mm.then_inc(a_filled, 1)

            def z_unit(b, s, unit):
                if unit not in Z_UNITS:
                    return
                pe.wait_ge(z_kept, of(b, NZ, z_at(unit) - 1))
                half = int(unit[-1])
                if unit[0] == "E":
                    pe.wait_ge(og_made, of(b, 1, 0))
                    mm = pe.matmul(ps_z[:, :, :], mean_of[:, :], og[:, 2 * half:2 * half + 2, :], start=True, stop=True)
                elif unit[0] == "Q":
                    pe.wait_ge(squared, of(b, 2, half))
                    mm = pe.matmul(ps_z[:, :, :], mean_of[:, :], sq[:, 2 * half:2 * half + 2, :], start=True, stop=True)
                elif unit[0] == "O":
                    pe.wait_ge(gated, of(b, 1, 0))
                    mm = to_tokens(ps_z, wt["o"], og, half)
                elif unit[0] == "T":
                    pe.wait_ge(normalised[1], of(b, 1, 0))
                    mm = transpose_rows(ps_z, sq_rows, half)
                elif unit[:2] == "FK":
                    pe.wait_ge(mixed2, of(b, 2, 0))
                    mm = to_features(ps_z, wt["fk"], xk2, half)
                elif unit[:2] == "FR":
                    pe.wait_ge(mixed2, of(b, 2, 1))
                    mm = to_tokens(ps_z, wt["fr"], xr2, half)
                elif unit[:2] == "FV":
                    pe.wait_ge(kk_made, of(b, 1, 0))
                    mm = to_tokens(ps_z, wt["fv"], kk, half)
                mm.then_inc(z_filled, 1)

            def c_unit(b, s, unit):
                if unit == "P":
                    return
                half = int(unit[1])
                pe.wait_ge(z_kept, of(b - 1, NZ, NZ - 1) if half == 0 else of(b, NZ, 0))
                pe.wait_ge(ruk_made, of(b, 2, 1))
                pe.matmul(ps_z[:, :, :], ones[:, :], ruk[:, 2 * half:2 * half + 2, :], start=True, stop=True).then_inc(z_filled, 1)

            def step(b, s, j):
                if j >= 1:
                    pe.wait_ge(rs_made, of(b, STEPS, j - 1))
                    if j == 1:
                        pe.wait_ge(og_made, of(b - 1, 1, 0))
                    i = (GROUP - j) * (P // GROUP)
                    for half in range(2):
                        mm = pe.matmul(ps_acc[:, 2 * half:2 * half + 2, :], spr[:, i:i + P],
                                       rs[(j - 1) % 2][:, 2 * half:2 * half + 2, :], start=(j == 1), stop=(j == STEPS))
                    mm.then_inc(summed, 1)
                if j < STEPS:
                    if j == 0:
                        pe.wait_ge(a_kept, of(b, NA, a_at("V1")))
                    pe.wait_ge(kv_made, of(b, STEPS, j - 2))
                    for half in range(2):
                        mm = pe.matmul(ps_v[j % 2][:, 2 * half:2 * half + 2, :], sel[:, j, :], vT[s][:, 2 * half:2 * half + 2, :],
                                       start=True, stop=True)
                    mm.then_inc(spread_v, 1)

            run(pe, step, a_unit, z_unit, c_unit)

        @block.scalar
        def _(act):
            act.wait_ge(w_loaded, 16 * W_LOADS)

            def a_unit(b, s, unit):
                if unit in ("LS", "LN", "SX") or unit[0] == "M":
                    return
                half = int(unit[-1]) if unit[-1] in "01" else 0
                if unit == "T0":
                    act.wait_ge(og_made, of(b - 2, 1, 0))
                    act.wait_ge(mixtures, of(b - 1, 5, 4))
                elif unit == "T1":
                    act.wait_ge(st_loaded, (b + 1) * 16)
                    act.activation(xaT[:, :, 0], st[s][:, :, 1], ACT.Copy)
                act.wait_ge(a_filled, of(b, NA, a_at(unit)))
                if unit[0] == "T":
                    for j in range(2):
                        c = 2 * half + j
                        ins = act.activation(xaT[:, c, 1:TOK + 1], ps_a[:, j, :], ACT.Identity, bias=col[:, LN1_B, c:c + 1],
                                             scale=col[:, LN1_W, c:c + 1])
                elif unit == "XX":
                    act.activation(xxT[:, :], ps_a[:, 0, :], ACT.Tanh)
                    ins = act.activation(xx4[:, :], ps_a[0:MIX, 1, :], ACT.Tanh)
                elif unit == "D1":
                    ins = act.activation(tdT[:, :], ps_a[0:DECAY, 0, :], ACT.Tanh)
                elif unit[:2] == "D2":
                    for j in range(2):
                        c = 2 * half + j
                        ins = act.activation(wE[s][:, c, 1:TOK + 1], ps_a[:, j, :], ACT.Exp, bias=col[:, DECAY0, c:c + 1])
                elif unit[0] == "G":
                    if half == 0:
                        act.wait_ge(gated, of(b - 2, 1, 0))
                    act.activation(g2[s][:, 2 * half:2 * half + 2, :], ps_a[:, :, :], ACT.Tanh, scale=0.5).then_inc(g_bent, 1)
                    return
                else:
                    dst = {"R": rT, "K": kT, "V": vT}[unit[0]][s]
                    ins = act.activation(dst[:, 2 * half:2 * half + 2, :], ps_a[:, :, :], ACT.Copy)
                ins.then_inc(a_kept, 1)
                if unit == "D21":
                    act.wait_ge(a_kept, of(b, NA, a_at("D21")))
                    act.activation(wE[s][:, :, 1:TOK + 1], wE[s][:, :, 1:TOK + 1], ACT.Exp, scale=-1.0).then_inc(decayed, 1)

            def z_unit(b, s, unit):
                if unit[0] == "E":
                    half = int(unit[1])
                    act.wait_ge(z_kept, of(b, NZ, z_at(unit)))
                    act.wait_ge(res_made, of(b - 1, 2, 1))
                    act.activation(sq[:, 2 * half:2 * half + 2, :], og[:, 2 * half:2 * half + 2, :], ACT.Square).then_inc(squared, 1)
                elif unit == "N1":
                    act.wait_ge(inverted, of(b, 2, 1))
                    act.activation(sq[:, :, :], sq[:, :, :], ACT.Sqrt).then_inc(rooted, 1)
                elif unit == "N2":
                    act.wait_ge(og_scaled, of(b, 1, 0))
                    for c in range(FT):
                        ins = act.activation(og[:, c, :], og[:, c, :], ACT.Identity, bias=col[:, GN_B, c:c + 1],
                                             scale=col[:, GN_W, c:c + 1])
                    ins.then_inc(og_affine, 1)
                elif unit[0] == "T":
                    half = int(unit[1])
                    if half == 0:
                        act.wait_ge(mixed2, of(b - 1, 2, 1))
                        act.wait_ge(z_loaded, (b + 1) * 32)
                        act.activation(xcT[:, :, 0], edge[:, :, 0], ACT.Copy)
                    act.wait_ge(z_filled, of(b, NZ, z_at(unit)))
                    for j in range(2):
                        c = 2 * half + j
                        ins = act.activation(xcT[:, c, 1:TOK + 1], ps_z[:, j, :], ACT.Identity, bias=col[:, LN2_B, c:c + 1],
                                             scale=col[:, LN2_W, c:c + 1])
                    ins.then_inc(z_kept, 1)
                elif unit[:2] == "FK":
                    half = int(unit[2])
                    act.wait_ge(z_filled, of(b, NZ, z_at(unit)))
                    act.activation(kk[:, 2 * half:2 * half + 2, :], ps_z[:, :, :], ACT.Relu).then_inc(z_kept, 1)
                elif unit[:2] == "FR":
                    m = int(unit[2])
                    act.wait_ge(z_filled, of(b, NZ, z_at(unit)))
                    act.activation(sq_rows[:, m, :], ps_z[:, :, :].rearrange("p a n -> p (a n)"), ACT.Tanh, scale=0.5).then_inc(z_kept, 1)

            def step(b, s, j):
                if j < STEPS:
                    act.wait_ge(scanned, of(b, STEPS, j - 2))
                    act.activation(kvE[j % 2][:, :, 0], st[s][:, :, 2 + j], ACT.Copy).then_inc(seeded, 1)

            run(act, step, a_unit, z_unit, NOTHING)

        @block.vector
        def _(dve):
            dve.wait_ge(w_loaded, 16 * W_LOADS)
            dve.wait_ge(const_made, 3)

            def statistics(i, b, rows):
                for m in range(TT):
                    ins = dve.bn_stats(stats[i][:, m, :], rows[:, m, :])
                ins.then_inc(counted[i], 1)
                dve.wait_ge(counted[i], of(b, 4, 0))
                dve.tensor_copy(var_eps[i][:, :], stats[i][:, :, 2]).then_inc(counted[i], 1)
                for m in range(TT):
                    ins = dve.bn_aggr(moments[i][:, m, :], stats[i][:, m, :])
                ins.then_inc(counted[i], 1)
                dve.wait_ge(counted[i], of(b, 4, 2))
                dve.tensor_scalar(var_eps[i][:, :], moments[i][:, :, 1], 1e-5, None, ALU.add).then_inc(counted[i], 1)

            def normalise(i, b, dst, rows):
                dve.wait_ge(powered[i], of(b, 1, 0))
                for m in range(TT):
                    ins = dve.tensor_scalar(dst[:, m, :], rows[:, m, :], moments[i][:, m, 0:1], rstd[i][:, m:m + 1],
                                            ALU.subtract, ALU.mult)
                ins.then_inc(normalised[i], 1)

            def a_unit(b, s, unit):
                if unit == "LS":
                    dve.wait_ge(x_loaded, (b + 1) * 16)
                    statistics(0, b, xin)
                elif unit == "LN":
                    dve.wait_ge(a_filled, of(b - 1, NA, a_at("T1")))
                    normalise(0, b, xn, xin)
                elif unit == "SX":
                    dve.wait_ge(a_kept, of(b, NA, a_at("T1")))
                    dve.tensor_tensor(sx[:, :, :], xaT[:, :, 0:TOK], xaT[:, :, 1:TOK + 1], ALU.subtract).then_inc(shifted, 1)
                    dve.wait_ge(shifted, of(b, 1, 0))
                    dve.wait_ge(a_filled, of(b - 1, NA, a_at("R1")))
                    for c in range(FT):
                        ins = dve.scalar_tensor_tensor(out=xm[0][:, c, :], in0=sx[:, c, :], scalar=col[:, MAA_X, c:c + 1],
                                                       in1=xaT[:, c, 1:TOK + 1], op0=ALU.mult, op1=ALU.add)
                    ins.then_inc(mixed_x, 1)
                elif unit[0] == "M":
                    half, o, f = int(unit[2]), MIXED.index(unit[1]), "kwvrg".index(unit[1])
                    dve.wait_ge(a_filled, of(b, NA, a_at(unit)))
                    if half == 0:
                        reader = (a_at("G1") - NA, a_at("XX"), a_at("D1"), a_at("K1"), a_at("V1"))[o]
                        dve.wait_ge(a_filled, of(b, NA, reader))
                    for j in range(2):
                        c = 2 * half + j
                        ins = dve.scalar_tensor_tensor(out=xm[(o + 1) % 2][:, c, :], in0=ps_a[:, j, :],
                                                       scalar=col[:, STACK + f, c:c + 1], in1=sx[:, c, :],
                                                       op0=ALU.add, op1=ALU.mult)
                    ins.then_inc(a_kept, 1)
                elif unit[0] == "G":
                    half = int(unit[1])
                    dve.wait_ge(g_bent, of(b, 2, half))
                    tile = g2[s][:, 2 * half:2 * half + 2, :]
                    dve.scalar_tensor_tensor(out=tile, in0=tile, scalar=1.0, in1=ps_a[:, :, :], op0=ALU.add,
                                             op1=ALU.mult).then_inc(a_kept, 1)

            def z_unit(b, s, unit):
                half = int(unit[-1]) if unit[-1] in "01" else 0
                here = slice(2 * half, 2 * half + 2)
                if unit in Z_UNITS and unit[0] != "T" and unit[:2] not in ("FK", "FR"):
                    dve.wait_ge(z_filled, of(b, NZ, z_at(unit)))
                if unit[0] == "E":
                    dve.tensor_tensor(og[:, here, :], og[:, here, :], ps_z[:, :, :], ALU.subtract).then_inc(z_kept, 1)
                elif unit[0] == "Q":
                    dve.tensor_scalar(sq[:, here, :], ps_z[:, :, :], 1e-5, None, ALU.add).then_inc(z_kept, 1)
                    dve.wait_ge(z_kept, of(b, NZ, z_at(unit)))
                    dve.reciprocal(sq[:, here, :], sq[:, here, :]).then_inc(inverted, 1)
                elif unit == "N3":
                    dve.wait_ge(og_affine, of(b, 1, 0))
                    dve.wait_ge(a_kept, of(b, NA, a_at("G1")))
                    dve.scalar_tensor_tensor(out=og[:, :, :], in0=og[:, :, :], scalar=0.5, in1=g2[s][:, :, :], op0=ALU.mult,
                                             op1=ALU.mult).then_inc(gated, 1)
                elif unit[0] == "O":
                    if half == 0:
                        dve.wait_ge(z_loaded, (b + 1) * 32)
                    dve.tensor_tensor(xres[:, half, :], ps_z[:, :, :].rearrange("p a n -> p (a n)"), xres[:, half, :],
                                      ALU.add).then_inc(z_kept, 1)
                elif unit == "LS":
                    dve.wait_ge(z_kept, of(b, NZ, z_at("O1")))
                    statistics(1, b, xres)
                elif unit == "LN":
                    normalise(1, b, sq_rows, xres)
                elif unit == "X":
                    dve.wait_ge(shifted2, of(b, 1, 0))
                    for dst, which in ((xk2, FFN_K), (xr2, FFN_R)):
                        for c in range(FT):
                            ins = dve.scalar_tensor_tensor(out=dst[:, c, :], in0=sx2[:, c, :], scalar=col[:, which, c:c + 1],
                                                           in1=xcT[:, c, 1:TOK + 1], op0=ALU.mult, op1=ALU.add)
                        ins.then_inc(mixed2, 1)
                elif unit[:2] == "FV":
                    row = sq_rows[:, half, :]
                    dve.scalar_tensor_tensor(out=row, in0=row, scalar=1.0, in1=ps_z[:, :, :].rearrange("p a n -> p (a n)"),
                                             op0=ALU.add, op1=ALU.mult).then_inc(z_kept, 1)
                    dve.wait_ge(z_kept, of(b, NZ, z_at(unit)))
                    dve.scalar_tensor_tensor(out=xres[:, half, :], in0=row, scalar=0.5, in1=xres[:, half, :], op0=ALU.mult,
                                             op1=ALU.add).then_inc(res_made, 1)

            def c_unit(b, s, unit):
                if unit == "P":
                    return
                half = int(unit[1])
                here = slice(2 * half, 2 * half + 2)
                dve.wait_ge(z_filled, of(b, NZ, half))
                dve.tensor_tensor(og[:, here, :], ps_z[:, :, :], vT[s][:, here, :], ALU.mult).then_inc(z_kept, 1)

            def step(b, s, j):
                if j < STEPS:
                    dve.wait_ge(spread_v, of(b, STEPS, j))
                    if j == 0:
                        dve.wait_ge(a_kept, of(b, NA, a_at("K1")))
                        dve.wait_ge(decayed, of(b, 1, 0))
                    dve.tensor_tensor(kvE[j % 2][:, :, 1:TOK + 1], ps_v[j % 2][:, :, :], kT[s][:, :, :], ALU.mult).then_inc(kv_made, 1)
                    dve.wait_ge(seeded, of(b, STEPS, j))
                    dve.wait_ge(kv_made, of(b, STEPS, j))
                    dve.wait_ge(rs_made, of(b, STEPS, j - 2))
                    dve.tensor_tensor_scan(sE[j % 2][:, :, :].rearrange("p c t -> p (c t)"),
                                           wE[s][:, :, :].rearrange("p c t -> p (c t)"),
                                           kvE[j % 2][:, :, :].rearrange("p c t -> p (c t)"), 0.0, ALU.mult, ALU.add
                                           ).then_inc(scanned, 1)
                else:
                    dve.wait_ge(summed, of(b, STEPS, STEPS - 1))
                    dve.wait_ge(z_kept, of(b, NZ, 1))
                    dve.tensor_tensor(og[:, :, :], ps_acc[:, :, :], og[:, :, :], ALU.add).then_inc(og_made, 1)

            run(dve, step, a_unit, z_unit, c_unit)


def build(nc, semaphores, ap, out):
    def between(name):
        return nc.dram_tensor(name, (BATCH, TOK, FEAT), F32, kind="Internal").ap()

    x1, x2, x3, x4, x5 = (between(f"x{i}") for i in range(1, 6))
    context_attention(nc, semaphores, ap["x"], ap["xT"], ap["cT"], ap["L0_xattn_w_q"], ap["L0_xattn_w_k"], ap["L0_xattn_w_v"],
                      ap["L0_w_oT"], ap["L0_xattn_alpha"], x1)
    semaphores.clear()
    channel_attention(nc, semaphores, x1, ap["c"], *(ap["L1_" + n] for n in ("Wqkv0T", "Winj0T", "Wqkv1T", "Winj1T", "WoT", "bo", "q_bias")), x2)
    semaphores.clear()
    w = ap["L2_xattn_w_qkv"]
    token_attention(nc, semaphores, "self", x2, None, ap["mask_self"], 1, ap["L2_ln1"], w[:, 0:FEAT], w[:, FEAT:2 * FEAT],
                    w[:, 2 * FEAT:3 * FEAT], ap["L2_xattn_w_ao"], ap["L2_qk1"], (ap["L2_bv1"], ap["L2_bo1"]), x3)
    semaphores.clear()
    w = ap["L2_xattn_w_kv"]
    token_attention(nc, semaphores, "cross", x3, ap["cT"], ap["mask_cross"], BATCH, ap["L2_ln2"], ap["L2_xattn_w_q"], w[:, 0:FEAT],
                    w[:, FEAT:2 * FEAT], ap["L2_xattn_w_co"], ap["L2_qk2"], (ap["L2_bv2"], ap["L2_bo2"]), x4)
    semaphores.clear()
    token_mlp(nc, semaphores, x4, ap["L2_xattn_w1"], ap["L2_xattn_w2"], ap["L2_ln3"], ap["L2_b1"], ap["L2_b2"], x5)
    semaphores.clear()
    weights = {n: ap[f"L3_W{n}T"] for n in ("r", "k", "v", "g", "o", "fk", "fr", "fv")}
    recurrent_block(nc, semaphores, x5, ap["L3_state"], weights, *(ap["L3_" + n] for n in
                    ("cols", "maa_w1", "maa_w2", "td_w1", "td_w2", "select", "spread", "head_sum", "group_mean")), out)


def lay_out(np, a):
    out = {}

    def put(name, array):
        out[name] = np.ascontiguousarray(array)

    put("x", a["x"])
    put("c", a["ctx_2048"])
    put("cT", a["ctx_2048"].transpose(0, 2, 1))
    if "L0_xattn_w_q" in a:
        put("xT", a["x"].transpose(0, 2, 1))
        for n in ("w_q", "w_k", "w_v"):
            put("L0_xattn_" + n, a["L0_xattn_" + n])
        put("L0_w_oT", a["L0_xattn_w_o"].T)
        put("L0_xattn_alpha", a["L0_xattn_alpha"].reshape(1, 1))
    if "L2_xattn_w_ao" in a:
        def col(v):
            return v.reshape(-1, P).T

        d = {n[len("L2_xattn_"):]: v for n, v in a.items() if n.startswith("L2_xattn_")}
        put("mask_self", a["mask_1x1xSxS2_fc1"][:, 0])
        put("mask_cross", a["mask_Bx1xSxS2_ff1"][:, 0])
        for n in ("w_qkv", "w_ao", "w_q", "w_kv", "w_co", "w1", "w2"):
            put("L2_xattn_" + n, d[n])
        for n in ("ln1", "ln2", "ln3"):
            put("L2_" + n, np.stack([col(d[n + "_s"]), col(d[n + "_b"])], 1))
        put("L2_qk1", np.stack([col(d["b_qkv"][:FEAT]), col(d["b_qkv"][FEAT:2 * FEAT])], 1))
        put("L2_qk2", np.stack([col(d["b_q"]), col(d["b_kv"][:FEAT])], 1))
        put("L2_bv1", d["b_qkv"][2 * FEAT:].reshape(1, FEAT))
        put("L2_bv2", d["b_kv"][FEAT:].reshape(1, FEAT))
        put("L2_bo1", d["b_ao"].reshape(1, FEAT))
        put("L2_bo2", d["b_co"].reshape(1, FEAT))
        put("L2_b1", col(d["b1"]))
        put("L2_b2", d["b2"].reshape(1, FEAT))
    if "L1_xattn_Wo" in a:
        for n in ("Wqkv0", "Winj0", "Wqkv1", "Winj1", "Wo"):
            put("L1_" + n + "T", a["L1_xattn_" + n].T)
        put("L1_bo", a["L1_xattn_bo"].reshape(TT, P).T)
        put("L1_q_bias", a["L1_xattn_r_w_bias"].reshape(-1, P).T)
    if "L3_xattn_Wr" in a:
        d = {n[len("L3_xattn_"):]: v for n, v in a.items() if n.startswith("L3_xattn_")}
        group, heads = 16, P // 16
        by_feature = np.arange(FEAT).reshape(FT, heads, group).transpose(0, 2, 1).reshape(-1)
        for n in ("Wr", "Wk", "Wfk", "Wfr", "Wfv"):
            put("L3_" + n + "T", d[n].T)
        for n in ("Wv", "Wg"):
            put("L3_" + n + "T", d[n].T[:, by_feature])
        put("L3_WoT", d["Wo"].T[by_feature])
        for n in ("maa_w1", "td_w1", "td_w2"):
            put("L3_" + n, d[n])
        put("L3_maa_w2", d["maa_w2"].reshape(-1, FEAT))
        vectors = [d[n].reshape(-1) for n in ("ln1_w", "ln1_b", "ln2_w", "ln2_b", "maa_x", "time_decay", "u")]
        vectors += [d[n][by_feature] for n in ("gn_w", "gn_b")]
        vectors += [d[n] for n in ("ffn_maa_k", "ffn_maa_r")] + list(d["maa_stack"][0])
        put("L3_cols", np.stack([v.reshape(-1, P).T for v in vectors], 1))
        c = a["ctx_2048"]
        edges = c[:, 0:2].transpose(0, 2, 1).reshape(BATCH, FT, P, 2)
        first = c[:, 2:2 + group].reshape(BATCH, FT, P, group)
        put("L3_state", np.concatenate([edges, first], 3).transpose(0, 2, 1, 3))
        p, m = np.arange(P)[:, None], np.arange(P)[None, :]
        put("L3_head_sum", (p // group == m % heads).astype(np.float32))
        put("L3_group_mean", ((p % heads == m % heads) / group).astype(np.float32))
        put("L3_select", np.stack([(p // heads == j) & (p % heads == m // group) for j in range(group)], 1).astype(np.float32))
        window = np.arange((2 * group - 1) * heads)[None, :]
        put("L3_spread", ((window // heads == group - 1) & (window % heads == p // group)).astype(np.float32))
    return out


def kernel(**inputs):
    import numpy as _np
    import concourse.bacc as _bacc
    from concourse import mybir as _mybir
    from concourse.bass_utils import run_bass_kernel_spmd as _run

    arrays = lay_out(_np, {n: _np.asarray(a) for n, a in inputs.items()})
    nc = _bacc.Bacc("TRN2", target_bir_lowering=False, num_devices=1)
    ap = {n: nc.dram_tensor("in_" + n, a.shape, _mybir.dt.from_np(a.dtype), kind="ExternalInput").ap()
          for n, a in arrays.items()}
    out = nc.dram_tensor("out", (BATCH, TOK, FEAT), _mybir.dt.float32, kind="ExternalOutput").ap()
    build(nc, Semaphores(nc), ap, out)
    r = _run(nc, [{"in_" + n: a for n, a in arrays.items()}], core_ids=[0])
    return r.results[0]["out"]
```

```python
from contextlib import ExitStack

import concourse.bass as bass
from concourse import mybir

P = 128
ALU = mybir.AluOpType
ACT = mybir.ActivationFunctionType
AXIS = mybir.AxisListType
F32 = mybir.dt.float32
F32R = mybir.dt.float32r

BATCH, TOK, FEAT = 8, 256, 512
TT, FT = TOK // P, FEAT // P


class Semaphores:

    def __init__(self, nc):
        self.nc, self.taken = nc, []

    def allocate(self, name):
        self.taken.append(self.nc.alloc_semaphore(name=name))
        return self.taken[-1]

    def clear(self):
        self.nc.clear_and_free_semaphores(self.taken)
        self.taken = []
        self.nc.all_engine_barrier()


def at(g, per_pass, k, unit=1):
    return (g * per_pass + k + 1) * unit


def open_loop(eng, sems):
    for s, count in sems:
        eng.sem_inc(s, count)


def make_identity(pool, ident, sem):
    pool.memset(ident[:, :], 0.0).then_inc(sem, 1)
    pool.wait_ge(sem, 1)
    pool.affine_select(out=ident[:, :], in_=ident[:, :], compare_op=ALU.not_equal, fill=1.0, base=0,
                       pattern=[[-1, P]], channel_multiplier=1).then_inc(sem, 1)


def context_attention(nc, semaphores, x, xT, cT, w_q, w_k, w_v, w_oT, alpha, x1):
    PAIRS = BATCH // 2
    SCALE = float(FEAT) ** -0.5
    ALL = slice(None)
    with ExitStack() as ctx:
        def sb(name, shape, dtype=F32):
            return ctx.enter_context(nc.sbuf_tensor("l0_" + name, shape, dtype))

        def parts(name, shape):
            return [sb(f"{name}_{part}", shape, F32R) for part in ("hi", "lo")]

        def ps(name, shape):
            return ctx.enter_context(nc.psum_tensor("l0_" + name, shape, F32))

        loop_sems = []

        def sem(name, credit=0):
            s = semaphores.allocate("l0_" + name)
            if credit:
                loop_sems.append((s, credit))
            return s

        def slots(name, credit=1):
            return [sem(f"{name}{u}", credit) for u in range(2)]

        wq, wk, wv, wo = (sb(n, [P, FT, FEAT]) for n in ("wq", "wk", "wv", "wo"))
        qk, vo = parts("qk", [P, FT, FEAT]), parts("vo", [P, FT, FEAT])
        ident = sb("ident", [P, P])
        alpha_col = sb("alpha_col", [P, 1])
        xt = [sb(f"xt{u}", [P, FT, TOK]) for u in range(2)]
        ct = [sb(f"ct{u}", [P, FT, TOK]) for u in range(2)]
        xn = [sb(f"xn{u}", [P, TT, FEAT]) for u in range(2)]
        xs, cs, yt = ([parts(f"{n}{u}", [P, FT, TOK]) for u in range(2)] for n in ("xs", "cs", "yt"))
        cv = [parts(f"cv{u}", [P, TT, FEAT]) for u in range(2)]
        pr = [sb(f"pr{u}", [P, TT, TOK]) for u in range(2)]
        prT = [parts(f"prT{u}", [P, TT, TOK]) for u in range(2)]
        res = [sb(f"res{u}", [P, TT, FEAT]) for u in range(2)]
        top = [sb(f"top{u}", [P, TT]) for u in range(2)]
        shift = [sb(f"shift{u}", [P, TT]) for u in range(2)]
        mass = [sb(f"mass{u}", [P, TT]) for u in range(2)]
        gain = [sb(f"gain{u}", [P, TT]) for u in range(2)]

        ps_y = ps("ps_y", [P, FT, TOK])
        ps_cv = ps("ps_cv", [P, TT, FEAT])
        ps_s = ps("ps_s", [P, TT, TOK])
        ps_t = ps("ps_t", [P, TT, TOK])
        ps_d = ps("ps_d", [P, TT, FEAT])

        ident_made, w_loaded, alpha_loaded = sem("ident_made"), sem("w_loaded"), sem("alpha_loaded")
        wv_loaded = sem("wv_loaded")
        w_summed, w_hi_kept, w_kept = sem("w_summed"), sem("w_hi_kept"), sem("w_kept")
        loaded, xn_loaded = slots("loaded", 32), slots("xn_loaded", 16)
        rounded, split = slots("rounded", 2), slots("split", 2)
        y_hi_kept, cv_hi_kept, prT_hi_kept = slots("y_hi_kept"), slots("cv_hi_kept"), slots("prT_hi_kept")
        stored = slots("stored", 16)
        y_summed = slots("y_summed")
        y_kept = slots("y_kept")
        cv_summed = slots("cv_summed")
        cv_kept = slots("cv_kept")
        scored = slots("scored")
        shifted = slots("shifted")
        probs_made = slots("probs_made")
        turned = slots("turned")
        turned_kept = slots("turned_kept")
        gained = slots("gained")
        delta_summed = slots("delta_summed")
        added = slots("added")
        inverted, topped = slots("inverted"), slots("topped")

        block = ctx.enter_context(nc.Block())

        def product(pe, out, terms):
            for i, (a, b) in enumerate(terms):
                pe.matmul(out, a[1], b[0], start=(i == 0), stop=False)
                pe.matmul(out, a[0], b[1], start=False, stop=False)
                mm = pe.matmul(out, a[0], b[0], start=False, stop=(i == len(terms) - 1))
            return mm

        def cut(tensors, *index):
            return [t[index] for t in tensors]

        def w_bank(m):
            return ps_y[:, 2 * m:2 * m + 2, :].rearrange("p a b -> p (a b)") if m < 2 else ps_cv[:, m - 2, :]

        @block.sync
        def _(sp):
            open_loop(sp, loop_sems)
            for w, src in ((wq, w_q), (wk, w_k)):
                sp.dma_start(w[:, :, :], src.rearrange("(t p) n -> p t n", p=P)).then_inc(w_loaded, 16)
            for w, src in ((wv, w_v), (wo, w_oT)):
                sp.dma_start(w[:, :, :], src.rearrange("(t p) n -> p t n", p=P)).then_inc(wv_loaded, 16)
            sp.dma_start(alpha_col[:, :], alpha.to_broadcast([P, 1])).then_inc(alpha_loaded, 16)

            def rows(a, g, u):
                b = 2 * g - 2 + u
                index = slice(b, b + 1) if isinstance(b, int) else bass.ds(b, 1)
                return a[index, :, :].rearrange("o (t p) n -> p (o t) n", p=P)

            def load(g):
                for u in range(2):
                    sp.wait_ge(split[u], at(g, 2, -1))
                    sp.dma_start(xt[u][:, :, :], rows(xT, g, u)).then_inc(loaded[u], 16)
                    sp.dma_start(ct[u][:, :, :], rows(cT, g, u)).then_inc(loaded[u], 16)

            def load_xn(g, u):
                sp.wait_ge(added[u], g)
                sp.dma_start(xn[u][:, :, :], rows(x, g, u)).then_inc(xn_loaded[u], 16)

            def store(g, u):
                sp.wait_ge(added[u], g + 1)
                sp.dma_start(rows(x1, g, u), res[u][:, :, :]).then_inc(stored[u], 16)

            load(1)
            for u in range(2):
                load_xn(1, u)
            with sp.Fori(2, PAIRS + 1) as g:
                load(g)
                for u in range(2):
                    store(g - 1, u)
                    load_xn(g, u)
            for u in range(2):
                store(PAIRS, u)
            for u in range(2):
                sp.wait_ge(stored[u], 16 * (PAIRS + 1))

        @block.gpsimd
        def _(pool):
            make_identity(pool, ident, ident_made)
            with pool.Fori(1, PAIRS + 1) as g:
                for u in range(2):
                    for i, (raw, (hi, lo)) in enumerate(((xt[u], xs[u]), (ct[u], cs[u]))):
                        pool.wait_ge(rounded[u], at(g, 2, i))
                        pool.tensor_tensor(lo[:, :, :], raw[:, :, :], hi[:, :, :].bitcast(F32), ALU.subtract).then_inc(split[u], 1)

        @block.tensor
        def _(pe):
            pe.wait_ge(w_loaded, 32)
            for k, (a, b) in enumerate(((wq, wk), (wv, wo))):
                if k == 1:
                    pe.wait_ge(wv_loaded, 32)
                for m in range(FT):
                    if k == 1:
                        pe.wait_ge(w_kept, m + 1)
                    for t in range(FT):
                        mm = pe.matmul(w_bank(m), a[:, t, m * P:(m + 1) * P], b[:, t, :], start=(t == 0), stop=(t == FT - 1))
                    mm.then_inc(w_summed, 1)
            pe.wait_ge(w_kept, 2 * FT)
            pe.wait_ge(ident_made, 2)
            with pe.Fori(1, PAIRS + 1) as g:
                def project_queries(u):
                    pe.wait_ge(split[u], at(g, 2, 0))
                    if u == 1:
                        pe.wait_ge(y_kept[0], g + 1)
                    for m in range(FT):
                        mm = product(pe, ps_y[:, m, :], [(cut(qk, ALL, t, slice(m * P, (m + 1) * P)), cut(xs[u], ALL, t, ALL))
                                                         for t in range(FT)])
                    mm.then_inc(y_summed[u], 1)

                def project_values(u):
                    pe.wait_ge(split[u], at(g, 2, 1))
                    if u == 1:
                        pe.wait_ge(cv_kept[0], g + 1)
                    for m in range(TT):
                        mm = product(pe, ps_cv[:, m, :], [(cut(cs[u], ALL, t, slice(m * P, (m + 1) * P)), cut(vo, ALL, t, ALL))
                                                          for t in range(FT)])
                    mm.then_inc(cv_summed[u], 1)

                def score(u):
                    pe.wait_ge(y_kept[u], g + 1)
                    if u == 1:
                        pe.wait_ge(probs_made[0], g + 1)
                    for m in range(TT):
                        mm = product(pe, ps_s[:, m, :], [(cut(yt[u], ALL, t, slice(m * P, (m + 1) * P)), cut(cs[u], ALL, t, ALL))
                                                         for t in range(FT)])
                    mm.then_inc(scored[u], 1)

                def turn(u):
                    pe.wait_ge(probs_made[u], g + 1)
                    if u == 1:
                        pe.wait_ge(turned_kept[0], g + 1)
                    for m in range(TT):
                        for t in range(TT):
                            mm = pe.transpose(ps_t[:, t, m * P:(m + 1) * P], pr[u][:, m, t * P:(t + 1) * P], ident[:, :])
                    mm.then_inc(turned[u], 1)

                def mix(u):
                    pe.wait_ge(turned_kept[u], g + 1)
                    pe.wait_ge(cv_kept[u], g + 1)
                    if u == 1:
                        pe.wait_ge(added[0], g + 1)
                    else:
                        pe.wait_ge(added[1], g)
                    for m in range(TT):
                        mm = product(pe, ps_d[:, m, :], [(cut(prT[u], ALL, t, slice(m * P, (m + 1) * P)), cut(cv[u], ALL, t, ALL))
                                                         for t in range(TT)])
                    mm.then_inc(delta_summed[u], 1)

                project_queries(0)
                project_values(0)
                project_queries(1)
                score(0)
                project_values(1)
                turn(0)
                score(1)
                mix(0)
                turn(1)
                mix(1)

        @block.scalar
        def _(act):
            for k, (hi, _) in enumerate((qk, vo)):
                for m in range(FT):
                    act.wait_ge(w_summed, FT * k + m + 1)
                    act.activation(hi[:, m, :], w_bank(m), ACT.Copy).then_inc(w_hi_kept, 1)
            with act.Fori(1, PAIRS + 1) as g:
                def round_inputs(u):
                    act.wait_ge(loaded[u], 32 * g + 32)
                    act.wait_ge(scored[u], g)
                    act.activation(xs[u][0][:, :, :], xt[u][:, :, :], ACT.Copy).then_inc(rounded[u], 1)
                    act.activation(cs[u][0][:, :, :], ct[u][:, :, :], ACT.Copy).then_inc(rounded[u], 1)

                def keep_queries(u):
                    act.wait_ge(y_summed[u], g + 1)
                    act.activation(yt[u][0][:, :, :], ps_y[:, :, :], ACT.Copy).then_inc(y_hi_kept[u], 1)

                def exponentials(u):
                    act.wait_ge(shifted[u], g + 1)
                    act.wait_ge(turned[u], g)
                    act.wait_ge(gained[u], g)
                    for m in range(TT):
                        ins = act.activation(pr[u][:, m, :], ps_s[:, m, :], ACT.Exp, bias=shift[u][:, m:m + 1],
                                             scale=SCALE, accum_out=mass[u][:, m:m + 1])
                    ins.then_inc(probs_made[u], 1)

                round_inputs(0)
                round_inputs(1)
                keep_queries(0)
                keep_queries(1)
                exponentials(0)
                exponentials(1)

        @block.vector
        def _(dve):
            dve.wait_ge(alpha_loaded, 16)
            for k, (hi, lo) in enumerate((qk, vo)):
                for m in range(FT):
                    dve.wait_ge(w_hi_kept, FT * k + m + 1)
                    dve.tensor_tensor(lo[:, m, :], w_bank(m), hi[:, m, :].bitcast(F32), ALU.subtract).then_inc(w_kept, 1)
            with dve.Fori(1, PAIRS + 1) as g:
                def keep_values(u):
                    dve.wait_ge(cv_summed[u], g + 1)
                    dve.tensor_copy(cv[u][0][:, :, :], ps_cv[:, :, :]).then_inc(cv_hi_kept[u], 1)
                    dve.wait_ge(cv_hi_kept[u], g + 1)
                    dve.tensor_tensor(cv[u][1][:, :, :], ps_cv[:, :, :], cv[u][0][:, :, :].bitcast(F32),
                                      ALU.subtract).then_inc(cv_kept[u], 1)

                def keep_queries(u):
                    dve.wait_ge(y_hi_kept[u], g + 1)
                    dve.tensor_tensor(yt[u][1][:, :, :], ps_y[:, :, :], yt[u][0][:, :, :].bitcast(F32),
                                      ALU.subtract).then_inc(y_kept[u], 1)

                def row_max(u):
                    dve.wait_ge(scored[u], g + 1)
                    dve.wait_ge(probs_made[u], g)
                    dve.tensor_reduce(top[u][:, :], ps_s[:, :, :], AXIS.X, ALU.max, negate=True).then_inc(topped[u], 1)
                    dve.wait_ge(topped[u], g + 1)
                    dve.tensor_scalar(shift[u][:, :], top[u][:, :], SCALE, None, ALU.mult).then_inc(shifted[u], 1)

                def keep_turned(u):
                    dve.wait_ge(turned[u], g + 1)
                    dve.wait_ge(probs_made[u], g + 1)
                    dve.tensor_copy(prT[u][0][:, :, :], ps_t[:, :, :]).then_inc(prT_hi_kept[u], 1)
                    dve.wait_ge(prT_hi_kept[u], g + 1)
                    dve.tensor_tensor(prT[u][1][:, :, :], ps_t[:, :, :], prT[u][0][:, :, :].bitcast(F32),
                                      ALU.subtract).then_inc(turned_kept[u], 1)
                    dve.reciprocal(gain[u][:, :], mass[u][:, :]).then_inc(inverted[u], 1)
                    dve.wait_ge(inverted[u], g + 1)
                    dve.tensor_scalar(gain[u][:, :], gain[u][:, :], alpha_col[:, 0:1], None, ALU.mult).then_inc(gained[u], 1)

                def add(u):
                    dve.wait_ge(delta_summed[u], g + 1)
                    dve.wait_ge(gained[u], g + 1)
                    dve.wait_ge(xn_loaded[u], 16 * g + 16)
                    dve.wait_ge(stored[u], 16 * g)
                    for m in range(TT):
                        ins = dve.scalar_tensor_tensor(out=res[u][:, m, :], in0=ps_d[:, m, :], scalar=gain[u][:, m:m + 1],
                                                       in1=xn[u][:, m, :], op0=ALU.mult, op1=ALU.add)
                    ins.then_inc(added[u], 1)

                keep_queries(0)
                keep_values(0)
                keep_queries(1)
                row_max(0)
                keep_values(1)
                keep_turned(0)
                row_max(1)
                add(0)
                keep_turned(1)
                add(1)


def channel_attention(nc, semaphores, z, c, w_qkv0T, w_inj0T, w_qkv1T, w_inj1T, w_oT, bo, q_bias, out):
    HEADS, DH = 16, 64
    INNER = HEADS * DH
    HP = HEADS // 2
    QT = FEAT // P
    STEPS = 2 * HEADS
    TILES = 2 * STEPS
    PROJECT_AHEAD = 2
    TURN_LAG, MIX_LAG = 2, 3
    OUTPUT_FROM = STEPS - 5
    SCALE = DH ** -0.5
    CT = TOK // P
    with ExitStack() as ctx:
        def sb(name, shape, dtype=F32):
            return ctx.enter_context(nc.sbuf_tensor("l1_" + name, shape, dtype))

        def ps(name, shape):
            return ctx.enter_context(nc.psum_tensor("l1_" + name, shape, F32))

        loop_sems = []

        def sem(name, credit=0):
            s = semaphores.allocate("l1_" + name)
            if credit:
                loop_sems.append((s, credit))
            return s

        w = [sb(f"w{i}", [P, CT, 3 * INNER]) for i in range(4)]
        wo_hi, wo_lo = sb("wo_hi", [P, HP, TOK], F32R), sb("wo_lo", [P, HP, TOK], F32R)
        ident, mean_of = sb("ident", [P, P]), sb("mean_of", [P, P])
        one = sb("one", [P, 1])
        bo_col, qb_col = sb("bo_col", [P, CT]), sb("qb_col", [P, HP])
        zt, ut, zres = sb("zt", [P, CT, FEAT]), sb("ut", [P, CT, FEAT]), sb("zres", [P, CT, FEAT])
        q = [sb(f"q{i}", [P, 2, FEAT], F32R) for i in range(2)]
        k = [sb(f"k{i}", [P, 2, FEAT], F32R) for i in range(2)]
        k_lo = [sb(f"k_lo{i}", [P, FEAT], F32R) for i in range(2)]
        vo = sb("vo", [P, HEADS, QT, 2 * DH], F32R)
        pr = sb("pr", [P, TURN_LAG + 1, 2, FEAT])
        p_hi = [sb(f"p_hi{i}", [P, QT, 2 * P], F32R) for i in range(2)]
        p_lo = [sb(f"p_lo{i}", [P, QT, 2 * P], F32R) for i in range(2)]
        shift, mass, inv = sb("shift", [P, 4]), sb("mass", [P, 4]), sb("inv", [P, 4])
        o_sum = sb("o_sum", [P, FEAT])
        wo_raw = pr[:, 0:2, :, :].rearrange("p a b n -> p (a b n)")
        xr, sq, rstd = pr[:, 0, :, :], pr[:, 1, :, :], pr[:, 1, 0, :]

        ps_q, ps_k = ps("ps_q", [P, FEAT]), ps("ps_k", [P, FEAT])
        ps_s = ps("ps_s", [P, 2, FEAT])
        ps_t = [ps(f"ps_t{h}", [P, QT, P]) for h in range(2)]
        ps_o = [ps(f"ps_o{i}", [P, FEAT]) for i in range(2)]

        mean_made, ident_made, wo_split = sem("mean_made"), sem("ident_made"), sem("wo_split")
        v_w_loaded, qk_w_loaded, o_w_loaded, cols_loaded = (sem(n) for n in ("v_w_loaded", "qk_w_loaded", "o_w_loaded", "cols_loaded"))
        zu_loaded, zres_loaded, stored = sem("zu_loaded", 32), sem("zres_loaded", 16), sem("stored", 16)
        v_summed, v_hi_kept, v_kept = sem("v_summed", 8), sem("v_hi_kept", 8), sem("v_kept", 8)
        q_summed, k_summed, q_hi_kept, k_hi_kept, q_kept, k_lo_kept = (
            sem(n, HP) for n in ("q_summed", "k_summed", "q_hi_kept", "k_hi_kept", "q_kept", "k_lo_kept"))
        k_mirrored = sem("k_mirrored", 2 * HP)
        scored, shifted, exped, inverted, scaled, turned, p_hi_kept, p_kept = (
            sem(n, TILES) for n in ("scored", "shifted", "exped", "inverted", "scaled", "turned", "p_hi_kept", "p_kept"))
        mixed, o_moved, o_summed, o_split = sem("mixed", STEPS), sem("o_moved", HEADS), sem("o_summed", HEADS), sem("o_split", 2 * HP)
        attn_summed, added, means_summed, centred, squared, vars_summed, rooted, normed = (
            sem(n, 1) for n in ("attn_summed", "added", "means_summed", "centred", "squared", "vars_summed", "rooted", "normed"))
        inv_var = sem("inv_var", 2)

        block = ctx.enter_context(nc.Block())

        def own(h):
            return slice(h * DH, (h + 1) * DH)

        def batch_rows(a, g):
            batch = slice(g - 1, g) if isinstance(g, int) else bass.ds(g - 1, 1)
            return a[batch, :, :].rearrange("o (t p) n -> p (o t) n", p=P)

        def run(eng, body, after_value, norm_parts):
            def one_pass(g, with_norm):
                if with_norm and -1 in norm_parts:
                    norm_parts[-1](g - 1)
                for e in range(8):
                    after_value(g, e)
                    if with_norm and e in norm_parts:
                        norm_parts[e](g - 1)
                body(g)

            one_pass(1, False)
            with eng.Fori(2, BATCH + 1) as g:
                one_pass(g, True)
            for e in sorted(norm_parts):
                norm_parts[e](BATCH)

        def pair_projected(n):
            pair, unit = divmod(n + PROJECT_AHEAD, QT)
            return (unit // 2, pair + 1) if n >= 0 and unit % 2 == 1 and pair + 1 < HP else (None, None)

        @block.sync
        def _(sp):
            open_loop(sp, loop_sems)
            w_dram = [a.rearrange("(t p) n -> p t n", p=P) for a in (w_qkv0T, w_inj0T, w_qkv1T, w_inj1T)]

            def load_w(lo, hi, s):
                for i in range(4):
                    sp.dma_start(w[i][:, :, lo:hi], w_dram[i][:, :, lo:hi]).then_inc(s, 16)

            def load(g):
                sp.wait_ge(k_summed, at(g, HP, -1))
                sp.wait_ge(q_summed, at(g, HP, -1))
                sp.dma_start(zt[:, :, :], batch_rows(z, g)).then_inc(zu_loaded, 16)
                sp.dma_start(ut[:, :, :], batch_rows(c, g)).then_inc(zu_loaded, 16)

            def load_zres(g):
                sp.wait_ge(stored, at(g, 1, -1, 16))
                sp.dma_start(zres[:, :, :], batch_rows(z, g)).then_inc(zres_loaded, 16)

            load_w(2 * INNER, 3 * INNER, v_w_loaded)
            load(1)
            load_w(0, 2 * INNER, qk_w_loaded)
            load_zres(1)
            with sp.Fori(2, BATCH + 1) as g:
                load(g)
                load_zres(g)

        @block.tensor
        def _(pe):
            pe.wait_ge(ident_made, 2)
            pe.wait_ge(mean_made, 1)
            pe.wait_ge(wo_split, 2)
            def body(g):
                def project(pair, part, half):
                    bank, summed = (ps_q, q_summed) if part == 0 else (ps_k, k_summed)
                    if half == 0:
                        pe.wait_ge(q_kept if part == 0 else k_lo_kept, at(g, HP, pair - 1))
                    cols = slice(part * INNER + pair * P, part * INNER + (pair + 1) * P)
                    here = slice(half * TOK, (half + 1) * TOK)
                    terms = [(w[2 * half + i], src, t) for i, src in enumerate((zt, ut)) for t in range(CT)]
                    for i, (wt, src, t) in enumerate(terms):
                        mm = pe.matmul(bank[:, here], wt[:, t, cols], src[:, t, here],
                                       start=(i == 0), stop=(i == len(terms) - 1), skip_group_check=True)
                    if half == 1:
                        mm.then_inc(summed, 1)

                def score(n):
                    pair, h, half = n // QT, n // 2 % 2, n % 2
                    if n % QT == 0:
                        pe.wait_ge(q_kept, at(g, HP, pair))
                        pe.wait_ge(k_lo_kept, at(g, HP, pair))
                        pe.wait_ge(k_mirrored, at(g, 2 * HP, 2 * pair + 1))
                    for i in range(2):
                        here = slice((2 * half + i) * P, (2 * half + i + 1) * P)
                        pe.wait_ge(exped, at(g, TILES, 2 * n + i - 2))
                        pe.matmul(ps_s[:, i, :], q[pair % 2][:, h, here], k[pair % 2][:, h, :], start=True, stop=False)
                        pe.matmul(ps_s[:, i, :], q[pair % 2][own(h), h, here], k_lo[pair % 2][own(h), :],
                                  start=False, stop=True).then_inc(scored, 1)

                def turn(n):
                    for i in range(2):
                        pe.wait_ge(scaled, at(g, TILES, 2 * n + i))
                        pe.wait_ge(p_kept, at(g, TILES, 2 * n + i - 2))
                        for t in range(QT):
                            mm = pe.transpose(ps_t[i][:, t, :], pr[:, n % (TURN_LAG + 1), i, t * P:(t + 1) * P], ident[:, :])
                        mm.then_inc(turned, 1)

                def mix(n):
                    head, half = n // 2, n % 2
                    pe.wait_ge(p_kept, at(g, TILES, 2 * n + 1))
                    if half == 0:
                        pe.wait_ge(o_summed, at(g, HEADS, head - 2))
                    for t in range(QT):
                        for part in (p_hi, p_lo):
                            mm = pe.matmul(ps_o[head % 2][:, half * 2 * P:(half + 1) * 2 * P], vo[:, head, t, :],
                                           part[n % 2][:, t, :], start=(t == 0 and part is p_hi),
                                           stop=(t == QT - 1 and part is p_lo), skip_group_check=True)
                    mm.then_inc(mixed, 1)

                pe.wait_ge(qk_w_loaded, 64)
                pe.wait_ge(added, at(g, 1, -1))
                def contract_output(t):
                    if t == 0:
                        pe.wait_ge(q_kept, at(g, HP, HP - 1))
                        pe.wait_ge(k_lo_kept, at(g, HP, HP - 1))
                    pe.wait_ge(o_split, at(g, 2 * HP, 2 * t + 1))
                    o_hi, o_lo = vo[:, 2 * t, :, :], vo[:, 2 * t + 1, :, :]
                    for m, bank in enumerate((ps_q, ps_k)):
                        here = slice(m * P, (m + 1) * P)
                        for wo, o in ((wo_lo, o_hi), (wo_hi, o_lo), (wo_hi, o_hi)):
                            mm = pe.matmul(bank[:, :], wo[:, t, here], o, start=(t == 0 and wo is wo_lo),
                                           stop=(t == HP - 1 and wo is wo_hi and o is o_hi), skip_group_check=True)
                    return mm

                for m in range(QT + PROJECT_AHEAD):
                    project(m // QT, m % QT // 2, m % 2)
                pe.wait_ge(v_kept, at(g, 8, 7))
                pe.wait_ge(normed, at(g, 1, -1))
                for n in range(STEPS + MIX_LAG):
                    if TURN_LAG <= n < STEPS + TURN_LAG:
                        turn(n - TURN_LAG)
                    if n < STEPS:
                        score(n)
                    if n < STEPS:
                        pair, unit = divmod(n + PROJECT_AHEAD, QT)
                        if pair + 1 < HP:
                            project(pair + 1, unit // 2, unit % 2)
                    if 0 <= n - OUTPUT_FROM < HP - 1:
                        contract_output(n - OUTPUT_FROM)
                    if n >= MIX_LAG:
                        mix(n - MIX_LAG)
                contract_output(HP - 1).then_inc(attn_summed, 1)

            def values(g, e):
                if e == 0:
                    pe.wait_ge(zu_loaded, at(g, 2, 1, 16))
                    pe.wait_ge(v_w_loaded, 64)
                if e >= 4:
                    pe.wait_ge(v_kept, at(g, 8, e - 4))
                lt, chunk = e // 2, e % 2
                terms = [(w[2 * (lt // 2) + i], src, t) for i, src in enumerate((zt, ut)) for t in range(CT)]
                bank = (ps_t[0][:, :, :], ps_t[1][:, :, :], ps_o[0][:, :], ps_o[1][:, :])[e % 4]
                for i, (wt, src, t) in enumerate(terms):
                    mm = pe.matmul(bank, src[:, t, lt * P:(lt + 1) * P],
                                   wt[:, t, 2 * INNER + chunk * FEAT:2 * INNER + (chunk + 1) * FEAT],
                                   start=(i == 0), stop=(i == len(terms) - 1))
                mm.then_inc(v_summed, 1)

            def means(g):
                pe.wait_ge(added, at(g, 1, 0))
                for t in range(CT):
                    mm = pe.matmul(ps_s[:, 0, :], mean_of[:, :], xr[:, t, :], start=(t == 0), stop=(t == CT - 1))
                mm.then_inc(means_summed, 1)

            def variances(g):
                pe.wait_ge(squared, at(g, 1, 0))
                for t in range(CT):
                    mm = pe.matmul(ps_s[:, 1, :], mean_of[:, :], sq[:, t, :], start=(t == 0), stop=(t == CT - 1))
                mm.then_inc(vars_summed, 1)

            run(pe, body, values, {0: means, 3: variances})

        def value_bank(e):
            bank = (ps_t[0][:, :, :], ps_t[1][:, :, :], ps_o[0][:, :], ps_o[1][:, :])[e % 4]
            return (bank.rearrange("p a b -> p (a b)") if e % 4 < 2 else bank).rearrange("p (h d) -> p h d", d=DH)

        def value_place(e, low):
            lt, chunk = e // 2, e % 2
            return vo[:, chunk * 8:(chunk + 1) * 8, lt, low * DH:(low + 1) * DH]

        @block.scalar
        def _(act):
            act.dma_start(wo_raw.rearrange("p (t n) -> p t n", n=TOK), w_oT.rearrange("(t p) n -> p t n", p=P)).then_inc(o_w_loaded, 16)
            act.dma_start(bo_col[:, :], bo).then_inc(cols_loaded, 16)
            act.dma_start(qb_col[:, :], q_bias).then_inc(cols_loaded, 16)
            act.wait_ge(o_w_loaded, 16)
            act.activation(wo_hi[:, :, :].rearrange("p t n -> p (t n)"), wo_raw, ACT.Copy).then_inc(wo_split, 1)
            act.wait_ge(cols_loaded, 32)
            def body(g):
                def queries_hi(pair):
                    act.wait_ge(q_summed, at(g, HP, pair))
                    act.wait_ge(scored, at(g, TILES, 2 * QT * (pair - 1) - 1))
                    for h in range(2):
                        ins = act.activation(q[pair % 2][own(h), h, :], ps_q[own(h), :], ACT.Identity,
                                             bias=qb_col[own(h), pair:pair + 1])
                    ins.then_inc(q_hi_kept, 1)

                def keys_hi(pair):
                    act.wait_ge(k_summed, at(g, HP, pair))
                    act.wait_ge(scored, at(g, TILES, 2 * QT * (pair - 1) - 1))
                    for h in range(2):
                        ins = act.activation(k[pair % 2][own(h), h, :], ps_k[own(h), :], ACT.Copy, scale=SCALE)
                    ins.then_inc(k_hi_kept, 1)

                def exponentials(n):
                    for i in range(2):
                        a = n % 2 * 2 + i
                        act.wait_ge(shifted, at(g, TILES, 2 * n + i))
                        act.wait_ge(turned, at(g, TILES, 2 * (n - TURN_LAG - 1) + i))
                        act.wait_ge(inverted, at(g, TILES, 2 * n + i - 4))
                        act.activation(pr[:, n % (TURN_LAG + 1), i, :], ps_s[:, i, :], ACT.Exp, bias=shift[:, a:a + 1],
                                       accum_out=mass[:, a:a + 1]).then_inc(exped, 1)

                def turned_hi(n):
                    act.wait_ge(mixed, at(g, STEPS, n - 2))
                    for i in range(2):
                        act.wait_ge(turned, at(g, TILES, 2 * n + i))
                        act.activation(p_hi[n % 2][:, :, i * P:(i + 1) * P], ps_t[i][:, :, :], ACT.Copy).then_inc(p_hi_kept, 1)

                def move_output(n):
                    if n % 2 == 1:
                        head, h = n // 2, n // 2 % 2
                        act.wait_ge(mixed, at(g, STEPS, n))
                        if h == 0:
                            act.wait_ge(o_split, at(g, 2 * HP, 2 * (head // 2) - 1))
                        act.activation(o_sum[own(h), :], ps_o[h][own(1 - h), :], ACT.Copy).then_inc(o_moved, 1)

                queries_hi(0)
                keys_hi(0)
                queries_hi(1)
                for n in range(STEPS + MIX_LAG + 1):
                    if n > MIX_LAG:
                        move_output(n - MIX_LAG - 1)
                    if TURN_LAG <= n < STEPS + TURN_LAG:
                        turned_hi(n - TURN_LAG)
                    if n < STEPS:
                        exponentials(n)
                    part, pair = pair_projected(n)
                    if pair is not None:
                        (queries_hi, keys_hi)[part](pair)

            def values_hi(g, e):
                act.wait_ge(v_summed, at(g, 8, e))
                act.activation(value_place(e, 0), value_bank(e), ACT.Copy).then_inc(v_hi_kept, 1)

            def squares(g):
                act.wait_ge(centred, at(g, 1, 0))
                act.activation(sq, zres[:, :, :], ACT.Square).then_inc(squared, 1)

            def root_and_store(g):
                act.wait_ge(inv_var, at(g, 2, 1))
                act.activation(rstd, rstd, ACT.Sqrt).then_inc(rooted, 1)
                act.wait_ge(normed, at(g, 1, 0))
                act.dma_start(batch_rows(out, g), zres[:, :, :]).then_inc(stored, 16)

            run(act, body, values_hi, {2: squares, 6: root_and_store})
            act.wait_ge(stored, 16 * (BATCH + 1))

        @block.gpsimd
        def _(pool):
            make_identity(pool, ident, ident_made)
            pool.memset(one[:, :], 1.0).then_inc(ident_made, 1)
            pool.wait_ge(ident_made, 3)
            with pool.Fori(1, BATCH + 1) as g:
                def mirror_keys(pair, n=0):
                    pool.wait_ge(scaled, at(g, TILES, 2 * n - 1))
                    pool.wait_ge(o_split, at(g, 2 * HP, 2 * max(0, (n - MIX_LAG - 1) // QT) - 1))
                    pool.wait_ge(k_hi_kept, at(g, HP, pair))
                    for h in range(2):
                        there = k[pair % 2][own(h), h, :].bitcast(F32)
                        ins = pool.tensor_tensor(k[pair % 2][own(1 - h), h, :], there, one[own(h), :].to_broadcast([DH, FEAT]), ALU.mult)
                        ins.then_inc(k_mirrored, 1)
                        pool.wait_ge(k_mirrored, at(g, 2 * HP, 2 * pair + h))

                def scale(n):
                    for i in range(2):
                        a = n % 2 * 2 + i
                        pool.wait_ge(inverted, at(g, TILES, 2 * n + i))
                        pool.tensor_tensor(pr[:, n % (TURN_LAG + 1), i, :], pr[:, n % (TURN_LAG + 1), i, :],
                                           inv[:, a:a + 1].to_broadcast([P, FEAT]), ALU.mult).then_inc(scaled, 1)

                def split_output(n):
                    if n % QT == QT - 1:
                        pair = n // QT
                        o_hi, o_lo = (vo[:, 2 * pair + i, :, :].rearrange("p a b -> p (a b)") for i in range(2))
                        pool.wait_ge(o_summed, at(g, HEADS, 2 * pair + 1))
                        pool.tensor_tensor(o_hi, o_sum[:, :], one[:, :].to_broadcast([P, FEAT]), ALU.mult).then_inc(o_split, 1)
                        pool.wait_ge(o_split, at(g, 2 * HP, 2 * pair))
                        pool.tensor_tensor(o_lo, o_sum[:, :], o_hi.bitcast(F32), ALU.subtract).then_inc(o_split, 1)

                mirror_keys(0)
                for n in range(STEPS + MIX_LAG + 1):
                    part, pair = pair_projected(n - 1)
                    if part == 1:
                        mirror_keys(pair, n)
                    if n < STEPS:
                        scale(n)
                    if n > MIX_LAG:
                        split_output(n - MIX_LAG - 1)

        @block.vector
        def _(dve):
            dve.memset(mean_of[:, :], 1.0 / TOK).then_inc(mean_made, 1)
            dve.wait_ge(wo_split, 1)
            dve.wait_ge(cols_loaded, 32)
            dve.tensor_tensor(wo_lo[:, :, :].rearrange("p t n -> p (t n)"), wo_raw,
                              wo_hi[:, :, :].rearrange("p t n -> p (t n)").bitcast(F32), ALU.subtract).then_inc(wo_split, 1)
            def body(g):
                def queries_lo(pair):
                    dve.wait_ge(q_hi_kept, at(g, HP, pair))
                    for h in range(2):
                        ins = dve.scalar_tensor_tensor(out=q[pair % 2][own(1 - h), h, :], in0=ps_q[own(h), :],
                                                       scalar=qb_col[own(h), pair:pair + 1],
                                                       in1=q[pair % 2][own(h), h, :].bitcast(F32), op0=ALU.add, op1=ALU.subtract)
                    ins.then_inc(q_kept, 1)

                def keys_lo(pair):
                    dve.wait_ge(k_hi_kept, at(g, HP, pair))
                    for h in range(2):
                        ins = dve.scalar_tensor_tensor(out=k_lo[pair % 2][own(h), :], in0=ps_k[own(h), :], scalar=SCALE,
                                                       in1=k[pair % 2][own(h), h, :].bitcast(F32), op0=ALU.mult, op1=ALU.subtract)
                    ins.then_inc(k_lo_kept, 1)

                def shifts(n):
                    for i in range(2):
                        a = n % 2 * 2 + i
                        dve.wait_ge(scored, at(g, TILES, 2 * n + i))
                        dve.wait_ge(exped, at(g, TILES, 2 * n + i - 4))
                        dve.tensor_reduce(shift[:, a:a + 1], ps_s[:, i, :], AXIS.X, ALU.max, negate=True).then_inc(shifted, 1)

                def inverse(n, i):
                    a = n % 2 * 2 + i
                    dve.wait_ge(exped, at(g, TILES, 2 * n + i))
                    dve.wait_ge(scaled, at(g, TILES, 2 * n + i - 4))
                    dve.reciprocal(inv[:, a:a + 1], mass[:, a:a + 1]).then_inc(inverted, 1)

                def inverses(n):
                    for i in range(2):
                        inverse(n, i)

                def turned_lo(n):
                    for i in range(2):
                        here = slice(i * P, (i + 1) * P)
                        dve.wait_ge(p_hi_kept, at(g, TILES, 2 * n + i))
                        dve.tensor_tensor(p_lo[n % 2][:, :, here], ps_t[i][:, :, :], p_hi[n % 2][:, :, here].bitcast(F32),
                                          ALU.subtract).then_inc(p_kept, 1)

                def sum_output(n):
                    if n % 2 == 1:
                        head, h = n // 2, n // 2 % 2
                        dve.wait_ge(o_moved, at(g, HEADS, head))
                        dve.tensor_tensor(o_sum[own(h), :], ps_o[h][own(h), :], o_sum[own(h), :], ALU.add).then_inc(o_summed, 1)

                queries_lo(0)
                keys_lo(0)
                queries_lo(1)
                for n in range(STEPS + MIX_LAG + 1):
                    if n < STEPS:
                        shifts(n)
                    if TURN_LAG <= n < STEPS + TURN_LAG:
                        turned_lo(n - TURN_LAG)
                    if n < STEPS:
                        inverses(n)
                    part, pair = pair_projected(n - 1)
                    if pair is not None:
                        (queries_lo, keys_lo)[part](pair)
                    if n > MIX_LAG:
                        sum_output(n - MIX_LAG - 1)

            def values_lo(g, e):
                dve.wait_ge(v_hi_kept, at(g, 8, e))
                dve.tensor_tensor(value_place(e, 1), value_bank(e), value_place(e, 0).bitcast(F32), ALU.subtract).then_inc(v_kept, 1)

            def add(g):
                dve.wait_ge(attn_summed, at(g, 1, 0))
                dve.wait_ge(zres_loaded, at(g, 1, 0, 16))
                for m, bank in enumerate((ps_q, ps_k)):
                    ins = dve.scalar_tensor_tensor(out=xr[:, m, :], in0=bank[:, :], scalar=bo_col[:, m:m + 1],
                                                   in1=zres[:, m, :], op0=ALU.add, op1=ALU.add)
                ins.then_inc(added, 1)

            def centre(g):
                dve.wait_ge(means_summed, at(g, 1, 0))
                for m in range(CT):
                    ins = dve.tensor_tensor(zres[:, m, :], xr[:, m, :], ps_s[:, 0, :], ALU.subtract)
                ins.then_inc(centred, 1)

            def invert(g):
                dve.wait_ge(vars_summed, at(g, 1, 0))
                dve.tensor_scalar(rstd, ps_s[:, 1, :], 1e-5, None, ALU.add).then_inc(inv_var, 1)
                dve.wait_ge(inv_var, at(g, 2, 0))
                dve.reciprocal(rstd, rstd).then_inc(inv_var, 1)

            def normalise(g):
                dve.wait_ge(rooted, at(g, 1, 0))
                for m in range(CT):
                    ins = dve.tensor_tensor(zres[:, m, :], zres[:, m, :], rstd, ALU.mult)
                ins.then_inc(normed, 1)

            run(dve, body, values_lo, {-1: add, 1: centre, 5: invert, 6: normalise})

def token_attention(nc, semaphores, tag, x, cT, mask, mask_batches, ln_cols, wq_d, wk_d, wv_d, wo_d, qk_cols, rows, out):
    HEADS, DH = 16, 32
    STEPS = HEADS // 2
    TILE_HEADS = P // DH
    RING = 4
    PASSES = BATCH // 2
    SCALE = DH ** -0.5
    CROSS = cT is not None
    ORDER = ("K0", "K1", "T0", "T1", "Q0", "Q1", "V0", "V1") if CROSS else ("T0", "T1", "Q0", "Q1", "K0", "K1", "V0", "V1")
    FILL = dict(zip((0, 2, 3, 4, 5, 6, 8, 9) if CROSS else (2, 3, 4, 5, 6, 7, 8, 9), ORDER))
    TURN_LAG, MIX_LAG = 2, 3
    LAST = STEPS + MIX_LAG
    with ExitStack() as ctx:
        def sb(name, shape):
            return ctx.enter_context(nc.sbuf_tensor(f"{tag}_{name}", shape, F32))

        def ps(name, shape):
            return ctx.enter_context(nc.psum_tensor(f"{tag}_{name}", shape, F32))

        loop_sems = []

        def sem(name, per_batch=0):
            s = semaphores.allocate(f"{tag}_{name}")
            if per_batch:
                loop_sems.append((s, 2 * per_batch))
            return s

        wq, wk, wv, wo = (sb(n, [P, FT, FEAT]) for n in ("wq", "wk", "wv", "wo"))
        ln_sb, qk_sb = sb("ln_cols", [P, 2, FT]), sb("qk_cols", [P, 2, FT])
        rows_sb = sb("rows", [P, 2, FEAT])
        ident = sb("ident", [P, P])
        half_power = sb("half_power", [P, TT])
        xs = [sb(f"xs{u}", [P, TT, FEAT]) for u in range(2)]
        cs = [sb(f"cs{u}", [P, FT, TOK]) for u in range(2)] if CROSS else None
        mk = [sb(f"mk{u}", [P, TT, TOK]) for u in range(2)]
        ma = [sb(f"ma{u}", [P, TT, TOK]) for u in range(2)]
        stats, moments, var_eps, rstd = sb("stats", [P, TT, 6]), sb("moments", [P, TT, 2]), sb("var_eps", [P, TT]), sb("rstd", [P, TT])
        xn = sb("xn", [P, TT, FEAT])
        lnT = sb("lnT", [P, FT, TOK])
        qT = [sb(f"qT{u}", [P, FT, TOK]) for u in range(2)]
        kT = [sb(f"kT{u}", [P, FT, TOK]) for u in range(2)]
        v = [sb(f"v{u}", [P, TT, FEAT]) for u in range(2)]
        pr = [sb(f"pr{i}", [P, 2, TT, TOK]) for i in range(RING)]
        pT = [sb(f"pT{i}", [P, 2, TT, TOK]) for i in range(2)]
        shift, mass, inv = ([sb(f"{n}{i}", [P, 2, TT]) for i in range(RING)] for n in ("shift", "mass", "inv"))
        ctxT = sb("ctxT", [P, FT, TOK])
        xb = sb("xb", [P, TT, FEAT])
        res = sb("res", [P, TT, FEAT])

        ps_s = [ps(f"ps_s{i}", [P, 2, TT, TOK]) for i in range(2)]
        ps_t = ps("ps_t", [P, 2, TT, TOK])
        ps_o = ps("ps_o", [P, TOK])
        ps_p = ps("ps_p", [P, 2, TOK])

        small_loaded, ident_made, const_made = sem("small_loaded"), sem("ident_made"), sem("const_made")
        w_loaded = {n: sem("w_loaded_" + n) for n in "QKVO"}
        x_loaded, mask_loaded, c_loaded = ([sem(f"{n}_loaded{u}") for u in range(2)] for n in ("x", "mask", "c"))
        stored = sem("stored", 16)
        counted, normalised, biased, mask_split = sem("counted", 4), sem("normalised", 1), sem("biased", 1), sem("mask_split", 2)
        powered = sem("powered", 1)
        filled, fill_kept = sem("filled", 8), sem("fill_kept", 8)
        scored, masked_mul, masked, shifted, exped, inverted, normed, turned, turned_kept = (
            sem(n, STEPS) for n in ("scored", "masked_mul", "masked", "shifted", "exped", "inverted", "normed", "turned", "turned_kept"))
        mixed, mixed_kept = sem("mixed", FT), sem("mixed_kept", FT)
        out_summed, added = sem("out_summed", 1), sem("added", 1)

        block = ctx.enter_context(nc.Block())

        def each_pass(eng, before, batch, finish):
            before(1, -1)
            batch(1, 0, False, True)
            batch(1, 1, False)
            with eng.Fori(2, PASSES) as g:
                batch(g, 0, False)
                batch(g, 1, False)
            batch(PASSES, 0, False)
            batch(PASSES, 1, True)
            finish(PASSES, 1)

        def arrived(g, u):
            return (g + (u + 1) // 2) * 16

        def fill_at(unit):
            return ORDER.index(unit)

        @block.sync
        def _(sp):
            open_loop(sp, loop_sems)

            def load(g, u, last=False, first=False):
                if last:
                    return
                b, s = 2 * (g - 1) + u + 1, (u + 1) % 2
                index = bass.ds(b, 1) if not isinstance(b, int) else slice(b, b + 1)

                def tiles(a, at_index=index):
                    return a[at_index, :, :].rearrange("o (t p) n -> p (o t) n", p=P)

                sp.wait_ge(biased, at(g, 2, u - 1))
                sp.wait_ge(normalised, at(g, 2, u - 1))
                sp.dma_start(xs[s][:, :, :], tiles(x)).then_inc(x_loaded[s], 16)
                if CROSS:
                    sp.wait_ge(filled, at(g, 16, u * 8 - 1))
                    sp.dma_start(cs[s][:, :, :], tiles(cT)).then_inc(c_loaded[s], 16)
                sp.wait_ge(masked, at(g, 2 * STEPS, u * STEPS - 1))
                sp.dma_start(mk[s][:, :, :], tiles(mask, index if mask_batches > 1 else slice(0, 1))).then_inc(mask_loaded[s], 16)

            load(1, -1)
            sp.dma_start(ln_sb[:, :, :], ln_cols).then_inc(small_loaded, 16)
            sp.dma_start(qk_sb[:, :, :], qk_cols).then_inc(small_loaded, 16)
            for i, row in enumerate(rows):
                sp.dma_start(rows_sb[:, i, :], row.to_broadcast([P, FEAT])).then_inc(small_loaded, 16)
            weights = {"Q": (wq, wq_d), "K": (wk, wk_d), "V": (wv, wv_d), "O": (wo, wo_d)}
            for n in "KQVO" if CROSS else "QKVO":
                sp.dma_start(weights[n][0][:, :, :], weights[n][1].rearrange("(t p) n -> p t n", p=P)).then_inc(w_loaded[n], 16)

            each_pass(sp, lambda g, u: None, load, lambda g, u: None)

        SMALL_DONE = 16 * 4

        @block.gpsimd
        def _(pool):
            make_identity(pool, ident, ident_made)
            pool.memset(half_power[:, :], -0.5).then_inc(const_made, 1)
            pool.wait_ge(small_loaded, SMALL_DONE)
            pool.wait_ge(const_made, 1)

            def prepare(g, u):
                pool.wait_ge(counted, at(g, 8, (u + 1) * 4 + 3))
                pool.wait_ge(normalised, at(g, 2, u))
                pool.tensor_tensor(rstd[:, :], var_eps[:, :], half_power[:, :], ALU.pow).then_inc(powered, 1)

            def batch(g, u, last, first=False):
                if not last:
                    prepare(g, u)
                for n in range(STEPS):
                    pool.wait_ge(masked_mul, at(g, 2 * STEPS, u * STEPS + n))
                    ins = pool.tensor_tensor(pr[n % RING][:, :, :, :].rearrange("p h t k -> p h (t k)"),
                                             pr[n % RING][:, :, :, :].rearrange("p h t k -> p h (t k)"),
                                             ma[u][:, :, :].rearrange("p t k -> p (t k)").unsqueeze(1).to_broadcast([P, 2, TT * TOK]),
                                             ALU.add)
                    ins.then_inc(masked, 1)
                    if n == 3:
                        pool.wait_ge(added, at(g, 2, u - 1))
                        pool.tensor_tensor(xb[:, :, :], xs[u][:, :, :], rows_sb[:, 1, :].unsqueeze(1).to_broadcast([P, TT, FEAT]),
                                           ALU.add).then_inc(biased, 1)

            each_pass(pool, prepare, batch, lambda g, u: None)

        @block.tensor
        def _(pe):
            pe.wait_ge(ident_made, 2)

            def fill(g, u, unit):
                s, i = (u + 1) % 2, fill_at(unit)
                base = (u + 1) * 8
                pe.wait_ge(fill_kept, at(g, 16, base + i - 1))
                src = cs[s] if CROSS and unit[0] in "KV" else lnT
                if unit[0] == "T":
                    if unit == "T0":
                        pe.wait_ge(normalised, at(g, 2, u + 1))
                    for j in range(2):
                        f = 2 * int(unit[1]) + j
                        for m in range(TT):
                            mm = pe.transpose(ps_p[:, j, m * P:(m + 1) * P], xn[:, m, f * P:(f + 1) * P], ident[:, :])
                else:
                    if src is lnT:
                        pe.wait_ge(fill_kept, at(g, 16, base + fill_at("T1")))
                    else:
                        pe.wait_ge(c_loaded[(u + 1) % 2], arrived(g, u))
                    if unit[0] == "V":
                        m = int(unit[1])
                        for t in range(FT):
                            mm = pe.matmul(ps_p[:, :, :], src[:, t, m * P:(m + 1) * P], wv[:, t, :],
                                           start=(t == 0), stop=(t == FT - 1))
                    else:
                        w = wq if unit[0] == "Q" else wk
                        for j in range(2):
                            f = 2 * int(unit[1]) + j
                            for t in range(FT):
                                mm = pe.matmul(ps_p[:, j, :], w[:, t, f * P:(f + 1) * P], src[:, t, :],
                                               start=(t == 0), stop=(t == FT - 1))
                mm.then_inc(filled, 1)

            def before(g, u):
                for unit in ORDER:
                    if unit[0] != "T":
                        pe.wait_ge(w_loaded[unit[0]], 16)
                    fill(g, u, unit)
                pe.wait_ge(w_loaded["O"], 16)

            def finish(g, u):
                pe.wait_ge(mixed_kept, at(g, 2 * FT, u * FT + FT - 1))
                for m in range(TT):
                    for t in range(FT):
                        mm = pe.matmul(ps_t[:, m, :, :], ctxT[:, t, m * P:(m + 1) * P], wo[:, t, :],
                                       start=(t == 0), stop=(t == FT - 1))
                mm.then_inc(out_summed, 1)

            def batch(g, u, last, first=False):
                e = u * STEPS
                for n in range(LAST):
                    if n < STEPS:
                        if n == 0:
                            pe.wait_ge(fill_kept, at(g, 16, u * 8 + 7))
                        pe.wait_ge(masked_mul, at(g, 2 * STEPS, e + n - 2))
                        for i in range(2):
                            h = 2 * n + i
                            r = slice(h % TILE_HEADS * DH, (h % TILE_HEADS + 1) * DH)
                            for m in range(TT):
                                mm = pe.matmul(ps_s[n % 2][:, i, m, :], qT[u][r, h // TILE_HEADS, m * P:(m + 1) * P],
                                               kT[u][r, h // TILE_HEADS, :], start=True, stop=True)
                        mm.then_inc(scored, 1)
                    if n == 1 and not first:
                        finish(g, u - 1)
                    if n in FILL and not last:
                        fill(g, u, FILL[n])
                    if 0 <= n - TURN_LAG < STEPS:
                        k = n - TURN_LAG
                        pe.wait_ge(normed, at(g, 2 * STEPS, e + k))
                        pe.wait_ge(turned_kept, at(g, 2 * STEPS, e + k - 1))
                        if k == 0:
                            pe.wait_ge(added, at(g, 2, u - 1))
                        for i in range(2):
                            for t in range(TT):
                                for m in range(TT):
                                    mm = pe.transpose(ps_t[:, i, t, m * P:(m + 1) * P],
                                                      pr[k % RING][:, i, m, t * P:(t + 1) * P], ident[:, :])
                        mm.then_inc(turned, 1)
                    if n >= MIX_LAG:
                        k = n - MIX_LAG
                        pe.wait_ge(turned_kept, at(g, 2 * STEPS, e + k))
                        if k % 2 == 0:
                            pe.wait_ge(mixed_kept, at(g, 2 * FT, u * FT + k // 2 - 1))
                        for i in range(2):
                            h = 2 * k + i
                            r = slice(h % TILE_HEADS * DH, (h % TILE_HEADS + 1) * DH)
                            for t in range(TT):
                                mm = pe.matmul(ps_o[r, :], v[u][:, t, h * DH:(h + 1) * DH], pT[k % 2][:, i, t, :],
                                               start=(t == 0), stop=(t == TT - 1))
                        if k % 2 == 1:
                            mm.then_inc(mixed, 1)

            each_pass(pe, before, batch, finish)

        @block.scalar
        def _(act):
            act.wait_ge(small_loaded, SMALL_DONE)

            def keep_fill(g, u, unit):
                if unit[0] == "V":
                    return
                s, i = (u + 1) % 2, fill_at(unit)
                act.wait_ge(filled, at(g, 16, (u + 1) * 8 + i))
                for j in range(2):
                    f = 2 * int(unit[1]) + j
                    if unit[0] == "T":
                        ins = act.activation(lnT[:, f, :], ps_p[:, j, :], ACT.Identity, bias=ln_sb[:, 1, f:f + 1],
                                             scale=ln_sb[:, 0, f:f + 1])
                    else:
                        ins = act.activation((qT if unit[0] == "Q" else kT)[s][:, f, :], ps_p[:, j, :], ACT.Identity,
                                             bias=qk_sb[:, "QK".index(unit[0]), f:f + 1])
                ins.then_inc(fill_kept, 1)

            def before(g, u):
                for unit in ORDER:
                    keep_fill(g, u, unit)

            def store(g, u):
                b = 2 * (g - 1) + u
                act.wait_ge(added, at(g, 2, u))
                act.dma_start(out[bass.ds(b, 1) if not isinstance(b, int) else slice(b, b + 1), :, :]
                              .rearrange("o (t p) n -> p (o t) n", p=P), res[:, :, :]).then_inc(stored, 16)

            def batch(g, u, last, first=False):
                e = u * STEPS
                for n in range(LAST):
                    if 1 <= n <= STEPS:
                        k = n - 1
                        act.wait_ge(shifted, at(g, 2 * STEPS, e + k))
                        act.wait_ge(inverted, at(g, 2 * STEPS, e + k - RING))
                        for i in range(2):
                            for m in range(TT):
                                tile = pr[k % RING][:, i, m, :]
                                ins = act.activation(tile, tile, ACT.Exp, bias=shift[k % RING][:, i, m:m + 1],
                                                     accum_out=mass[k % RING][:, i, m:m + 1])
                        ins.then_inc(exped, 1)
                    if n in FILL and not last:
                        keep_fill(g, u, FILL[n])
                    if 0 <= n - TURN_LAG < STEPS:
                        k = n - TURN_LAG
                        act.wait_ge(turned, at(g, 2 * STEPS, e + k))
                        act.wait_ge(mixed, at(g, 2 * FT, u * FT + (k - 2) // 2))
                        act.activation(pT[k % 2][:, :, :, :], ps_t[:, :, :, :], ACT.Copy).then_inc(turned_kept, 1)
                    if n == 2 and not first:
                        store(g, u - 1)
                    if n >= MIX_LAG and (n - MIX_LAG) % 2 == 1:
                        f = (n - MIX_LAG) // 2
                        act.wait_ge(mixed, at(g, 2 * FT, u * FT + f))
                        if f == 0:
                            act.wait_ge(out_summed, at(g, 2, u - 1))
                        act.activation(ctxT[:, f, :], ps_o[:, :], ACT.Copy).then_inc(mixed_kept, 1)

            each_pass(act, before, batch, store)
            act.wait_ge(stored, 16 * (BATCH + 2))

        @block.vector
        def _(dve):
            dve.wait_ge(small_loaded, SMALL_DONE)

            def statistics(g, u):
                s = (u + 1) % 2
                dve.wait_ge(x_loaded[s], arrived(g, u))
                for m in range(TT):
                    ins = dve.bn_stats(stats[:, m, :], xs[s][:, m, :])
                ins.then_inc(counted, 1)
                dve.wait_ge(counted, at(g, 8, (u + 1) * 4))
                dve.wait_ge(powered, at(g, 2, u))
                dve.tensor_copy(var_eps[:, :], stats[:, :, 2]).then_inc(counted, 1)
                for m in range(TT):
                    ins = dve.bn_aggr(moments[:, m, :], stats[:, m, :])
                ins.then_inc(counted, 1)
                dve.wait_ge(counted, at(g, 8, (u + 1) * 4 + 2))
                dve.tensor_scalar(var_eps[:, :], moments[:, :, 1], 1e-5, None, ALU.add).then_inc(counted, 1)

            def split_mask(g, u):
                s = (u + 1) % 2
                dve.wait_ge(mask_loaded[s], arrived(g, u))
                dve.wait_ge(masked, at(g, 2 * STEPS, u * STEPS - 1))
                dve.tensor_scalar(ma[s][:, :, :], mk[s][:, :, :], 1e4, -1e4, ALU.mult, ALU.add).then_inc(mask_split, 1)
                dve.wait_ge(mask_split, at(g, 4, (u + 1) * 2))
                dve.tensor_scalar(mk[s][:, :, :], mk[s][:, :, :], SCALE, None, ALU.mult).then_inc(mask_split, 1)

            def normalise(g, u):
                s = (u + 1) % 2
                dve.wait_ge(powered, at(g, 2, u + 1))
                dve.wait_ge(filled, at(g, 16, u * 8 + fill_at("T1")))
                for m in range(TT):
                    ins = dve.tensor_scalar(xn[:, m, :], xs[s][:, m, :], moments[:, m, 0:1], rstd[:, m:m + 1],
                                            ALU.subtract, ALU.mult)
                ins.then_inc(normalised, 1)

            def keep_values(g, u, unit):
                i, m = fill_at(unit), int(unit[1])
                dve.wait_ge(filled, at(g, 16, (u + 1) * 8 + i))
                dve.tensor_tensor(v[(u + 1) % 2][:, m, :], ps_p[:, :, :].rearrange("p a b -> p (a b)"), rows_sb[:, 0, :],
                                  ALU.add).then_inc(fill_kept, 1)

            def before(g, u):
                statistics(g, u)
                normalise(g, u)
                split_mask(g, u)
                keep_values(g, u, "V0")
                keep_values(g, u, "V1")

            def add(g, u):
                dve.wait_ge(out_summed, at(g, 2, u))
                dve.wait_ge(biased, at(g, 2, u))
                dve.wait_ge(stored, at(g, 2, u - 1, 16))
                dve.tensor_tensor(res[:, :, :], ps_t[:, :, :, :].rearrange("p m a b -> p m (a b)"), xb[:, :, :],
                                  ALU.add).then_inc(added, 1)

            def batch(g, u, last, first=False):
                e = u * STEPS
                dve.wait_ge(mask_split, at(g, 4, u * 2 + 1))
                for n in range(LAST):
                    if 0 <= n - TURN_LAG < STEPS:
                        k = n - TURN_LAG
                        dve.wait_ge(exped, at(g, 2 * STEPS, e + k))
                        dve.reciprocal(inv[k % RING][:, :, :], mass[k % RING][:, :, :]).then_inc(inverted, 1)
                        dve.wait_ge(inverted, at(g, 2 * STEPS, e + k))
                        for i in range(2):
                            for m in range(TT):
                                tile = pr[k % RING][:, i, m, :]
                                ins = dve.tensor_scalar(tile, tile, inv[k % RING][:, i, m:m + 1], None, ALU.mult)
                        ins.then_inc(normed, 1)
                    if n < STEPS:
                        dve.wait_ge(scored, at(g, 2 * STEPS, e + n))
                        dve.wait_ge(turned, at(g, 2 * STEPS, e + n - RING))
                        dve.tensor_tensor(pr[n % RING][:, :, :, :].rearrange("p h t k -> p h (t k)"),
                                          ps_s[n % 2][:, :, :, :].rearrange("p h t k -> p h (t k)"),
                                          mk[u][:, :, :].rearrange("p t k -> p (t k)").unsqueeze(1).to_broadcast([P, 2, TT * TOK]),
                                          ALU.mult).then_inc(masked_mul, 1)
                    if n == 0 and not last:
                        statistics(g, u)
                    if n == 1 and not last:
                        normalise(g, u)
                    if 1 <= n <= STEPS:
                        k = n - 1
                        dve.wait_ge(masked, at(g, 2 * STEPS, e + k))
                        dve.wait_ge(exped, at(g, 2 * STEPS, e + k - RING))
                        dve.tensor_reduce(shift[k % RING][:, :, :], pr[k % RING][:, :, :, :], AXIS.X, ALU.max,
                                          negate=True).then_inc(shifted, 1)
                    if n == 1 and not first:
                        add(g, u - 1)
                    if n == 4 and not last:
                        split_mask(g, u)
                    if n in FILL and not last and FILL[n][0] == "V":
                        keep_values(g, u, FILL[n])

            each_pass(dve, before, batch, add)

def token_mlp(nc, semaphores, x, w1_d, w2_d, ln_cols, b1, b2, out):
    HID = 4 * FEAT
    CHUNKS = HID // (2 * P)
    RING = 4
    PASSES = BATCH // 2
    Y_LAG = 3
    PIECES = 2 * FT
    TURN_STEPS = (4, 6)
    with ExitStack() as ctx:
        def sb(name, shape, dtype=F32):
            return ctx.enter_context(nc.sbuf_tensor("mlp_" + name, shape, dtype))

        def ps(name, shape):
            return ctx.enter_context(nc.psum_tensor("mlp_" + name, shape, F32))

        loop_sems = []

        def sem(name, per_batch=0):
            s = semaphores.allocate("mlp_" + name)
            if per_batch:
                loop_sems.append((s, 2 * per_batch))
            return s

        w1_hi, w1_lo = (sb("w1_" + n, [P, FT, HID], F32R) for n in ("hi", "lo"))
        w2_hi, w2_lo = (sb("w2_" + n, [P, 2 * CHUNKS, FEAT], F32R) for n in ("hi", "lo"))
        ln_sb, b1_sb, b2_row = sb("ln_cols", [P, 2, FT]), sb("b1", [P, 2 * CHUNKS]), sb("b2", [P, FEAT])
        ident, half_power = sb("ident", [P, P]), sb("half_power", [P, TT])
        xs = [sb(f"xs{u}", [P, TT, FEAT]) for u in range(2)]
        stats, moments, var_eps, rstd = sb("stats", [P, TT, 6]), sb("moments", [P, TT, 2]), sb("var_eps", [P, TT]), sb("rstd", [P, TT])
        xn = sb("xn", [P, TT, FEAT])
        ln_raw = sb("ln_raw", [P, FT, TOK])
        ln_hi, ln_lo = ([sb(f"ln_{n}{u}", [P, FT, TOK], F32R) for u in range(2)] for n in ("hi", "lo"))
        pre_ring, cube_ring = sb("pre", [P, RING, 2, TOK]), sb("cube", [P, RING, 2, TOK])
        pre, cube = ([ring[:, i, :, :] for i in range(RING)] for ring in (pre_ring, cube_ring))
        hid_hi, hid_lo = ([sb(f"hid_{n}{i}", [P, 2, TOK], F32R) for i in range(RING)] for n in ("hi", "lo"))
        xb_res = sb("xb_res", [P, 2, TT, FEAT])
        xb, res = xb_res[:, 0, :, :], xb_res[:, 1, :, :]
        stages = [ring[:, :, :, :].rearrange("p a b n -> p (a b n)") for ring in (pre_ring, cube_ring, xb_res)]

        ps_h = [ps(f"ps_h{i}", [P, 2, TOK]) for i in range(2)]
        ps_y = ps("ps_y", [P, TT, FEAT])
        ps_t = [ps(f"ps_t{i}", [P, 2, TOK]) for i in range(2)]

        cols_loaded, ident_made, const_made = (sem(n) for n in ("cols_loaded", "ident_made", "const_made"))
        piece_loaded = [sem(f"piece_loaded{i}") for i in range(3)]
        piece_hi, piece_split = sem("piece_hi"), sem("piece_split")
        loaded, stored = [sem(f"loaded{u}") for u in range(2)], sem("stored", 16)
        counted, powered, normalised, biased = sem("counted", 4), sem("powered", 1), sem("normalised", 1), sem("biased", 1)
        turned, turned_kept, ln_rounded, ln_split = sem("turned", 2), sem("turned_kept", 2), sem("ln_rounded", 2), sem("ln_split", 2)
        h_summed, squared, squared1, cubed, bent, gelled, hid_rounded, hid_split = (
            sem(n, CHUNKS) for n in ("h_summed", "squared", "squared1", "cubed", "bent", "gelled", "hid_rounded", "hid_split"))
        y_used, added = sem("y_used", CHUNKS), sem("added", 1)

        block = ctx.enter_context(nc.Block())

        def piece_of(i, part):
            if i < FT:
                return (w1_hi, w1_lo)[part][:, i, :]
            k = i - FT
            return (w2_hi, w2_lo)[part][:, 4 * k:4 * (k + 1), :].rearrange("p t n -> p (t n)")

        def each_pass(eng, before, batch):
            before(1, -1)
            with eng.Fori(1, PASSES) as g:
                batch(g, 0, False)
                batch(g, 1, False)
            batch(PASSES, 0, False)
            batch(PASSES, 1, True)

        def rows_of(a, b):
            index = bass.ds(b, 1) if not isinstance(b, int) else slice(b, b + 1)
            return a[index, :, :].rearrange("o (t p) n -> p (o t) n", p=P)

        @block.sync
        def _(sp):
            open_loop(sp, loop_sems)

            def load(g, u, last=False):
                if last:
                    return
                sp.wait_ge(added, at(g, 2, u - 1))
                sp.wait_ge(biased, at(g, 2, u - 1))
                sp.dma_start(xs[(u + 1) % 2][:, :, :], rows_of(x, 2 * (g - 1) + u + 1)).then_inc(loaded[(u + 1) % 2], 16)

            load(1, -1)
            sp.dma_start(ln_sb[:, :, :], ln_cols).then_inc(cols_loaded, 16)
            sp.dma_start(b1_sb[:, :], b1).then_inc(cols_loaded, 16)
            sp.dma_start(b2_row[:, :], b2.to_broadcast([P, FEAT])).then_inc(cols_loaded, 16)
            for i in range(PIECES):
                if i >= 3:
                    sp.wait_ge(piece_split, i - 2)
                if i < FT:
                    sp.dma_start(stages[i % 3], w1_d[i * P:(i + 1) * P, :]).then_inc(piece_loaded[i % 3], 16)
                else:
                    rows = w2_d[4 * (i - FT) * P:4 * (i - FT + 1) * P, :]
                    sp.dma_start(stages[i % 3].rearrange("p (t n) -> p t n", n=FEAT),
                                 rows.rearrange("(t p) n -> p t n", p=P)).then_inc(piece_loaded[i % 3], 16)
            each_pass(sp, lambda g, u: None, load)

        @block.gpsimd
        def _(pool):
            make_identity(pool, ident, ident_made)
            pool.memset(half_power[:, :], -0.5).then_inc(const_made, 1)
            pool.wait_ge(cols_loaded, 48)
            pool.wait_ge(const_made, 1)

            def split_hidden(g, e, k):
                pool.wait_ge(hid_rounded, at(g, 2 * CHUNKS, e + k))
                pool.tensor_tensor(hid_lo[k % RING][:, :, :], pre[k % RING], hid_hi[k % RING][:, :, :].bitcast(F32),
                                   ALU.subtract).then_inc(hid_split, 1)

            def prepare(g, u):
                pool.wait_ge(counted, at(g, 8, (u + 1) * 4 + 3))
                pool.wait_ge(normalised, at(g, 2, u))
                pool.tensor_tensor(rstd[:, :], var_eps[:, :], half_power[:, :], ALU.pow).then_inc(powered, 1)

            def batch(g, u, last):
                e = u * CHUNKS
                for n in range(CHUNKS + 1):
                    if n == 1:
                        pool.wait_ge(piece_split, PIECES)
                        pool.wait_ge(added, at(g, 2, u - 1))
                        pool.tensor_tensor(xb, xs[u][:, :, :], b2_row[:, :].unsqueeze(1).to_broadcast([P, TT, FEAT]),
                                           ALU.add).then_inc(biased, 1)
                    if n < CHUNKS:
                        pool.wait_ge(squared1, at(g, 2 * CHUNKS, e + n))
                        pool.tensor_tensor(cube[n % RING], cube[n % RING], pre[n % RING], ALU.mult).then_inc(cubed, 1)
                    if n >= 1:
                        split_hidden(g, e, n - 1)
                    if n == 2 and not last:
                        prepare(g, u)

            each_pass(pool, prepare, batch)

        @block.tensor
        def _(pe):
            pe.wait_ge(ident_made, 2)

            def turn(g, u, i):
                pe.wait_ge(turned_kept, at(g, 4, u * 2 + i))
                pe.wait_ge(normalised, at(g, 2, u + 1))
                for j in range(2):
                    f = 2 * i + j
                    for m in range(TT):
                        mm = pe.transpose(ps_t[i][:, j, m * P:(m + 1) * P], xn[:, m, f * P:(f + 1) * P], ident[:, :])
                mm.then_inc(turned, 1)

            def before(g, u):
                turn(g, u, 0)
                turn(g, u, 1)
                pe.wait_ge(piece_split, FT)

            def batch(g, u, last):
                e = u * CHUNKS
                pe.wait_ge(ln_split, at(g, 4, u * 2 + 1))
                for n in range(CHUNKS + Y_LAG):
                    if n < CHUNKS:
                        pe.wait_ge(squared, at(g, 2 * CHUNKS, e + n - 2))
                        for j in range(2):
                            f = 2 * n + j
                            for t in range(FT):
                                for w1, ln in ((w1_lo, ln_hi), (w1_hi, ln_lo), (w1_hi, ln_hi)):
                                    mm = pe.matmul(ps_h[n % 2][:, j, :], w1[:, t, f * P:(f + 1) * P], ln[u][:, t, :],
                                                   start=(t == 0 and w1 is w1_lo),
                                                   stop=(t == FT - 1 and w1 is w1_hi and ln is ln_hi))
                        mm.then_inc(h_summed, 1)
                    if n in TURN_STEPS and not last:
                        turn(g, u, TURN_STEPS.index(n))
                    if n >= Y_LAG:
                        k = n - Y_LAG
                        pe.wait_ge(hid_split, at(g, 2 * CHUNKS, e + k))
                        if k == 0:
                            pe.wait_ge(added, at(g, 2, u - 1))
                            pe.wait_ge(piece_split, PIECES)
                        for j in range(2):
                            f = 2 * k + j
                            for m in range(TT):
                                for hid, w2 in ((hid_hi, w2_lo), (hid_lo, w2_hi), (hid_hi, w2_hi)):
                                    mm = pe.matmul(ps_y[:, m, :], hid[k % RING][:, j, m * P:(m + 1) * P], w2[:, f, :],
                                                   start=(f == 0 and w2 is w2_lo),
                                                   stop=(f == 2 * CHUNKS - 1 and hid is hid_hi and w2 is w2_hi))
                        mm.then_inc(y_used, 1)

            each_pass(pe, before, batch)

        @block.scalar
        def _(act):
            act.wait_ge(cols_loaded, 48)

            def keep_turned(g, u, i):
                act.wait_ge(turned, at(g, 4, (u + 1) * 2 + i))
                act.wait_ge(ln_split, at(g, 4, u * 2 + i))
                for j in range(2):
                    f = 2 * i + j
                    ins = act.activation(ln_raw[:, f, :], ps_t[i][:, j, :], ACT.Identity, bias=ln_sb[:, 1, f:f + 1],
                                         scale=ln_sb[:, 0, f:f + 1])
                ins.then_inc(turned_kept, 1)

            def before(g, u):
                keep_turned(g, u, 0)
                keep_turned(g, u, 1)
                for i in range(PIECES):
                    act.wait_ge(piece_loaded[i % 3], 16 * (i // 3 + 1))
                    act.activation(piece_of(i, 0), stages[i % 3], ACT.Copy).then_inc(piece_hi, 1)
                act.wait_ge(piece_split, PIECES)

            def batch(g, u, last):
                e = u * CHUNKS
                for n in range(CHUNKS + 1):
                    if n < CHUNKS:
                        act.wait_ge(h_summed, at(g, 2 * CHUNKS, e + n))
                        act.wait_ge(hid_split, at(g, 2 * CHUNKS, e + n - RING))
                        for j in range(2):
                            act.activation(pre[n % RING][:, j, :], ps_h[n % 2][:, j, :], ACT.Identity,
                                           bias=b1_sb[:, 2 * n + j:2 * n + j + 1])
                        for j in range(2):
                            ins = act.activation(cube[n % RING][:, j, :], ps_h[n % 2][:, j, :], ACT.Square,
                                                 bias=b1_sb[:, 2 * n + j:2 * n + j + 1])
                        ins.then_inc(squared, 1)
                    if 1 <= n <= CHUNKS:
                        k = n - 1
                        act.wait_ge(cubed, at(g, 2 * CHUNKS, e + k))
                        act.activation(cube[k % RING], cube[k % RING], ACT.Tanh, scale=0.7978845608028654).then_inc(bent, 1)
                    if n >= 1:
                        k = n - 1
                        act.wait_ge(gelled, at(g, 2 * CHUNKS, e + k))
                        act.wait_ge(y_used, at(g, 2 * CHUNKS, e + k - RING))
                        act.activation(hid_hi[k % RING][:, :, :], pre[k % RING], ACT.Copy).then_inc(hid_rounded, 1)
                    if n in TURN_STEPS and not last:
                        keep_turned(g, u, TURN_STEPS.index(n))
                act.wait_ge(added, at(g, 2, u))
                act.dma_start(rows_of(out, 2 * (g - 1) + u), res).then_inc(stored, 16)

            each_pass(act, before, batch)
            act.wait_ge(stored, 16 * (BATCH + 2))

        @block.vector
        def _(dve):
            def statistics(g, u):
                s = (u + 1) % 2
                dve.wait_ge(loaded[s], (g + (u + 1) // 2) * 16)
                for m in range(TT):
                    ins = dve.bn_stats(stats[:, m, :], xs[s][:, m, :])
                ins.then_inc(counted, 1)

            def moment(g, u):
                dve.wait_ge(counted, at(g, 8, (u + 1) * 4))
                dve.tensor_copy(var_eps[:, :], stats[:, :, 2]).then_inc(counted, 1)
                for m in range(TT):
                    ins = dve.bn_aggr(moments[:, m, :], stats[:, m, :])
                ins.then_inc(counted, 1)
                dve.wait_ge(counted, at(g, 8, (u + 1) * 4 + 2))
                dve.tensor_scalar(var_eps[:, :], moments[:, :, 1], 1e-5, None, ALU.add).then_inc(counted, 1)

            def normalise(g, u):
                s = (u + 1) % 2
                dve.wait_ge(powered, at(g, 2, u + 1))
                dve.wait_ge(turned, at(g, 4, u * 2 + 1))
                for m in range(TT):
                    ins = dve.tensor_scalar(xn[:, m, :], xs[s][:, m, :], moments[:, m, 0:1], rstd[:, m:m + 1],
                                            ALU.subtract, ALU.mult)
                ins.then_inc(normalised, 1)

            def split_turned(g, u, i):
                s, here = (u + 1) % 2, slice(2 * i, 2 * i + 2)
                dve.wait_ge(turned_kept, at(g, 4, (u + 1) * 2 + i))
                dve.tensor_copy(ln_hi[s][:, here, :], ln_raw[:, here, :]).then_inc(ln_rounded, 1)
                dve.wait_ge(ln_rounded, at(g, 4, (u + 1) * 2 + i))
                dve.tensor_tensor(ln_lo[s][:, here, :], ln_raw[:, here, :], ln_hi[s][:, here, :].bitcast(F32),
                                  ALU.subtract).then_inc(ln_split, 1)

            def before(g, u):
                statistics(g, u)
                moment(g, u)
                normalise(g, u)
                split_turned(g, u, 0)
                split_turned(g, u, 1)
                for i in range(PIECES):
                    dve.wait_ge(piece_hi, i + 1)
                    dve.tensor_tensor(piece_of(i, 1), stages[i % 3], piece_of(i, 0).bitcast(F32),
                                      ALU.subtract).then_inc(piece_split, 1)

            def batch(g, u, last):
                e = u * CHUNKS
                for n in range(CHUNKS + 1):
                    if n < CHUNKS:
                        dve.wait_ge(squared, at(g, 2 * CHUNKS, e + n))
                        dve.tensor_scalar(cube[n % RING], cube[n % RING], 0.044715, 1.0, ALU.mult, ALU.add).then_inc(squared1, 1)
                    if n >= 1:
                        k = n - 1
                        dve.wait_ge(bent, at(g, 2 * CHUNKS, e + k))
                        dve.scalar_tensor_tensor(out=pre[k % RING], in0=cube[k % RING], scalar=1.0,
                                                 in1=pre[k % RING], op0=ALU.add, op1=ALU.mult).then_inc(gelled, 1)
                    if n == 1 and not last:
                        statistics(g, u)
                    if n == 2 and not last:
                        moment(g, u)
                    if n == 3 and not last:
                        normalise(g, u)
                    if n - 1 in TURN_STEPS and not last:
                        split_turned(g, u, TURN_STEPS.index(n - 1))
                dve.wait_ge(y_used, at(g, 2 * CHUNKS, e + CHUNKS - 1))
                dve.wait_ge(biased, at(g, 2, u))
                dve.wait_ge(stored, at(g, 2, u - 1, 16))
                dve.scalar_tensor_tensor(out=res, in0=ps_y[:, :, :], scalar=0.5, in1=xb,
                                         op0=ALU.mult, op1=ALU.add).then_inc(added, 1)

            each_pass(dve, before, batch)


def recurrent_block(nc, semaphores, x, state, w, cols, maa_w1, maa_w2, td_w1, td_w2, select, spread, head_sum, group_mean, out):
    GROUP = 16
    MIX = 32
    DECAY = td_w1.shape[1]
    WEIGHTS = ("r", "k", "v", "g", "o", "fk", "fr", "fv")
    A_UNITS = ("T0", "T1", "XX", "Mw0", "Mw1", "Mk0", "Mk1", "D1", "K0", "D20", "D21", "K1", "Mv0", "Mv1", "V0", "V1",
               "Mr0", "Mr1", "R0", "R1", "Mg0", "Mg1", "G0", "G1")
    Z_UNITS = ("C0", "C1", "E0", "E1", "Q0", "Q1", "O0", "O1", "T0", "T1", "FK0", "FK1", "FR0", "FR1", "FV0", "FV1")
    MIXED = "wkvrg"
    NA, NZ = len(A_UNITS), len(Z_UNITS)
    SCHEDULE = (
        "A:LS L:G0 A:LN", "Z:E0 L:G1 Z:E1", "A:T0 Z:Q0 A:T1 Z:Q1", "A:SX Z:I0", "A:XX Z:I1",
        "A:Mw0 Z:N1 A:Mw1 Z:N2 A:Mk0 A:Mk1", "A:D1 Z:N3 A:K0", "A:D20 Z:O0 A:D21 Z:O1 A:K1 Z:LS",
        "A:Mv0 A:Mv1 Z:LN", "Z:T0 A:V0 Z:T1 Z:X", "A:V1 Z:FK0", "A:Mr0 Z:FK1 A:Mr1", "Z:FR0 A:R0", "A:R1 Z:FR1",
        "C:P A:Mg0 Z:FV0 A:Mg1", "Z:FV1 C:C0 C:C1")
    STEPS = GROUP
    with ExitStack() as ctx:
        def sb(name, shape, dtype=F32):
            return ctx.enter_context(nc.sbuf_tensor("rec_" + name, shape, dtype))

        def ps(name, shape):
            return ctx.enter_context(nc.psum_tensor("rec_" + name, shape, F32))

        loop_sems = []

        def sem(name, per_batch=0):
            s = semaphores.allocate("rec_" + name)
            if per_batch:
                loop_sems.append((s, 2 * per_batch))
            return s

        def of(b, per_batch, k, unit=1):
            return at(b + 2, per_batch, k, unit)

        wt = {n: sb("w_" + n, [P, FT, FEAT]) for n in WEIGHTS}
        m1 = sb("m1", [P, FT, 5 * MIX])
        m2a, t1, t2_m2b = sb("m2a", [P, FEAT]), sb("t1", [P, FT, DECAY]), sb("t2_m2b", [DECAY + MIX, FEAT])
        t2, m2b = t2_m2b[0:DECAY, :], t2_m2b[DECAY:DECAY + MIX, :]
        sel, spr, ones = sb("sel", [P, GROUP, P], F32R), sb("spr", [P, (2 * GROUP - 1) * (P // GROUP)]), sb("ones", [P, P])
        mean_of = sb("mean_of", [P, P])
        NC = 16
        col = sb("cols", [P, NC, FT])
        LN1_W, LN1_B, LN2_W, LN2_B, MAA_X, DECAY0, U, GN_W, GN_B, FFN_K, FFN_R, STACK = range(12)
        ident, half_power = sb("ident", [P, P]), sb("half_power", [P, TT])

        xin = sb("xin", [P, TT, FEAT])
        stats, moments, var_eps, rstd = ([sb(f"{n}{i}", sh) for i in "az"] for n, sh in
                                         (("stats", [P, TT, 6]), ("moments", [P, TT, 2]), ("var_eps", [P, TT]), ("rstd", [P, TT])))
        st = [sb(f"st{u}", [P, FT, 2 + GROUP]) for u in range(2)]
        edge = sb("edge", [P, FT, 2])
        xaT, sx = sb("xaT", [P, FT, TOK + 1]), sb("sx", [P, FT, TOK])
        xm = [sb(f"xm{i}", [P, FT, TOK]) for i in range(2)]
        xxT, tdT_xx4 = sb("xxT", [P, TOK]), sb("tdT_xx4", [DECAY + MIX, TOK])
        tdT, xx4 = tdT_xx4[0:DECAY, :], tdT_xx4[DECAY:DECAY + MIX, :]
        rT, kT, g2 = ([sb(f"{n}{u}", [P, FT, TOK]) for u in range(2)] for n in ("rT", "kT", "g2"))
        v_hi, v_lo = ([sb(f"{n}{u}", [P, FT, TOK], F32R) for u in range(2)] for n in ("v_hi", "v_lo"))
        wE = [sb(f"wE{u}", [P, FT, TOK + 1]) for u in range(2)]
        kvE = [sb(f"kvE{i}", [P, FT, TOK + 1]) for i in range(2)]
        sE = [sb(f"sE{i}", [P, FT, TOK + 1]) for i in range(2)]
        rs = [sb(f"rs{i}", [P, FT, TOK]) for i in range(2)]
        og, sq = sb("og", [P, FT, TOK]), sb("sq", [P, FT, TOK])
        xres = sb("xres", [P, TT, FEAT])
        xcT, sx2, xk2, xr2 = sb("xcT", [P, FT, TOK + 1]), sb("sx2", [P, FT, TOK]), sb("xk2", [P, FT, TOK]), sb("xr2", [P, FT, TOK])
        kk, ruk = og, xr2
        sq_rows = sq[:, :, :].rearrange("p (m a) n -> p m (a n)", m=TT)

        ps_v = [ps(f"ps_v{i}", [P, FT, TOK]) for i in range(2)]
        ps_acc = ps("ps_acc", [P, FT, TOK])
        ps_a, ps_z = ps("ps_a", [P, 2, TOK]), ps("ps_z", [P, 2, TOK])

        w_loaded, ident_made, const_made = sem("w_loaded"), sem("ident_made"), sem("const_made")
        x_loaded, st_loaded, z_loaded, stored = sem("x_loaded"), sem("st_loaded"), sem("z_loaded"), sem("stored", 16)
        a_filled, a_kept, z_filled, z_kept = sem("a_filled", NA), sem("a_kept", NA), sem("z_filled", NZ), sem("z_kept", NZ)
        counted = [sem(f"counted_{i}", 4) for i in "az"]
        powered = [sem(f"powered_{i}", 1) for i in "az"]
        normalised = [sem(f"normalised_{i}", 1) for i in "az"]
        shifted, mixed_x, mixtures, decayed, g_bent, v_hi_kept = (
            sem("shifted", 1), sem("mixed_x", 1), sem("mixtures", 5), sem("decayed", 1), sem("g_bent", 2), sem("v_hi_kept", 2))
        spread_v, kv_made, seeded, scanned, rs_made, summed = (
            sem(n, STEPS) for n in ("spread_v", "kv_made", "seeded", "scanned", "rs_made", "summed"))
        ruk_made, v_joined, og_made = sem("ruk_made", 2), sem("v_joined", 2), sem("og_made", 1)
        sel_loaded, sel_made, a_w_loaded, z_w_loaded = (sem(n) for n in ("sel_loaded", "sel_made", "a_w_loaded", "z_w_loaded"))
        squared, inverted, rooted, og_scaled, og_affine, gated = (
            sem("squared", 2), sem("inverted", 2), sem("rooted", 1), sem("og_scaled", 1), sem("og_affine", 1), sem("gated", 1))
        shifted2, mixed2, kk_made, res_made = sem("shifted2", 1), sem("mixed2", 2), sem("kk_made", 1), sem("res_made", 2)
        W_LOADS = 9

        block = ctx.enter_context(nc.Block())

        def run(eng, step, a_unit, z_unit, c_unit, inner):
            names = " ".join(SCHEDULE).split()

            def body(b, s, with_z, with_a):
                for j in range(STEPS):
                    step(b, s, j, with_a)
                    for n, name in enumerate(SCHEDULE[j].split()):
                        if n == 1:
                            inner(b, s, j, with_z)
                        stage, unit = name.split(":")
                        if stage == "A" and with_a:
                            a_unit(b + 1, 1 - s, unit)
                        elif stage == "Z" and with_z:
                            z_unit(b - 1, 1 - s, unit)
                        elif stage == "L":
                            a_unit(b, s, unit)
                        elif stage == "C":
                            c_unit(b, s, unit)

            for name in names:
                if name.startswith("A:"):
                    a_unit(0, 0, name[2:])
            step(-1, 1, STEPS - 1, True)
            body(0, 0, False, True)
            with eng.Fori(1, BATCH // 2) as p:
                body(2 * p - 1, 1, True, True)
                body(2 * p, 0, True, True)
            body(BATCH - 1, 1, True, False)
            inner(BATCH, 0, 0, True)
            for name in names:
                if name.startswith("Z:"):
                    z_unit(BATCH - 1, 1, name[2:])

        def batch_of(a, b):
            return a[bass.ds(b, 1) if not isinstance(b, int) else slice(b, b + 1)]

        def token_rows(a, b):
            return batch_of(a, b).rearrange("o (t p) n -> p (o t) n", p=P)

        def feature_rows(a, b):
            return batch_of(a, b).rearrange("o p t n -> p (o t) n")

        def a_at(unit):
            return A_UNITS.index(unit)

        def z_at(unit):
            return Z_UNITS.index(unit)

        NOTHING = lambda *_: None

        @block.sync
        def _(sp):
            open_loop(sp, loop_sems)

            def load_x(b):
                sp.wait_ge(a_filled, of(b - 1, NA, a_at("T1")))
                sp.dma_start(xin[:, :, :], token_rows(x, b)).then_inc(x_loaded, 16)

            def load_st(b, s):
                sp.wait_ge(og_made, of(b - 2, 1, 0))
                sp.dma_start(st[s][:, :, :], feature_rows(state, b)).then_inc(st_loaded, 16)

            def load_z(b):
                sp.wait_ge(stored, of(b - 1, 1, 0, 16))
                sp.wait_ge(z_kept, of(b - 1, NZ, z_at("T0")))
                sp.dma_start(xres[:, :, :], token_rows(x, b)).then_inc(z_loaded, 16)
                sp.dma_start(edge[:, :, :], feature_rows(state, b)[:, :, 0:2]).then_inc(z_loaded, 16)

            def store(b):
                sp.wait_ge(res_made, of(b, 2, 1))
                sp.dma_start(token_rows(out, b), xres[:, :, :]).then_inc(stored, 16)

            load_x(0)
            load_st(0, 0)
            sp.dma_start(col[:, :, :], cols).then_inc(w_loaded, 16)
            sp.dma_start(m1[:, :, :], maa_w1.rearrange("(t p) n -> p t n", p=P)).then_inc(w_loaded, 16)
            sp.dma_start(m2a[:, :], maa_w2[0:P, :]).then_inc(w_loaded, 16)
            sp.dma_start(m2b, maa_w2[P:P + MIX, :]).then_inc(w_loaded, 16)
            sp.dma_start(t1[:, :, :], td_w1.rearrange("(t p) n -> p t n", p=P)).then_inc(w_loaded, 16)
            sp.dma_start(t2, td_w2).then_inc(w_loaded, 16)
            sp.dma_start(spr[:, :], spread).then_inc(w_loaded, 16)
            sp.dma_start(ones[:, :], head_sum).then_inc(w_loaded, 16)
            sp.dma_start(mean_of[:, :], group_mean).then_inc(w_loaded, 16)
            for n in "kvrg":
                sp.dma_start(wt[n][:, :, :], w[n].rearrange("(t p) n -> p t n", p=P)).then_inc(a_w_loaded, 16)
            for h in range(2):
                sp.dma_start(rs[h][:, :, :].rearrange("p c t -> p (c t)"),
                             select[:, h * 8:(h + 1) * 8, :].rearrange("p j n -> p (j n)")).then_inc(sel_loaded, 16)
            for n in WEIGHTS[4:]:
                sp.dma_start(wt[n][:, :, :], w[n].rearrange("(t p) n -> p t n", p=P)).then_inc(z_w_loaded, 16)
            load_x(1)
            load_st(1, 1)
            load_x(2)
            load_st(2, 0)

            def body(b, s, ahead=True):
                load_z(b - 1)
                if ahead:
                    load_x(b + 2)
                store(b - 1)
                if ahead:
                    load_st(b + 2, s)

            for b in range(1, BATCH):
                body(b, b % 2, b + 2 < BATCH)
            load_z(BATCH - 1)
            store(BATCH - 1)
            sp.wait_ge(stored, 16 * (BATCH + 2))

        @block.gpsimd
        def _(pool):
            make_identity(pool, ident, ident_made)
            pool.memset(half_power[:, :], -0.5).then_inc(const_made, 1)
            pool.memset(wE[0][:, :, 0], 0.0).then_inc(const_made, 1)
            pool.memset(wE[1][:, :, 0], 0.0).then_inc(const_made, 1)
            pool.wait_ge(w_loaded, 16 * W_LOADS)
            pool.wait_ge(const_made, 3)

            def power(i, b):
                pool.wait_ge(counted[i], of(b, 4, 3))
                pool.wait_ge(normalised[i], of(b - 1, 1, 0))
                pool.tensor_tensor(rstd[i][:, :], var_eps[i][:, :], half_power[:, :], ALU.pow).then_inc(powered[i], 1)

            def a_unit(b, s, unit):
                if unit == "LS":
                    power(0, b)
                elif unit[0] == "M" and unit[2] == "1":
                    o = MIXED.index(unit[1])
                    pool.wait_ge(a_kept, of(b, NA, a_at(unit)))
                    pool.tensor_tensor(xm[(o + 1) % 2][:, :, :], xm[(o + 1) % 2][:, :, :], xaT[:, :, 1:TOK + 1],
                                       ALU.add).then_inc(mixtures, 1)

            def z_unit(b, s, unit):
                if unit == "N1":
                    pool.wait_ge(rooted, of(b, 1, 0))
                    pool.tensor_tensor(og[:, :, :], og[:, :, :], sq[:, :, :], ALU.mult).then_inc(og_scaled, 1)
                elif unit == "LS":
                    power(1, b)
                elif unit == "X":
                    pool.wait_ge(z_kept, of(b, NZ, z_at("T1")))
                    pool.wait_ge(mixed2, of(b - 1, 2, 1))
                    pool.tensor_tensor(sx2[:, :, :], xcT[:, :, 0:TOK], xcT[:, :, 1:TOK + 1], ALU.subtract).then_inc(shifted2, 1)
                elif unit == "FK1":
                    pool.wait_ge(z_kept, of(b, NZ, z_at("FK1")))
                    pool.tensor_tensor(kk[:, :, :], kk[:, :, :], kk[:, :, :], ALU.mult).then_inc(kk_made, 1)

            def c_unit(b, s, unit):
                if unit == "P":
                    pool.wait_ge(a_kept, of(b, NA, a_at("R1")))
                    pool.wait_ge(z_filled, of(b - 1, NZ, z_at("FR1")))
                    pool.tensor_tensor(ruk[:, :, :], rT[s][:, :, :], kT[s][:, :, :], ALU.mult).then_inc(ruk_made, 1)
                    pool.wait_ge(ruk_made, of(b, 2, 0))
                    pool.tensor_tensor(ruk[:, :, :], ruk[:, :, :], col[:, U, :].unsqueeze(2).to_broadcast([P, FT, TOK]),
                                       ALU.mult).then_inc(ruk_made, 1)

            def step(b, s, j, _):
                if isinstance(b, int) and b < 0:
                    pool.wait_ge(sel_loaded, 32)
                    for h in range(2):
                        pool.tensor_copy(sel[:, h * 8:(h + 1) * 8, :].rearrange("p j n -> p (j n)"),
                                         rs[h][:, :, :].rearrange("p c t -> p (c t)")).then_inc(sel_made, 1)
                    return
                if j == 0:
                    pool.wait_ge(a_kept, of(b, NA, a_at("R1")))
                if isinstance(b, int) and b == 0 and j == 0:
                    pool.wait_ge(sel_made, 2)
                pool.wait_ge(scanned, of(b, STEPS, j))
                pool.wait_ge(summed, of(b, STEPS, j - 2))
                pool.tensor_tensor(rs[j % 2][:, :, :], sE[j % 2][:, :, 0:TOK], rT[s][:, :, :], ALU.mult).then_inc(rs_made, 1)

            run(pool, step, a_unit, z_unit, c_unit, NOTHING)

        @block.tensor
        def _(pe):
            pe.wait_ge(ident_made, 2)
            pe.wait_ge(w_loaded, 16 * W_LOADS)

            def transpose_rows(bank, rows, half):
                for j in range(2):
                    f = 2 * half + j
                    for m in range(TT):
                        mm = pe.transpose(bank[:, j, m * P:(m + 1) * P], rows[:, m, f * P:(f + 1) * P], ident[:, :])
                return mm

            def to_features(bank, weight, src, half):
                for j in range(2):
                    f = 2 * half + j
                    for t in range(FT):
                        mm = pe.matmul(bank[:, j, :], weight[:, t, f * P:(f + 1) * P], src[:, t, :],
                                       start=(t == 0), stop=(t == FT - 1))
                return mm

            def to_tokens(bank, weight, src, m):
                for t in range(FT):
                    mm = pe.matmul(bank[:, :, :], src[:, t, m * P:(m + 1) * P], weight[:, t, :],
                                   start=(t == 0), stop=(t == FT - 1))
                return mm

            def a_unit(b, s, unit):
                if unit in ("LS", "LN", "SX"):
                    return
                pe.wait_ge(a_kept, of(b, NA, a_at(unit) - 1))
                half = int(unit[-1]) if unit[-1] in "01" else 0
                if unit[0] == "T":
                    pe.wait_ge(normalised[0], of(b, 1, 0))
                    mm = transpose_rows(ps_a, xin, half)
                elif unit == "XX":
                    pe.wait_ge(mixed_x, of(b, 1, 0))
                    for j, rows in enumerate((P, MIX)):
                        for t in range(FT):
                            mm = pe.matmul(ps_a[0:rows, j, :], m1[:, t, j * P:j * P + rows], xm[0][:, t, :],
                                           start=(t == 0), stop=(t == FT - 1))
                elif unit[0] == "M":
                    f = "kwvrg".index(unit[1])
                    if unit == "Mw0":
                        pe.wait_ge(a_kept, of(b, NA, a_at("XX")))
                    r = slice(f * MIX, (f + 1) * MIX) if f < 4 else slice(0, MIX)
                    w2, xx = (m2a, xxT) if f < 4 else (m2b, xx4)
                    for j in range(2):
                        c = 2 * half + j
                        mm = pe.matmul(ps_a[:, j, :], w2[r, c * P:(c + 1) * P], xx[r, :], start=True, stop=True)
                elif unit == "D1":
                    pe.wait_ge(mixtures, of(b, 5, 0))
                    for t in range(FT):
                        mm = pe.matmul(ps_a[0:DECAY, 0, :], t1[:, t, :], xm[1][:, t, :], start=(t == 0), stop=(t == FT - 1))
                elif unit[:2] == "D2":
                    pe.wait_ge(a_kept, of(b, NA, a_at("D1")))
                    for j in range(2):
                        c = 2 * half + j
                        mm = pe.matmul(ps_a[:, j, :], t2[:, c * P:(c + 1) * P], tdT, start=True, stop=True)
                else:
                    if unit == "K0" and isinstance(b, int) and b == 0:
                        pe.wait_ge(a_w_loaded, 64)
                    elif unit == "K0" and isinstance(b, int) and b == 1:
                        pe.wait_ge(z_w_loaded, 64)
                    o = MIXED.index(unit[0].lower())
                    pe.wait_ge(mixtures, of(b, 5, o))
                    mm = to_features(ps_a, wt[unit[0].lower()], xm[(o + 1) % 2], half)
                mm.then_inc(a_filled, 1)

            def z_unit(b, s, unit):
                if unit not in Z_UNITS:
                    return
                pe.wait_ge(z_kept, of(b, NZ, z_at(unit) - 1))
                half = int(unit[-1])
                if unit[0] == "E":
                    pe.wait_ge(og_made, of(b, 1, 0))
                    mm = pe.matmul(ps_z[:, :, :], mean_of[:, :], og[:, 2 * half:2 * half + 2, :], start=True, stop=True)
                elif unit[0] == "Q":
                    pe.wait_ge(squared, of(b, 2, half))
                    mm = pe.matmul(ps_z[:, :, :], mean_of[:, :], sq[:, 2 * half:2 * half + 2, :], start=True, stop=True)
                elif unit[0] == "O":
                    pe.wait_ge(gated, of(b, 1, 0))
                    mm = to_tokens(ps_z, wt["o"], og, half)
                elif unit[0] == "T":
                    pe.wait_ge(normalised[1], of(b, 1, 0))
                    mm = transpose_rows(ps_z, sq_rows, half)
                elif unit[:2] == "FK":
                    pe.wait_ge(mixed2, of(b, 2, 0))
                    mm = to_features(ps_z, wt["fk"], xk2, half)
                elif unit[:2] == "FR":
                    pe.wait_ge(mixed2, of(b, 2, 1))
                    mm = to_tokens(ps_z, wt["fr"], xr2, half)
                elif unit[:2] == "FV":
                    pe.wait_ge(kk_made, of(b, 1, 0))
                    mm = to_tokens(ps_z, wt["fv"], kk, half)
                mm.then_inc(z_filled, 1)

            def c_unit(b, s, unit):
                if unit == "P":
                    return
                half = int(unit[1])
                pe.wait_ge(z_kept, of(b - 1, NZ, NZ - 1) if half == 0 else of(b, NZ, 0))
                pe.wait_ge(ruk_made, of(b, 2, 1))
                pe.matmul(ps_z[:, :, :], ones[:, :], ruk[:, 2 * half:2 * half + 2, :], start=True, stop=True).then_inc(z_filled, 1)

            def spread(b, s, j):
                if j == 0:
                    pe.wait_ge(a_kept, of(b, NA, a_at("V1")))
                pe.wait_ge(kv_made, of(b, STEPS, j - 2))
                if isinstance(b, int) and b == 0 and j == 0:
                    pe.wait_ge(sel_made, 2)
                for half in range(2):
                    for part in (v_lo, v_hi):
                        mm = pe.matmul(ps_v[j % 2][:, 2 * half:2 * half + 2, :], sel[:, j, :],
                                       part[s][:, 2 * half:2 * half + 2, :], start=part is v_lo, stop=part is v_hi)
                mm.then_inc(spread_v, 1)

            def sum_rows(b, j):
                pe.wait_ge(rs_made, of(b, STEPS, j))
                if j == 0:
                    pe.wait_ge(og_made, of(b - 1, 1, 0))
                i = (GROUP - 1 - j) * (P // GROUP)
                for half in range(2):
                    mm = pe.matmul(ps_acc[:, 2 * half:2 * half + 2, :], spr[:, i:i + P],
                                   rs[j % 2][:, 2 * half:2 * half + 2, :], start=(j == 0), stop=(j == STEPS - 1))
                mm.then_inc(summed, 1)

            def step(b, s, j, batch_follows):
                if j < STEPS - 1:
                    spread(b, s, j + 1)
                elif batch_follows:
                    spread(b + 1, 1 - s, 0)

            def inner(b, s, j, batch_before):
                if j > 0:
                    sum_rows(b, j - 1)
                elif batch_before:
                    sum_rows(b - 1, STEPS - 1)

            run(pe, step, a_unit, z_unit, c_unit, inner)

        @block.scalar
        def _(act):
            act.wait_ge(w_loaded, 16 * W_LOADS)

            def a_unit(b, s, unit):
                if unit in ("LS", "LN", "SX") or unit[0] == "M":
                    return
                half = int(unit[-1]) if unit[-1] in "01" else 0
                if unit == "T0":
                    act.wait_ge(og_made, of(b - 2, 1, 0))
                    act.wait_ge(mixtures, of(b - 1, 5, 4))
                elif unit == "T1":
                    act.wait_ge(st_loaded, (b + 1) * 16)
                    act.activation(xaT[:, :, 0], st[s][:, :, 1], ACT.Copy)
                act.wait_ge(a_filled, of(b, NA, a_at(unit)))
                if unit[0] == "T":
                    for j in range(2):
                        c = 2 * half + j
                        ins = act.activation(xaT[:, c, 1:TOK + 1], ps_a[:, j, :], ACT.Identity, bias=col[:, LN1_B, c:c + 1],
                                             scale=col[:, LN1_W, c:c + 1])
                elif unit == "XX":
                    act.activation(xxT[:, :], ps_a[:, 0, :], ACT.Tanh)
                    ins = act.activation(xx4, ps_a[0:MIX, 1, :], ACT.Tanh)
                elif unit == "D1":
                    ins = act.activation(tdT, ps_a[0:DECAY, 0, :], ACT.Tanh)
                elif unit[:2] == "D2":
                    for j in range(2):
                        c = 2 * half + j
                        ins = act.activation(wE[s][:, c, 1:TOK + 1], ps_a[:, j, :], ACT.Exp, bias=col[:, DECAY0, c:c + 1])
                elif unit[0] == "G":
                    if half == 0:
                        act.wait_ge(gated, of(b - 2, 1, 0))
                    act.activation(g2[s][:, 2 * half:2 * half + 2, :], ps_a[:, :, :], ACT.Tanh, scale=0.5).then_inc(g_bent, 1)
                    return
                elif unit[0] == "V":
                    act.activation(v_hi[s][:, 2 * half:2 * half + 2, :], ps_a[:, :, :], ACT.Copy).then_inc(v_hi_kept, 1)
                    return
                else:
                    dst = {"R": rT, "K": kT}[unit[0]][s]
                    ins = act.activation(dst[:, 2 * half:2 * half + 2, :], ps_a[:, :, :], ACT.Copy)
                ins.then_inc(a_kept, 1)
                if unit == "D21":
                    act.wait_ge(a_kept, of(b, NA, a_at("D21")))
                    act.activation(wE[s][:, :, 1:TOK + 1], wE[s][:, :, 1:TOK + 1], ACT.Exp, scale=-1.0).then_inc(decayed, 1)

            def z_unit(b, s, unit):
                if unit[0] == "E":
                    half = int(unit[1])
                    act.wait_ge(z_kept, of(b, NZ, z_at(unit)))
                    act.wait_ge(res_made, of(b - 1, 2, 1))
                    act.activation(sq[:, 2 * half:2 * half + 2, :], og[:, 2 * half:2 * half + 2, :], ACT.Square).then_inc(squared, 1)
                elif unit == "N1":
                    act.wait_ge(inverted, of(b, 2, 1))
                    act.activation(sq[:, :, :], sq[:, :, :], ACT.Sqrt).then_inc(rooted, 1)
                elif unit == "N2":
                    act.wait_ge(og_scaled, of(b, 1, 0))
                    for c in range(FT):
                        ins = act.activation(og[:, c, :], og[:, c, :], ACT.Identity, bias=col[:, GN_B, c:c + 1],
                                             scale=col[:, GN_W, c:c + 1])
                    ins.then_inc(og_affine, 1)
                elif unit[0] == "T":
                    half = int(unit[1])
                    if half == 0:
                        act.wait_ge(mixed2, of(b - 1, 2, 1))
                        act.wait_ge(z_loaded, (b + 1) * 32)
                        act.activation(xcT[:, :, 0], edge[:, :, 0], ACT.Copy)
                    act.wait_ge(z_filled, of(b, NZ, z_at(unit)))
                    for j in range(2):
                        c = 2 * half + j
                        ins = act.activation(xcT[:, c, 1:TOK + 1], ps_z[:, j, :], ACT.Identity, bias=col[:, LN2_B, c:c + 1],
                                             scale=col[:, LN2_W, c:c + 1])
                    ins.then_inc(z_kept, 1)
                elif unit[:2] == "FK":
                    half = int(unit[2])
                    act.wait_ge(z_filled, of(b, NZ, z_at(unit)))
                    act.activation(kk[:, 2 * half:2 * half + 2, :], ps_z[:, :, :], ACT.Relu).then_inc(z_kept, 1)
                elif unit[:2] == "FR":
                    m = int(unit[2])
                    act.wait_ge(z_filled, of(b, NZ, z_at(unit)))
                    act.activation(sq_rows[:, m, :], ps_z[:, :, :].rearrange("p a n -> p (a n)"), ACT.Tanh, scale=0.5).then_inc(z_kept, 1)

            def step(b, s, j, _):
                if not (isinstance(b, int) and b < 0):
                    act.wait_ge(scanned, of(b, STEPS, j - 2))
                    act.activation(kvE[j % 2][:, :, 0], st[s][:, :, 2 + j], ACT.Copy).then_inc(seeded, 1)

            run(act, step, a_unit, z_unit, NOTHING, NOTHING)

        @block.vector
        def _(dve):
            dve.wait_ge(w_loaded, 16 * W_LOADS)
            dve.wait_ge(const_made, 3)

            def statistics(i, b, rows):
                for m in range(TT):
                    ins = dve.bn_stats(stats[i][:, m, :], rows[:, m, :])
                ins.then_inc(counted[i], 1)
                dve.wait_ge(counted[i], of(b, 4, 0))
                dve.tensor_copy(var_eps[i][:, :], stats[i][:, :, 2]).then_inc(counted[i], 1)
                for m in range(TT):
                    ins = dve.bn_aggr(moments[i][:, m, :], stats[i][:, m, :])
                ins.then_inc(counted[i], 1)
                dve.wait_ge(counted[i], of(b, 4, 2))
                dve.tensor_scalar(var_eps[i][:, :], moments[i][:, :, 1], 1e-5, None, ALU.add).then_inc(counted[i], 1)

            def normalise(i, b, dst, rows):
                dve.wait_ge(powered[i], of(b, 1, 0))
                for m in range(TT):
                    ins = dve.tensor_scalar(dst[:, m, :], rows[:, m, :], moments[i][:, m, 0:1], rstd[i][:, m:m + 1],
                                            ALU.subtract, ALU.mult)
                ins.then_inc(normalised[i], 1)

            def a_unit(b, s, unit):
                if unit == "LS":
                    dve.wait_ge(x_loaded, (b + 1) * 16)
                    statistics(0, b, xin)
                elif unit == "LN":
                    normalise(0, b, xin, xin)
                elif unit == "SX":
                    dve.wait_ge(a_kept, of(b, NA, a_at("T1")))
                    dve.tensor_tensor(sx[:, :, :], xaT[:, :, 0:TOK], xaT[:, :, 1:TOK + 1], ALU.subtract).then_inc(shifted, 1)
                    dve.wait_ge(shifted, of(b, 1, 0))
                    dve.wait_ge(a_filled, of(b - 1, NA, a_at("R1")))
                    for c in range(FT):
                        ins = dve.scalar_tensor_tensor(out=xm[0][:, c, :], in0=sx[:, c, :], scalar=col[:, MAA_X, c:c + 1],
                                                       in1=xaT[:, c, 1:TOK + 1], op0=ALU.mult, op1=ALU.add)
                    ins.then_inc(mixed_x, 1)
                elif unit[0] == "M":
                    half, o, f = int(unit[2]), MIXED.index(unit[1]), "kwvrg".index(unit[1])
                    dve.wait_ge(a_filled, of(b, NA, a_at(unit)))
                    if half == 0:
                        reader = (a_at("G1") - NA, a_at("XX"), a_at("D1"), a_at("K1"), a_at("V1"))[o]
                        dve.wait_ge(a_filled, of(b, NA, reader))
                    for j in range(2):
                        c = 2 * half + j
                        ins = dve.scalar_tensor_tensor(out=xm[(o + 1) % 2][:, c, :], in0=ps_a[:, j, :],
                                                       scalar=col[:, STACK + f, c:c + 1], in1=sx[:, c, :],
                                                       op0=ALU.add, op1=ALU.mult)
                    ins.then_inc(a_kept, 1)
                elif unit[0] == "V":
                    half = int(unit[1])
                    here = slice(2 * half, 2 * half + 2)
                    dve.wait_ge(v_hi_kept, of(b, 2, half))
                    dve.tensor_tensor(v_lo[s][:, here, :], ps_a[:, :, :], v_hi[s][:, here, :].bitcast(F32),
                                      ALU.subtract).then_inc(a_kept, 1)
                elif unit[0] == "G":
                    half = int(unit[1])
                    dve.wait_ge(g_bent, of(b, 2, half))
                    tile = g2[s][:, 2 * half:2 * half + 2, :]
                    dve.scalar_tensor_tensor(out=tile, in0=tile, scalar=1.0, in1=ps_a[:, :, :], op0=ALU.add,
                                             op1=ALU.mult).then_inc(a_kept, 1)

            def z_unit(b, s, unit):
                half = int(unit[-1]) if unit[-1] in "01" else 0
                here = slice(2 * half, 2 * half + 2)
                if unit in Z_UNITS and unit[0] != "T" and unit[:2] not in ("FK", "FR"):
                    dve.wait_ge(z_filled, of(b, NZ, z_at(unit)))
                if unit[0] == "E":
                    dve.tensor_tensor(og[:, here, :], og[:, here, :], ps_z[:, :, :], ALU.subtract).then_inc(z_kept, 1)
                elif unit[0] == "Q":
                    dve.tensor_scalar(sq[:, here, :], ps_z[:, :, :], 1e-5, None, ALU.add).then_inc(z_kept, 1)
                elif unit[0] == "I":
                    here = slice(2 * int(unit[1]), 2 * int(unit[1]) + 2)
                    dve.wait_ge(z_kept, of(b, NZ, z_at("Q" + unit[1])))
                    dve.reciprocal(sq[:, here, :], sq[:, here, :]).then_inc(inverted, 1)
                elif unit == "N3":
                    dve.wait_ge(og_affine, of(b, 1, 0))
                    dve.wait_ge(a_kept, of(b, NA, a_at("G1")))
                    dve.scalar_tensor_tensor(out=og[:, :, :], in0=og[:, :, :], scalar=0.5, in1=g2[s][:, :, :], op0=ALU.mult,
                                             op1=ALU.mult).then_inc(gated, 1)
                elif unit[0] == "O":
                    if half == 0:
                        dve.wait_ge(z_loaded, (b + 1) * 32)
                    dve.tensor_tensor(xres[:, half, :], ps_z[:, :, :].rearrange("p a n -> p (a n)"), xres[:, half, :],
                                      ALU.add).then_inc(z_kept, 1)
                elif unit == "LS":
                    dve.wait_ge(z_kept, of(b, NZ, z_at("O1")))
                    statistics(1, b, xres)
                elif unit == "LN":
                    normalise(1, b, sq_rows, xres)
                elif unit == "X":
                    dve.wait_ge(shifted2, of(b, 1, 0))
                    for dst, which in ((xk2, FFN_K), (xr2, FFN_R)):
                        for c in range(FT):
                            ins = dve.scalar_tensor_tensor(out=dst[:, c, :], in0=sx2[:, c, :], scalar=col[:, which, c:c + 1],
                                                           in1=xcT[:, c, 1:TOK + 1], op0=ALU.mult, op1=ALU.add)
                        ins.then_inc(mixed2, 1)
                elif unit[:2] == "FV":
                    row = sq_rows[:, half, :]
                    dve.scalar_tensor_tensor(out=row, in0=row, scalar=1.0, in1=ps_z[:, :, :].rearrange("p a n -> p (a n)"),
                                             op0=ALU.add, op1=ALU.mult).then_inc(z_kept, 1)
                    dve.wait_ge(z_kept, of(b, NZ, z_at(unit)))
                    dve.scalar_tensor_tensor(out=xres[:, half, :], in0=row, scalar=0.5, in1=xres[:, half, :], op0=ALU.mult,
                                             op1=ALU.add).then_inc(res_made, 1)

            def c_unit(b, s, unit):
                if unit == "P":
                    return
                half = int(unit[1])
                here = slice(2 * half, 2 * half + 2)
                dve.wait_ge(z_filled, of(b - 1, NZ, z_at("FV1")))
                dve.tensor_tensor(og[:, here, :], v_hi[s][:, here, :].bitcast(F32), v_lo[s][:, here, :].bitcast(F32),
                                  ALU.add).then_inc(v_joined, 1)
                dve.wait_ge(z_filled, of(b, NZ, half))
                dve.wait_ge(v_joined, of(b, 2, half))
                dve.tensor_tensor(og[:, here, :], ps_z[:, :, :], og[:, here, :], ALU.mult).then_inc(z_kept, 1)

            def step(b, s, j, _):
                if isinstance(b, int) and b < 0:
                    return
                dve.wait_ge(spread_v, of(b, STEPS, j))
                if j == 0:
                    dve.wait_ge(a_kept, of(b, NA, a_at("K1")))
                    dve.wait_ge(decayed, of(b, 1, 0))
                dve.tensor_tensor(kvE[j % 2][:, :, 1:TOK + 1], ps_v[j % 2][:, :, :], kT[s][:, :, :], ALU.mult).then_inc(kv_made, 1)
                dve.wait_ge(seeded, of(b, STEPS, j))
                dve.wait_ge(kv_made, of(b, STEPS, j))
                dve.wait_ge(rs_made, of(b, STEPS, j - 2))
                dve.tensor_tensor_scan(sE[j % 2][:, :, :].rearrange("p c t -> p (c t)"),
                                       wE[s][:, :, :].rearrange("p c t -> p (c t)"),
                                       kvE[j % 2][:, :, :].rearrange("p c t -> p (c t)"), 0.0, ALU.mult, ALU.add
                                       ).then_inc(scanned, 1)

            def inner(b, s, j, batch_before):
                if j == 0 and batch_before:
                    dve.wait_ge(summed, of(b - 1, STEPS, STEPS - 1))
                    dve.wait_ge(z_kept, of(b - 1, NZ, 1))
                    dve.tensor_tensor(og[:, :, :], ps_acc[:, :, :], og[:, :, :], ALU.add).then_inc(og_made, 1)

            run(dve, step, a_unit, z_unit, c_unit, inner)

def build(nc, semaphores, ap, out):
    def between(name):
        return nc.dram_tensor(name, (BATCH, TOK, FEAT), F32, kind="Internal").ap()

    x1, x2, x3, x4, x5 = (between(f"x{i}") for i in range(1, 6))
    context_attention(nc, semaphores, ap["x"], ap["xT"], ap["cT"], ap["L0_xattn_w_q"], ap["L0_xattn_w_k"], ap["L0_xattn_w_v"],
                      ap["L0_w_oT"], ap["L0_xattn_alpha"], x1)
    semaphores.clear()
    channel_attention(nc, semaphores, x1, ap["c"], *(ap["L1_" + n] for n in ("Wqkv0T", "Winj0T", "Wqkv1T", "Winj1T", "WoT", "bo", "q_bias")), x2)
    semaphores.clear()
    w = ap["L2_xattn_w_qkv"]
    token_attention(nc, semaphores, "self", x2, None, ap["mask_self"], 1, ap["L2_ln1"], w[:, 0:FEAT], w[:, FEAT:2 * FEAT],
                    w[:, 2 * FEAT:3 * FEAT], ap["L2_xattn_w_ao"], ap["L2_qk1"], (ap["L2_bv1"], ap["L2_bo1"]), x3)
    semaphores.clear()
    w = ap["L2_xattn_w_kv"]
    token_attention(nc, semaphores, "cross", x3, ap["cT"], ap["mask_cross"], BATCH, ap["L2_ln2"], ap["L2_xattn_w_q"], w[:, 0:FEAT],
                    w[:, FEAT:2 * FEAT], ap["L2_xattn_w_co"], ap["L2_qk2"], (ap["L2_bv2"], ap["L2_bo2"]), x4)
    semaphores.clear()
    token_mlp(nc, semaphores, x4, ap["L2_xattn_w1"], ap["L2_xattn_w2"], ap["L2_ln3"], ap["L2_b1"], ap["L2_b2"], x5)
    semaphores.clear()
    weights = {n: ap[f"L3_W{n}T"] for n in ("r", "k", "v", "g", "o", "fk", "fr", "fv")}
    recurrent_block(nc, semaphores, x5, ap["L3_state"], weights, *(ap["L3_" + n] for n in
                    ("cols", "maa_w1", "maa_w2", "td_w1", "td_w2", "select", "spread", "head_sum", "group_mean")), out)


def lay_out(np, a):
    out = {}

    def put(name, array):
        out[name] = np.ascontiguousarray(array)

    put("x", a["x"])
    put("c", a["ctx_2048"])
    put("cT", a["ctx_2048"].transpose(0, 2, 1))
    if "L0_xattn_w_q" in a:
        put("xT", a["x"].transpose(0, 2, 1))
        for n in ("w_q", "w_k", "w_v"):
            put("L0_xattn_" + n, a["L0_xattn_" + n])
        put("L0_w_oT", a["L0_xattn_w_o"].T)
        put("L0_xattn_alpha", a["L0_xattn_alpha"].reshape(1, 1))
    if "L2_xattn_w_ao" in a:
        def col(v):
            return v.reshape(-1, P).T

        d = {n[len("L2_xattn_"):]: v for n, v in a.items() if n.startswith("L2_xattn_")}
        put("mask_self", a["mask_1x1xSxS2_fc1"][:, 0])
        put("mask_cross", a["mask_Bx1xSxS2_ff1"][:, 0])
        for n in ("w_qkv", "w_ao", "w_q", "w_kv", "w_co", "w1", "w2"):
            put("L2_xattn_" + n, d[n])
        for n in ("ln1", "ln2", "ln3"):
            put("L2_" + n, np.stack([col(d[n + "_s"]), col(d[n + "_b"])], 1))
        put("L2_qk1", np.stack([col(d["b_qkv"][:FEAT]), col(d["b_qkv"][FEAT:2 * FEAT])], 1))
        put("L2_qk2", np.stack([col(d["b_q"]), col(d["b_kv"][:FEAT])], 1))
        put("L2_bv1", d["b_qkv"][2 * FEAT:].reshape(1, FEAT))
        put("L2_bv2", d["b_kv"][FEAT:].reshape(1, FEAT))
        put("L2_bo1", d["b_ao"].reshape(1, FEAT))
        put("L2_bo2", d["b_co"].reshape(1, FEAT))
        put("L2_b1", col(d["b1"]))
        put("L2_b2", d["b2"].reshape(1, FEAT))
    if "L1_xattn_Wo" in a:
        for n in ("Wqkv0", "Winj0", "Wqkv1", "Winj1", "Wo"):
            put("L1_" + n + "T", a["L1_xattn_" + n].T)
        put("L1_bo", a["L1_xattn_bo"].reshape(TT, P).T)
        put("L1_q_bias", a["L1_xattn_r_w_bias"].reshape(-1, P).T)
    if "L3_xattn_Wr" in a:
        d = {n[len("L3_xattn_"):]: v for n, v in a.items() if n.startswith("L3_xattn_")}
        group, heads = 16, P // 16
        by_feature = np.arange(FEAT).reshape(FT, heads, group).transpose(0, 2, 1).reshape(-1)
        for n in ("Wr", "Wk", "Wfk", "Wfr", "Wfv"):
            put("L3_" + n + "T", d[n].T)
        for n in ("Wv", "Wg"):
            put("L3_" + n + "T", d[n].T[:, by_feature])
        put("L3_WoT", d["Wo"].T[by_feature])
        for n in ("maa_w1", "td_w1", "td_w2"):
            put("L3_" + n, d[n])
        put("L3_maa_w2", d["maa_w2"].reshape(-1, FEAT))
        vectors = [d[n].reshape(-1) for n in ("ln1_w", "ln1_b", "ln2_w", "ln2_b", "maa_x", "time_decay", "u")]
        vectors += [d[n][by_feature] for n in ("gn_w", "gn_b")]
        vectors += [d[n] for n in ("ffn_maa_k", "ffn_maa_r")] + list(d["maa_stack"][0])
        put("L3_cols", np.stack([v.reshape(-1, P).T for v in vectors], 1))
        c = a["ctx_2048"]
        edges = c[:, 0:2].transpose(0, 2, 1).reshape(BATCH, FT, P, 2)
        first = c[:, 2:2 + group].reshape(BATCH, FT, P, group)
        put("L3_state", np.concatenate([edges, first], 3).transpose(0, 2, 1, 3))
        p, m = np.arange(P)[:, None], np.arange(P)[None, :]
        put("L3_head_sum", (p // group == m % heads).astype(np.float32))
        put("L3_group_mean", ((p % heads == m % heads) / group).astype(np.float32))
        put("L3_select", np.stack([(p // heads == j) & (p % heads == m // group) for j in range(group)], 1).astype(np.float32))
        window = np.arange((2 * group - 1) * heads)[None, :]
        put("L3_spread", ((window // heads == group - 1) & (window % heads == p // group)).astype(np.float32))
    return out


def kernel(**inputs):
    import numpy as _np
    import concourse.bacc as _bacc
    from concourse import mybir as _mybir
    from concourse.bass_utils import run_bass_kernel_spmd as _run

    arrays = lay_out(_np, {n: _np.asarray(a) for n, a in inputs.items()})
    nc = _bacc.Bacc("TRN2", target_bir_lowering=False, num_devices=1)
    ap = {n: nc.dram_tensor("in_" + n, a.shape, _mybir.dt.from_np(a.dtype), kind="ExternalInput").ap()
          for n, a in arrays.items()}
    out = nc.dram_tensor("out", (BATCH, TOK, FEAT), _mybir.dt.float32, kind="ExternalOutput").ap()
    build(nc, Semaphores(nc), ap, out)
    r = _run(nc, [{"in_" + n: a for n, a in arrays.items()}], core_ids=[0])
    return r.results[0]["out"]
```
